# Optimizing a Trainium2 kernel written in Bass

```python
import numpy as np
import jax
import jax.numpy as jnp

def _softmax(x, axis=-1):
    return jax.nn.softmax(x, axis=axis)

def _gelu(x):
    return jax.nn.gelu(x, approximate=True)

def _silu(x):
    return jax.nn.silu(x)

def _sigmoid(x):
    return jax.nn.sigmoid(x)

def _layernorm(x, axis=-1, eps=1e-05):
    m = jnp.mean(x, axis=axis, keepdims=True)
    v = jnp.var(x, axis=axis, keepdims=True)
    return (x - m) / jnp.sqrt(v + eps)

def _scatter_add(tgt, idx, src, axis=0):
    return tgt.at[idx].add(src)

def _segment_sum(src, seg, n):
    return jax.ops.segment_sum(src, seg, n)
kernel_name = 'mk_early_fusion_embed_d1_tok_img256_r4_73974f'

def setup_inputs(seed: int=0):
    np.random.seed(seed)
    _w = jnp.asarray

    def _rec_inputs():
        import jax
        import jax.numpy as jnp
        _rk = jax.random.key(seed)
        x = -0.000596345 + 1.00056 * jax.random.normal(jax.random.fold_in(_rk, 1), (64, 64, 64, 3), jnp.float32)
        x_txt = jax.random.randint(jax.random.fold_in(_rk, 51), (64, 77), 0, 64, jnp.int32)
        return (x, x_txt)
    x, x_txt = _rec_inputs()

    def _L0_tok_setup():
        import jax, jax.numpy as jnp
        import numpy as np
        B, H, W = (16, 64, 64)
        WIDTH, LAYERS, M1, M2 = (32, 4, 12, 12)
        EPS = 1e-05

        def layer_norm(x, g, b):
            mu = jnp.mean(x, axis=-1, keepdims=True)
            var = jnp.mean((x - mu) ** 2, axis=-1, keepdims=True)
            return (x - mu) * jax.lax.rsqrt(var + EPS) * g + b

        def gelu(x):
            return jax.nn.gelu(x, approximate=False)

        def spectral_conv(x, w1, w2):
            b, c, h, w = x.shape
            x_ft = jnp.fft.rfft2(x)
            out_ft = jnp.zeros((b, w1.shape[1], h, w // 2 + 1), dtype=x_ft.dtype)
            out_ft = out_ft.at[:, :, :M1, :M2].set(jnp.einsum('bixy,ioxy->boxy', x_ft[:, :, :M1, :M2], w1))
            out_ft = out_ft.at[:, :, -M1:, :M2].set(jnp.einsum('bixy,ioxy->boxy', x_ft[:, :, -M1:, :M2], w2))
            return jnp.fft.irfft2(out_ft, s=(h, w))
        key = jax.random.key(seed)
        ks = jax.random.split(key, 16)
        scale = 1.0 / (WIDTH * WIDTH)
        d = {'x': jax.random.normal(ks[0], (B, H, W, 3), jnp.float32), 'fc0_w': jax.random.normal(ks[1], (3, WIDTH), jnp.float32) * 0.5, 'fc0_b': jnp.zeros((WIDTH,), jnp.float32), 'ln0_g': jnp.ones((WIDTH,), jnp.float32), 'ln0_b': jnp.zeros((WIDTH,), jnp.float32), 'w1r': jax.random.uniform(ks[2], (LAYERS, WIDTH, WIDTH, M1, M2), jnp.float32) * scale, 'w1i': jax.random.uniform(ks[3], (LAYERS, WIDTH, WIDTH, M1, M2), jnp.float32) * scale, 'w2r': jax.random.uniform(ks[4], (LAYERS, WIDTH, WIDTH, M1, M2), jnp.float32) * scale, 'w2i': jax.random.uniform(ks[5], (LAYERS, WIDTH, WIDTH, M1, M2), jnp.float32) * scale, 'conv_w': jax.random.normal(ks[6], (LAYERS, WIDTH, WIDTH), jnp.float32) * (1.0 / np.sqrt(WIDTH)), 'conv_b': jnp.zeros((LAYERS, WIDTH), jnp.float32), 'ln_g': jnp.ones((LAYERS, WIDTH), jnp.float32), 'ln_b': jnp.zeros((LAYERS, WIDTH), jnp.float32), 'fc1_w': jax.random.normal(ks[7], (WIDTH, 128), jnp.float32) * (1.0 / np.sqrt(WIDTH)), 'fc1_b': jnp.zeros((128,), jnp.float32), 'fc2_w': jax.random.normal(ks[8], (128, 64), jnp.float32) * (1.0 / np.sqrt(128)), 'fc2_b': jnp.zeros((64,), jnp.float32), 'fc3_w': jax.random.normal(ks[9], (64, 1), jnp.float32) * (1.0 / np.sqrt(64)), 'fc3_b': jnp.zeros((1,), jnp.float32)}
        return d
    _L0_tok_all = _L0_tok_setup()
    _L0_tok_in = {k: v for k, v in _L0_tok_all.items() if k in ('fc0_w', 'fc0_b', 'ln0_g', 'ln0_b', 'w1r', 'w1i', 'w2r', 'w2i', 'conv_w', 'conv_b', 'ln_g', 'ln_b', 'fc1_w', 'fc1_b', 'fc2_w', 'fc2_b', 'fc3_w', 'fc3_b')}
    del _L0_tok_all

    def _L0_txt_setup():
        import jax, jax.numpy as jnp
        import numpy as np
        BATCH = 32
        SEQ = 1024
        HID = 64
        VOCAB = 8000
        NEXT_ID = 5
        EPS = 1e-05

        def _positions(state):
            eq = state == NEXT_ID
            starts = jnp.pad(eq[:, :-1], ((0, 0), (1, 0)))
            instr = jnp.cumsum(starts.astype(jnp.int32), axis=-1)
            pos = jnp.arange(state.shape[-1], dtype=jnp.int32)
            seg_start = jnp.where(starts, pos[None, :], 0)
            last_start = jax.lax.cummax(seg_start, axis=1)
            args = pos[None, :] - last_start
            return (instr, args)
        key = jax.random.key(seed)
        ks = jax.random.split(key, 6)
        state = jax.random.randint(ks[0], (BATCH, SEQ), 0, 64, dtype=jnp.int64)
        token_emb = jax.random.normal(ks[1], (VOCAB, HID), dtype=jnp.float32) * 0.02
        instr_emb = jax.random.normal(ks[2], (SEQ, HID), dtype=jnp.float32) * 0.02
        arg_emb = jax.random.normal(ks[3], (SEQ, HID), dtype=jnp.float32) * 0.02
        gamma = jnp.ones((HID,), dtype=jnp.float32)
        beta = jnp.zeros((HID,), dtype=jnp.float32)
        return {'state': state, 'token_emb': token_emb, 'instr_emb': instr_emb, 'arg_emb': arg_emb, 'gamma': gamma, 'beta': beta}
    _L0_txt_all = _L0_txt_setup()
    _L0_txt_in = {k: v for k, v in _L0_txt_all.items() if k in ('token_emb', 'instr_emb', 'arg_emb', 'gamma', 'beta')}
    del _L0_txt_all

    def _L0_attn_setup():
        import jax, jax.numpy as jnp
        import numpy as np
        import math
        B, N, DIM = (2, 1024, 64)
        NUM_HEADS = 8
        HEAD_DIM = DIM // NUM_HEADS
        WINDOW = 7

        def local_mask(seq_len: int, window_size: int=WINDOW) -> jnp.ndarray:
            grid = int(math.isqrt(seq_len))
            idx = jnp.arange(seq_len)
            row, col = (idx // grid, idx % grid)
            half = window_size // 2
            ok_row = jnp.abs(row[:, None] - row[None, :]) <= half
            ok_col = jnp.abs(col[:, None] - col[None, :]) <= half
            return ok_row & ok_col
        key = jax.random.key(seed)
        k1, k2, k3, k4 = jax.random.split(key, 4)
        x = jax.random.normal(k1, (B, N, DIM), dtype=jnp.float32)
        W_qkv = jax.random.normal(k2, (3 * DIM, DIM), dtype=jnp.float32) * DIM ** (-0.5)
        W_proj = jax.random.normal(k3, (DIM, DIM), dtype=jnp.float32) * DIM ** (-0.5)
        b_proj = jax.random.normal(k4, (DIM,), dtype=jnp.float32) * 0.01
        temperature = jnp.ones((1,), dtype=jnp.float32)
        return {'x': x, 'W_qkv': W_qkv, 'W_proj': W_proj, 'b_proj': b_proj, 'temperature': temperature}
    _L0_attn_all = _L0_attn_setup()
    _L0_attn_in = {k: v for k, v in _L0_attn_all.items() if k in ('W_qkv', 'W_proj', 'b_proj', 'temperature')}
    del _L0_attn_all

    def _L0_ffn_setup():
        import jax, jax.numpy as jnp
        import numpy as np
        B, T, IN_DIM = (64, 64, 64)
        HID, OUT_DIM = (128, 64)
        N_LAYERS, N_EXPERTS, N_SHARED = (2, 16, 1)
        key = jax.random.key(seed)
        ks = jax.random.split(key, 10)
        s = 0.02
        x = jax.random.normal(ks[0], (B, T, IN_DIM), dtype=jnp.float32)
        route_id = jax.random.randint(ks[1], (B,), 0, N_EXPERTS)
        Wi = jax.random.normal(ks[2], (HID, IN_DIM), dtype=jnp.float32) * s
        bi = jnp.zeros((HID,), dtype=jnp.float32)
        Wr = jax.random.normal(ks[3], (N_LAYERS, N_EXPERTS, HID, HID), dtype=jnp.float32) * s
        br = jax.random.normal(ks[4], (N_LAYERS, N_EXPERTS, HID), dtype=jnp.float32) * s
        Ws = jax.random.normal(ks[5], (N_LAYERS, N_SHARED, HID, HID), dtype=jnp.float32) * s
        bs = jax.random.normal(ks[6], (N_LAYERS, N_SHARED, HID), dtype=jnp.float32) * s
        Wo = jax.random.normal(ks[7], (OUT_DIM, HID), dtype=jnp.float32) * s
        bo = jnp.zeros((OUT_DIM,), dtype=jnp.float32)
        return {'x': x, 'route_id': route_id, 'Wi': Wi, 'bi': bi, 'Wr': Wr, 'br': br, 'Ws': Ws, 'bs': bs, 'Wo': Wo, 'bo': bo}
    _L0_ffn_all = _L0_ffn_setup()
    _L0_ffn_in = {k: v for k, v in _L0_ffn_all.items() if k in ('route_id', 'Wi', 'bi', 'Wr', 'br', 'Ws', 'bs', 'Wo', 'bo')}
    del _L0_ffn_all
    return {'x': x, 'x_txt': x_txt, 'L0_tok_fc0_w': _L0_tok_in['fc0_w'], 'L0_tok_fc0_b': _L0_tok_in['fc0_b'], 'L0_tok_ln0_g': _L0_tok_in['ln0_g'], 'L0_tok_ln0_b': _L0_tok_in['ln0_b'], 'L0_tok_w1r': _L0_tok_in['w1r'], 'L0_tok_w1i': _L0_tok_in['w1i'], 'L0_tok_w2r': _L0_tok_in['w2r'], 'L0_tok_w2i': _L0_tok_in['w2i'], 'L0_tok_conv_w': _L0_tok_in['conv_w'], 'L0_tok_conv_b': _L0_tok_in['conv_b'], 'L0_tok_ln_g': _L0_tok_in['ln_g'], 'L0_tok_ln_b': _L0_tok_in['ln_b'], 'L0_tok_fc1_w': _L0_tok_in['fc1_w'], 'L0_tok_fc1_b': _L0_tok_in['fc1_b'], 'L0_tok_fc2_w': _L0_tok_in['fc2_w'], 'L0_tok_fc2_b': _L0_tok_in['fc2_b'], 'L0_tok_fc3_w': _L0_tok_in['fc3_w'], 'L0_tok_fc3_b': _L0_tok_in['fc3_b'], 'L0_txt_token_emb': _L0_txt_in['token_emb'], 'L0_txt_instr_emb': _L0_txt_in['instr_emb'], 'L0_txt_arg_emb': _L0_txt_in['arg_emb'], 'L0_txt_gamma': _L0_txt_in['gamma'], 'L0_txt_beta': _L0_txt_in['beta'], 'L0_attn_W_qkv': _L0_attn_in['W_qkv'], 'L0_attn_W_proj': _L0_attn_in['W_proj'], 'L0_attn_b_proj': _L0_attn_in['b_proj'], 'L0_attn_temperature': _L0_attn_in['temperature'], 'L0_ffn_route_id': _L0_ffn_in['route_id'], 'L0_ffn_Wi': _L0_ffn_in['Wi'], 'L0_ffn_bi': _L0_ffn_in['bi'], 'L0_ffn_Wr': _L0_ffn_in['Wr'], 'L0_ffn_br': _L0_ffn_in['br'], 'L0_ffn_Ws': _L0_ffn_in['Ws'], 'L0_ffn_bs': _L0_ffn_in['bs'], 'L0_ffn_Wo': _L0_ffn_in['Wo'], 'L0_ffn_bo': _L0_ffn_in['bo']}

def reference(x, x_txt, L0_tok_fc0_w, L0_tok_fc0_b, L0_tok_ln0_g, L0_tok_ln0_b, L0_tok_w1r, L0_tok_w1i, L0_tok_w2r, L0_tok_w2i, L0_tok_conv_w, L0_tok_conv_b, L0_tok_ln_g, L0_tok_ln_b, L0_tok_fc1_w, L0_tok_fc1_b, L0_tok_fc2_w, L0_tok_fc2_b, L0_tok_fc3_w, L0_tok_fc3_b, L0_txt_token_emb, L0_txt_instr_emb, L0_txt_arg_emb, L0_txt_gamma, L0_txt_beta, L0_attn_W_qkv, L0_attn_W_proj, L0_attn_b_proj, L0_attn_temperature, L0_ffn_route_id, L0_ffn_Wi, L0_ffn_bi, L0_ffn_Wr, L0_ffn_br, L0_ffn_Ws, L0_ffn_bs, L0_ffn_Wo, L0_ffn_bo):
    import jax
    import jax.numpy as jnp

    def _L0_tok_ref(x, fc0_w, fc0_b, ln0_g, ln0_b, w1r, w1i, w2r, w2i, conv_w, conv_b, ln_g, ln_b, fc1_w, fc1_b, fc2_w, fc2_b, fc3_w, fc3_b):
        import jax, jax.numpy as jnp
        import numpy as np
        B, H, W = (16, 64, 64)
        WIDTH, LAYERS, M1, M2 = (32, 4, 12, 12)
        EPS = 1e-05

        def layer_norm(x, g, b):
            mu = jnp.mean(x, axis=-1, keepdims=True)
            var = jnp.mean((x - mu) ** 2, axis=-1, keepdims=True)
            return (x - mu) * jax.lax.rsqrt(var + EPS) * g + b

        def gelu(x):
            return jax.nn.gelu(x, approximate=False)

        def spectral_conv(x, w1, w2):
            b, c, h, w = x.shape
            x_ft = jnp.fft.rfft2(x)
            out_ft = jnp.zeros((b, w1.shape[1], h, w // 2 + 1), dtype=x_ft.dtype)
            out_ft = out_ft.at[:, :, :M1, :M2].set(jnp.einsum('bixy,ioxy->boxy', x_ft[:, :, :M1, :M2], w1))
            out_ft = out_ft.at[:, :, -M1:, :M2].set(jnp.einsum('bixy,ioxy->boxy', x_ft[:, :, -M1:, :M2], w2))
            return jnp.fft.irfft2(out_ft, s=(h, w))
        h = layer_norm(x @ fc0_w + fc0_b, ln0_g, ln0_b)
        h = jnp.transpose(h, (0, 3, 1, 2))
        for i in range(LAYERS):
            w1 = w1r[i] + 1j * w1i[i]
            w2 = w2r[i] + 1j * w2i[i]
            x1 = spectral_conv(h, w1, w2)
            x2 = jnp.einsum('bchw,oc->bohw', h, conv_w[i]) + conv_b[i][None, :, None, None]
            h = x1 + x2
            h = jnp.transpose(h, (0, 2, 3, 1))
            h = layer_norm(h, ln_g[i], ln_b[i])
            if i < LAYERS - 1:
                h = gelu(h)
            h = jnp.transpose(h, (0, 3, 1, 2))
        h = jnp.transpose(h, (0, 2, 3, 1))
        h = gelu(h @ fc1_w + fc1_b)
        h = gelu(h @ fc2_w + fc2_b)
        h = h @ fc3_w + fc3_b
        return h[..., 0]

    def _L0_txt_ref(state, token_emb, instr_emb, arg_emb, gamma, beta):
        import jax, jax.numpy as jnp
        import numpy as np
        BATCH = 32
        SEQ = 1024
        HID = 64
        VOCAB = 8000
        NEXT_ID = 5
        EPS = 1e-05

        def _positions(state):
            eq = state == NEXT_ID
            starts = jnp.pad(eq[:, :-1], ((0, 0), (1, 0)))
            instr = jnp.cumsum(starts.astype(jnp.int32), axis=-1)
            pos = jnp.arange(state.shape[-1], dtype=jnp.int32)
            seg_start = jnp.where(starts, pos[None, :], 0)
            last_start = jax.lax.cummax(seg_start, axis=1)
            args = pos[None, :] - last_start
            return (instr, args)
        instr, args = _positions(state)
        embedded = token_emb[state] + instr_emb[instr] + arg_emb[args]
        mean = jnp.mean(embedded, axis=-1, keepdims=True)
        var = jnp.mean(jnp.square(embedded - mean), axis=-1, keepdims=True)
        normed = (embedded - mean) * jax.lax.rsqrt(var + EPS)
        return normed * gamma + beta

    def _L0_attn_ref(x, W_qkv, W_proj, b_proj, temperature):
        import jax, jax.numpy as jnp
        import numpy as np
        import math
        B, N, DIM = (2, 1024, 64)
        NUM_HEADS = 8
        HEAD_DIM = DIM // NUM_HEADS
        WINDOW = 7

        def local_mask(seq_len: int, window_size: int=WINDOW) -> jnp.ndarray:
            grid = int(math.isqrt(seq_len))
            idx = jnp.arange(seq_len)
            row, col = (idx // grid, idx % grid)
            half = window_size // 2
            ok_row = jnp.abs(row[:, None] - row[None, :]) <= half
            ok_col = jnp.abs(col[:, None] - col[None, :]) <= half
            return ok_row & ok_col
        Bb, Nn, C = x.shape
        scale = HEAD_DIM ** (-0.5)
        qkv = (x @ W_qkv.T).reshape(Bb, Nn, 3, NUM_HEADS, HEAD_DIM)
        qkv = jnp.transpose(qkv, (2, 0, 3, 1, 4))
        q, k, v = (qkv[0], qkv[1], qkv[2])
        attn = jnp.einsum('bhqd,bhkd->bhqk', q, k) * (scale * temperature[0])
        mask = local_mask(Nn)
        attn = jnp.where(mask[None, None, :, :], attn, -jnp.inf)
        attn = jax.nn.softmax(attn, axis=-1)
        out = jnp.einsum('bhqk,bhkd->bhqd', attn, v)
        out = jnp.transpose(out, (0, 2, 1, 3)).reshape(Bb, Nn, C)
        return out @ W_proj.T + b_proj

    def _L0_ffn_ref(x, route_id, Wi, bi, Wr, br, Ws, bs, Wo, bo):
        import jax, jax.numpy as jnp
        import numpy as np
        B, T, IN_DIM = (64, 64, 64)
        HID, OUT_DIM = (128, 64)
        N_LAYERS, N_EXPERTS, N_SHARED = (2, 16, 1)
        flat = x.reshape(-1, x.shape[-1])
        n_tok = flat.shape[0]
        route = jnp.repeat(route_id, n_tok // route_id.shape[0])
        h = jax.nn.relu(flat @ Wi.T + bi)
        n_layers, n_experts = (Wr.shape[0], Wr.shape[1])
        for l in range(n_layers):
            shared = (jnp.einsum('nd,shd->snh', h, Ws[l]) + bs[l][:, None, :]).mean(axis=0)
            routed = jnp.zeros_like(h)
            for e in range(n_experts):
                ye = h @ Wr[l, e].T + br[l, e]
                routed = routed + jnp.where((route == e)[:, None], ye, 0.0)
            h = jax.nn.relu(shared + routed + h)
        out = h @ Wo.T + bo
        return out.reshape(*x.shape[:-1], out.shape[-1])
    h = _L0_tok_ref(x, L0_tok_fc0_w, L0_tok_fc0_b, L0_tok_ln0_g, L0_tok_ln0_b, L0_tok_w1r, L0_tok_w1i, L0_tok_w2r, L0_tok_w2i, L0_tok_conv_w, L0_tok_conv_b, L0_tok_ln_g, L0_tok_ln_b, L0_tok_fc1_w, L0_tok_fc1_b, L0_tok_fc2_w, L0_tok_fc2_b, L0_tok_fc3_w, L0_tok_fc3_b)
    h = jnp.concatenate([h, _L0_txt_ref(x_txt, L0_txt_token_emb, L0_txt_instr_emb, L0_txt_arg_emb, L0_txt_gamma, L0_txt_beta)], axis=1)
    h = h + _L0_attn_ref(_layernorm(h, axis=-1), L0_attn_W_qkv, L0_attn_W_proj, L0_attn_b_proj, L0_attn_temperature)
    h = h + _L0_ffn_ref(_layernorm(h, axis=-1), L0_ffn_route_id, L0_ffn_Wi, L0_ffn_bi, L0_ffn_Wr, L0_ffn_br, L0_ffn_Ws, L0_ffn_bs, L0_ffn_Wo, L0_ffn_bo)
    return h

_drawn_inputs = setup_inputs


def setup_inputs(seed=0):
    import zlib

    import numpy as np

    out = dict(_drawn_inputs(seed))
    spreads = {'L0_tok_fc0_b': (0.0, 0.1),
     'L0_tok_ln0_g': (1.0, 0.2),
     'L0_tok_ln0_b': (0.0, 0.1),
     'L0_tok_conv_b': (0.0, 0.1),
     'L0_tok_ln_g': (1.0, 0.2),
     'L0_tok_ln_b': (0.0, 0.1),
     'L0_tok_fc1_b': (0.0, 0.1),
     'L0_tok_fc2_b': (0.0, 0.1),
     'L0_txt_gamma': (1.0, 0.2),
     'L0_txt_beta': (0.0, 0.1),
     'L0_ffn_bi': (0.0, 0.469),
     'L0_ffn_bo': (0.0, 0.1)}
    factors = {'L0_tok_w1r': 64.0,
     'L0_tok_w1i': 64.0,
     'L0_tok_w2r': 64.0,
     'L0_tok_w2i': 64.0,
     'L0_attn_b_proj': 4.368,
     'L0_ffn_Wr': 6.295,
     'L0_ffn_br': 8.0,
     'L0_ffn_Ws': 6.02,
     'L0_ffn_bs': 8.0}
    for name, (base, spread) in spreads.items():
        noise = np.random.default_rng([zlib.crc32(name.encode()), seed]).standard_normal(out[name].shape)
        drawn = base * np.exp(spread * noise) if base else spread * noise
        out[name] = jnp.asarray(drawn.astype(out[name].dtype))
    for name, factor in factors.items():
        out[name] = (out[name] * factor).astype(out[name].dtype)
    return out
```

```python
import numpy as np
import concourse.bass as bass
from concourse import mybir
from contextlib import ExitStack

F32 = mybir.dt.float32
I32 = mybir.dt.int32
ALU = mybir.AluOpType
ACT = mybir.ActivationFunctionType
AX = mybir.AxisListType

IMGS, Y, X, C = 64, 64, 64, 32
PAIRS = IMGS // 2
KX, KYH = 12, 12
KY = 2 * KYH
MODES = KYH * KX
LAYERS = 4
CHUNKS = 4
YC = Y // CHUNKS
STEM = 0
COUPLES = PAIRS // 2
TRIG = 2 * KX
EPS = 1e-5
TXT, VOCAB = 77, 8000
TOK = Y + TXT
WCH = MODES // COUPLES


def at_least(eng, sem, value):
    if isinstance(value, int) and value <= 0:
        return
    eng.wait_ge(sem, value)


def waits_apart(eng, passed):
    eng.sem_inc(passed, 1)


def each_step(eng, step, drain, per=CHUNKS):
    def couple(i, pairs=2):
        for p in range(pairs):
            for j in range(per):
                step(i, p, j)
    couple(0)
    couple(1)
    with eng.Fori(2, COUPLES - 1) as i:
        couple(i)
    couple(COUPLES - 1)
    couple(COUPLES, drain)


def behind(i, p, j, lag, per=CHUNKS):
    n, j = divmod(per * p + j - lag, per)
    i, p = i + n // 2, n % 2
    if isinstance(i, int) and not 0 <= i < COUPLES:
        return None
    return i, p, j


def token_network(nc, t, tokens):
    with ExitStack() as ctx:
        def sb(name, shape, dt=F32):
            return ctx.enter_context(nc.sbuf_tensor(name, shape, dt))

        def sem(name):
            return ctx.enter_context(nc.semaphore(name))

        h_dram = nc.dram_tensor("h_scratch", [PAIRS, 128, 16 * 128], F32).ap()
        g_dram = nc.dram_tensor("g_scratch", [IMGS, 2, KY, KX * 2 * C], F32).ap()
        cb_dram = nc.dram_tensor("cb_scratch", [LAYERS, Y * C], F32).ap()

        wsb = sb("wsb", [128, MODES, 2, C])
        xsb = sb("xsb", [128, MODES, IMGS])
        hc = [sb(f"hc{p}", [128, 16, 128]) for p in range(2)]
        hp = [sb(f"hp{p}", [128, C, Y]) for p in range(2)]
        zb = [sb(f"zb{p}", [128, Y, C]) for p in range(2)]
        gt = [sb(f"gt{p}", [128, 2, KX, 2, C]) for p in range(2)]
        asb = sb("asb", [128, 2, 2 * KX, 2, C])
        sq = [sb(f"sq{p}", [128, YC, C]) for p in range(2)]
        zt = [sb(f"zt{p}", [128, YC, C]) for p in range(2)]
        var = [sb(f"var{p}", [128, YC]) for p in range(2)]
        ve = [sb(f"ve{p}", [128, YC]) for p in range(2)]
        rstd = [sb(f"rstd{p}", [128, YC]) for p in range(2)]
        mhalf = sb("mhalf", [128, YC])
        wmean = sb("wmean", [128, 2 * WCH])
        gs = [sb(f"gs{p}", [IMGS, 2, KX, 2, C]) for p in range(2)]
        xin = [sb(f"xin{p}", [128, CHUNKS, 128]) for p in range(2)]
        a1 = [sb(f"a1{p}", [128, 512]) for p in range(2)]
        a2 = [sb(f"a2{p}", [128, 512]) for p in range(2)]
        hst = [sb(f"hst{p}", [4, 16, 128]) for p in range(2)]

        ident = sb("ident", [128, 128])
        d1 = sb("d1", [128, 2, KX, 3])
        cy = sb("cy", [128, 2, KY])
        dyi = sb("dyi", [128, Y])
        ex = sb("ex", [128, 128])
        sgn = sb("sgn", [128, 1])
        cw = sb("cw", [128, LAYERS, 4, C])
        cwm = sb("cwm", [128, LAYERS * 4])
        cbt = hp[0][0:LAYERS].rearrange("l c y -> l (c y)").rearrange("l (y c) -> l y c", c=C)
        cbm = hp[1][0:LAYERS, 0, :]
        f0 = sb("f0", [128, YC, C])
        f0m = sb("f0m", [128, YC])
        lnp = sb("lnp", [128, LAYERS + 1, 2])
        fc1 = sb("fc1", [128, 4, 128])
        fc1b = sb("fc1b", [128, 1])
        fc2 = sb("fc2", [128, 64])
        fc2b = sb("fc2b", [128, 1])
        fc3 = sb("fc3", [128, 2, 4])
        fc3b = sb("fc3b", [4, 1])

        ps = ctx.enter_context(nc.psum_tensor("ps", [128, 8, 512], F32))
        main_ps = [ps[:, b, :] for b in (0, 1)]
        t1_ps, t2_ps, z_ps, x_ps = ps[:, 2, :], ps[:, 3, :], ps[0:2 * TRIG, 4, :], ps[:, 5, 0:MODES * 2]
        a_ps = ps[0:Y, 6:8, 0:4 * 2 * KX * 3]
        f1_ps = [ps[:, 6, :], ps[:, 7, :]]
        f2_ps = [ps[:, 3, :], ps[:, 5, :]]
        f3_ps = ps[64:68, 4, :]

        const_in = sem("const_in")
        small_step = sem("small_step")
        passed = sem("passed")
        zeroed = sem("zeroed")
        consts_ready = sem("consts_ready")
        cb_out = sem("cb_out")
        zbias_in = sem("zbias_in")
        xin_in = [sem(f"xin_in{p}") for p in range(2)]
        w_in = sem("w_in")
        w_mean = sem("w_mean")
        w_sub = sem("w_sub")
        w_cent = sem("w_cent")
        main_ready = sem("main_ready")
        sq_ready = sem("sq_ready")
        var_ready = sem("var_ready")
        ve_ready = sem("ve_ready")
        rstd_ready = sem("rstd_ready")
        z_ready = sem("z_ready")
        t1_ready = sem("t1_ready")
        hc_ready = sem("hc_ready")
        t2_ready = sem("t2_ready")
        hp_ready = sem("hp_ready")
        a_psr = sem("a_psr")
        a_ready = [sem(f"a_ready{b}") for b in range(2)]
        x_psr = sem("x_psr")
        x_ready = sem("x_ready")
        z_psr = sem("z_psr")
        zb_ready = sem("zb_ready")
        h_out = [sem(f"h_out{j}") for j in range(CHUNKS)]
        h_in = [[sem(f"h_in{p}{j}") for j in range(CHUNKS)] for p in range(2)]
        gt_in = [sem(f"gt_in{p}") for p in range(2)]
        mix_ready = sem("mix_ready")
        gs_a = sem("gs_a")
        gs_b = sem("gs_b")
        g_out = [sem(f"g_out{p}") for p in range(2)]
        f1_psr = sem("f1_psr")
        a1_ready = sem("a1_ready")
        f2_psr = sem("f2_psr")
        a2_ready = sem("a2_ready")
        f3_psr = sem("f3_psr")
        hst_ready = sem("hst_ready")
        tok_out = [sem(f"tok_out{p}") for p in range(2)]

        block = ctx.enter_context(nc.Block())
        loads = [(ident, t["ident"]), (d1, t["d1"]), (cy, t["cy"]), (dyi, t["dyi"]), (ex, t["ex"]),
                 (sgn, t["sgn"]), (cw, t["conv_w"]), (cbt, t["conv_b"]), (f0, t["fc0"]), (lnp, t["lnp"]),
                 (fc1, t["fc1_w"]), (fc1b, t["fc1_b"]), (fc2, t["fc2_w"]), (fc2b, t["fc2_b"]),
                 (fc3, t["fc3_w"]), (fc3b, t["fc3_b"])]
        NCONST = 16 * (len(loads) + 2)

        def rank(s, i, p):
            return s * PAIRS + 2 * i + p

        def stored(eng, s, r):
            if r >= 2:
                eng.wait_ge(g_out[r % 2], 16 * (KY // 2 * (s - 1) + r // 2))

        @block.sync
        def _(sp):
            for dst, src in loads:
                sp.dma_start(dst[:], src[:]).then_inc(const_in, 16)
            sp.wait_ge(zeroed, 7)
            for p in range(2):
                sp.dma_start(xin[p][48:49], t["ones"][:, 0:512].rearrange("a (j n) -> a j n", j=CHUNKS)).then_inc(const_in, 16)
            for p in range(2):
                sp.dma_start(xin[p][0:48], t["x"][p]).then_inc(xin_in[p], 16)
            sp.wait_ge(consts_ready, 1)
            sp.dma_start(cb_dram.rearrange("l (y c) -> l y c", c=C), cbt[:]).then_inc(cb_out, 16)
            sp.wait_ge(cb_out, 16)

            def load_w(s, i):
                if not (isinstance(i, int) and i == 0 and isinstance(s, int) and s == 0):
                    sp.wait_ge(w_cent, s * COUPLES + i)
                    waits_apart(sp, passed)
                sp.dma_start(wsb[:, bass.ds(i * WCH, WCH)], t["w"][bass.ds(s, 1), :, bass.ds(i * WCH, WCH)]
                             .rearrange("a p m s c -> (a p) m s c")).then_inc(w_in, 16)

            def h_chunk(i, p, j):
                return h_dram[bass.ds(2 * i + p, 1), :, 512 * j:512 * j + 512].rearrange("a p n -> (a p) n")

            def hc_chunk(p, j):
                return hc[p][:, 4 * j:4 * j + 4, :].rearrange("p a n -> p (a n)")

            def store_h(s, i, p, j):
                sp.wait_ge(hc_ready, 4 * rank(s, i, p) + j + 1)
                waits_apart(sp, passed)
                sp.dma_start(h_chunk(i, p, j), hc_chunk(p, j)).then_inc(h_out[j], 16)

            def load_h(i, p, j):
                sp.dma_start(hc_chunk(p, j), h_chunk(i, p, j)).then_inc(h_in[p][j], 16)

            def load_gt(i, p):
                sp.dma_start(gt[p][0:2 * KY].rearrange("k m x s c -> k m (x s c)"),
                             g_dram[bass.ds(4 * i + 2 * p, 2)].rearrange("m a k n -> (a k) m n")).then_inc(gt_in[p], 16)

            def stem_step(i, p, j):
                if behind(i, p, j, 0):
                    if p == 0 and j == 0:
                        load_w(0, i)
                if c := behind(i, p, j, 2):
                    store_h(0, *c)
                    if c[2] == 3 and (nxt := behind(*c, -2 * CHUNKS)):
                        sp.wait_ge(main_ready, 4 * rank(0, c[0], c[1]) + 4)
                        waits_apart(sp, passed)
                        sp.dma_start(xin[c[1]][0:48], t["x"][bass.ds(2 * nxt[0] + nxt[1], 1)]
                                     .rearrange("a k j n -> (a k) j n")).then_inc(xin_in[c[1]], 16)
            each_step(sp, stem_step, 1)

            def between(s):
                for j in range(CHUNKS):
                    sp.wait_ge(h_out[j], 16 * PAIRS * s)
                waits_apart(sp, passed)
                sp.wait_ge(t2_ready, 4 * PAIRS * s)
                waits_apart(sp, passed)
                for p in range(2):
                    for j in range(CHUNKS):
                        load_h(0, p, j)
                    sp.dma_start(zb[p][2 * TRIG:2 * TRIG + 1].rearrange("a y c -> a (y c)"),
                                 cb_dram[bass.ds(s - 1, 1)]).then_inc(zbias_in, 16)
                for r in range(KY):
                    row = (s - 1) * KY + r
                    sp.wait_ge(gs_a, row + 1)
                    sp.wait_ge(gs_b, row + 1)
                    waits_apart(sp, passed)
                    sp.dma_start(g_dram[:, :, r, :], gs[r % 2][:].rearrange("i a x s c -> i a (x s c)")
                                 ).then_inc(g_out[r % 2], 16)
                for b in range(2):
                    sp.wait_ge(g_out[b], 16 * (KY // 2) * s)
                    waits_apart(sp, passed)
                for p in range(2):
                    load_gt(0, p)

            def layer_pass(s, final):
                between(s)

                def step(i, p, j):
                    if behind(i, p, j, 0) and j == 0:
                        if p == 0 and not final:
                            load_w(s, i)
                        if nxt := behind(i, p, 0, -2 * CHUNKS):
                            sp.wait_ge(z_psr, 4 * (rank(s, i, p) - PAIRS) + 4)
                            waits_apart(sp, passed)
                            load_gt(*nxt[0:2])
                    if not final and (c := behind(i, p, j, 2)):
                        store_h(s, *c)
                    if c := behind(i, p, j, 3):
                        if nxt := behind(*c, -2 * CHUNKS):
                            if final:
                                sp.wait_ge(hst_ready, 4 * (2 * c[0] + c[1]) + c[2] + 1)
                                waits_apart(sp, passed)
                            else:
                                sp.wait_ge(h_out[c[2]], 16 * (PAIRS * s + 2 * c[0] + c[1] + 1))
                                waits_apart(sp, passed)
                                sp.wait_ge(t2_ready, 4 * rank(s, c[0], c[1]) + c[2] + 1)
                                waits_apart(sp, passed)
                            load_h(*nxt)
                        if final and c[2] == 3:
                            n = 2 * c[0] + c[1]
                            sp.wait_ge(hst_ready, 4 * n + 4)
                            waits_apart(sp, passed)
                            for m in range(2):
                                sp.dma_start(tokens[bass.ds(2 * n + m, 1), 0:Y, :]
                                             .rearrange("a (j k) x -> (a k) j x", k=4),
                                             hst[c[1]][:, :, 64 * m:64 * m + 64]).then_inc(tok_out[c[1]], 16)
                each_step(sp, step, 1)

            with sp.Fori(1, LAYERS) as s:
                layer_pass(s, False)
            layer_pass(LAYERS, True)
            for p in range(2):
                sp.wait_ge(tok_out[p], 32 * COUPLES)

        @block.tensor
        def _(pe):
            pe.wait_ge(const_in, NCONST)
            pe.wait_ge(consts_ready, 4)

            def main(s, i, p, j):
                g = rank(s, i, p)
                q = 4 * g + j
                m = main_ps[j % 2]
                at_least(pe, z_ready, q - 1)
                if s is STEM:
                    if j == 0:
                        pe.wait_ge(xin_in[p], 16 * (i + 1))
                    nc.tensor.matmul(m, xin[p][:, j, :], f0[:].rearrange("k y c -> k (y c)"),
                                     start=True, stop=True).then_inc(main_ready, 1)
                    return
                pe.wait_ge(h_in[p][j], 16 * (COUPLES * (s - 1) + i + 1))
                if j == 0:
                    pe.wait_ge(zb_ready, 4 * (g - PAIRS) + 4)
                    if isinstance(i, int) and i == 0 and p == 0:
                        pe.wait_ge(zbias_in, 32 * s)
                nc.tensor.matmul(m, ex[:], zb[p][:, YC * j:YC * j + YC, :].rearrange("k y c -> k (y c)"),
                                 start=True, stop=False, skip_group_check=True)
                for k in range(4):
                    last = nc.tensor.matmul(m[:, 128 * k:128 * k + 128], hc[p][:, 4 * j + k, :],
                                            cw[:, bass.ds(s - 1, 1)].rearrange("p a y c -> p (a y c)"),
                                            start=False, stop=True, skip_group_check=True)
                last.then_inc(main_ready, 1)

            def i1(s, i, p, j):
                idx = 4 * (rank(s, i, p) - PAIRS) + j
                if j == 0:
                    pe.wait_ge(gt_in[p], 16 * (COUPLES * (s - 1) + i + 1))
                if not (isinstance(i, int) and i == 0 and p == 0 and j == 0):
                    pe.wait_ge(zb_ready, idx)
                for k in range(8):
                    last = nc.tensor.matmul(z_ps[:, 64 * k:64 * k + 64],
                                            gt[p][:, :, :, :, 8 * j + k].rearrange("k m x s -> k (m x s)"),
                                            dyi[:], start=True, stop=True)
                last.then_inc(z_psr, 1)

            def t1(s, i, p, j):
                q = 4 * rank(s, i, p) + j
                pe.wait_ge(z_ready, q + 1)
                at_least(pe, hc_ready, q)
                for k in range(4):
                    last = nc.tensor.transpose(t1_ps[:, 128 * k:128 * k + 128],
                                               zt[j % 2][:, 4 * k:4 * k + 4, :].rearrange("p y c -> p (y c)"), ident[:])
                last.then_inc(t1_ready, 1)

            def t2(s, i, p, j):
                q = 4 * rank(s, i, p) + j
                pe.wait_ge(hc_ready, q + 1)
                at_least(pe, hp_ready, q)
                for k in range(4):
                    last = nc.tensor.transpose(t2_ps[:, 128 * k:128 * k + 128], hc[p][:, 4 * j + k, :], ident[:])
                last.then_inc(t2_ready, 1)

            def f1(s, i, p, j):
                g = rank(s, i, p)
                if j == 0:
                    pe.wait_ge(hp_ready, 4 * g + 4)
                for b in range(2):
                    at_least(pe, a_ready[b], 4 * g + j)
                for k in range(8):
                    last = nc.tensor.matmul(a_ps[:, k // 4, 72 * (k % 4):72 * (k % 4) + 72], hp[p][:, 8 * j + k, :],
                                            d1[:].rearrange("p m x s -> p (m x s)"), start=True, stop=True)
                last.then_inc(a_psr, 1)

            def f2(s, i, p, half):
                g = rank(s, i, p)
                if half == 0:
                    for b in range(2):
                        pe.wait_ge(a_ready[b], 4 * g + 4)
                    at_least(pe, x_ready, g)
                for k in range(KX // 2 * half, KX // 2 * half + KX // 2):
                    for a in range(2):
                        last = nc.tensor.matmul(x_ps[:, KY * k:KY * k + KY],
                                                asb[:, a, 2 * k:2 * k + 2].rearrange("y x s c -> y (x s c)"),
                                                cy[:, a, :], start=(a == 0), stop=(a == 1))
                if half:
                    last.then_inc(x_psr, 1)

            def run_pass(s):
                def step(i, p, j):
                    if c := behind(i, p, j, 3):
                        t2(s, *c)
                    if c := behind(i, p, j, 2):
                        t1(s, *c)
                    if behind(i, p, j, 0):
                        main(s, i, p, j)
                    prev = behind(i, p, j, CHUNKS)
                    if prev and j >= 2:
                        f1(s, prev[0], prev[1], 2 * (j - 2))
                    if s is not STEM and (c := behind(i, p, j, -CHUNKS)):
                        i1(s, *c)
                    if prev and j >= 2:
                        f1(s, prev[0], prev[1], 2 * (j - 2) + 1)
                    if j < 2 and (c := behind(i, p, j, 2 * CHUNKS)):
                        f2(s, c[0], c[1], j)
                each_step(pe, step, 2)

            def mix(s):
                pe.wait_ge(x_ready, PAIRS * s)
                pe.wait_ge(w_cent, COUPLES * s)
                waits_apart(pe, passed)
                for r in range(KY):
                    row = (s - 1) * KY + r
                    if r >= 2:
                        pe.wait_ge(gs_a, row - 1)
                        waits_apart(pe, passed)
                    for a in range(6):
                        for b in range(2):
                            k = slice(64 * b, 64 * b + 64)
                            last = nc.tensor.matmul(
                                ps[0:IMGS, 4 * (r % 2) + b, 64 * a:64 * a + 64],
                                xsb[k, KY * a + r, :], wsb[k, KY * a + r].rearrange("k s c -> k (s c)"),
                                start=True, stop=True, tile_position=(64 * b, 0))
                    last.then_inc(mix_ready, 1)
                pe.wait_ge(gs_a, KY * s)

            def head(i, p, j):
                c = 4 * (2 * i + p) + j
                pe.wait_ge(hc_ready, 4 * rank(LAYERS, i, p) + j + 1)

                def fc1_row(y):
                    at_least(pe, a1_ready, 4 * c + y - 1)
                    nc.tensor.matmul(f1_ps[y % 2], fc1[:, y, :],
                                     hc[p][:, 4 * j:4 * j + 4, :].rearrange("c a n -> c (a n)"),
                                     start=True, stop=True).then_inc(f1_psr, 1)

                def fc2_row(y):
                    pe.wait_ge(a1_ready, 4 * c + y + 1)
                    if y % 2 == 0:
                        at_least(pe, a2_ready, 2 * c + y // 2 - 1)
                    nc.tensor.matmul(f2_ps[y // 2][64 * (y % 2):64 * (y % 2) + 64], fc2[:], a1[y % 2][:],
                                     start=True, stop=True).then_inc(f2_psr, 1)

                def fc3_rows(b):
                    pe.wait_ge(a2_ready, 2 * c + b + 1)
                    if b == 0:
                        at_least(pe, hst_ready, c)
                    ins = nc.tensor.matmul(f3_ps, fc3[:, b], a2[b][:], start=(b == 0), stop=(b == 1))
                    ins.then_inc(f3_psr, 1)

                fc1_row(0)
                fc1_row(1)
                fc2_row(0)
                fc1_row(2)
                fc2_row(1)
                fc1_row(3)
                fc2_row(2)
                fc3_rows(0)
                fc2_row(3)
                fc3_rows(1)

            def final_pass(s):
                def step(i, p, j):
                    if c := behind(i, p, j, 2):
                        t1(s, *c)
                    if behind(i, p, j, 0):
                        main(s, i, p, j)
                    if c := behind(i, p, j, -CHUNKS):
                        i1(s, *c)
                    if c := behind(i, p, j, 3):
                        head(*c)
                each_step(pe, step, 1)

            run_pass(STEM)
            with pe.Fori(1, LAYERS) as s:
                mix(s)
                for j in range(CHUNKS):
                    i1(s, 0, 0, j)
                run_pass(s)
            mix(LAYERS)
            for j in range(CHUNKS):
                i1(LAYERS, 0, 0, j)
            final_pass(LAYERS)

        @block.scalar
        def _(act):
            act.wait_ge(const_in, NCONST)

            def square(s, i, p, j):
                q = 4 * rank(s, i, p) + j
                act.wait_ge(main_ready, q + 1)
                at_least(act, var_ready, q - 1)
                nc.scalar.activation(sq[j % 2][:].rearrange("p y c -> p (y c)"), main_ps[j % 2], ACT.Square
                                     ).then_inc(sq_ready, 1)

            def activate(s, i, p, j, func):
                q = 4 * rank(s, i, p) + j
                if s is STEM:
                    at_least(act, h_out[j], 16 * (2 * i + p - 1))
                act.wait_ge(t1_ready, q + 1)
                waits_apart(act, passed)
                nc.scalar.activation(hc[p][:, 4 * j:4 * j + 4, :].rearrange("p a n -> p (a n)"), t1_ps, func,
                                     bias=lnp[:, bass.ds(s, 1), 1], scale=lnp[:, bass.ds(s, 1), 0]
                                     ).then_inc(hc_ready, 1)

            def a_copy(s, i, p, j):
                act.wait_ge(a_psr, 4 * rank(s, i, p) + j + 1)
                for a in range(2):
                    last = nc.scalar.copy(asb[0:Y, a, :, :, 8 * j:8 * j + 4].rearrange("p x s g -> p g x s"),
                                          a_ps[:, 0].rearrange("p (g x s) -> p g x s", g=4, s=3)[:, :, :, a:a + 2])
                last.then_inc(a_ready[0], 1)

            def x_copy(s, i, p):
                act.wait_ge(x_psr, rank(s, i, p) + 1)
                nc.scalar.copy(xsb[:, :, bass.ds(4 * i + 2 * p, 2)].rearrange("p k m -> p m k"),
                               x_ps.rearrange("p (m k) -> p m k", m=2)).then_inc(x_ready, 1)

            def run_pass(s, func):
                def step(i, p, j):
                    if c := behind(i, p, j, 2):
                        activate(s, *c, func)
                    if behind(i, p, j, 0):
                        square(s, i, p, j)
                    prev = behind(i, p, j, CHUNKS)
                    if prev and j >= 2:
                        a_copy(s, prev[0], prev[1], 2 * (j - 2))
                        a_copy(s, prev[0], prev[1], 2 * (j - 2) + 1)
                    if j == 1 and (c := behind(i, p, j, 2 * CHUNKS)):
                        x_copy(s, c[0], c[1])
                each_step(act, step, 2)

            def mix(s):
                for r in range(KY):
                    act.wait_ge(gs_a, (s - 1) * KY + r + 1)
                    nc.scalar.copy(gs[r % 2][:, 1, :, 0, :], gs[r % 2][:, 0, :, 1, :])
                    nc.scalar.mul(gs[r % 2][:, 1, :, 1, :], gs[r % 2][:, 0, :, 0, :], -1.0).then_inc(gs_b, 1)

            def head(i, p, j):
                c = 4 * (2 * i + p) + j

                def gelu1(y):
                    act.wait_ge(f1_psr, 4 * c + y + 1)
                    at_least(act, f2_psr, 4 * c + y - 1)
                    nc.scalar.activation(a1[y % 2][:], f1_ps[y % 2], ACT.Gelu, bias=fc1b[:]).then_inc(a1_ready, 1)

                def gelu2(b):
                    act.wait_ge(f2_psr, 4 * c + 2 * b + 2)
                    at_least(act, f3_psr, 2 * c + b - 1)
                    nc.scalar.activation(a2[b][:], f2_ps[b], ACT.Gelu, bias=fc2b[:]).then_inc(a2_ready, 1)

                gelu1(0)
                gelu1(1)
                gelu1(2)
                gelu2(0)
                gelu1(3)
                gelu2(1)

            def final_pass(s):
                def step(i, p, j):
                    if c := behind(i, p, j, 2):
                        activate(s, *c, ACT.Identity)
                    if behind(i, p, j, 0):
                        square(s, i, p, j)
                    if c := behind(i, p, j, 3):
                        head(*c)
                each_step(act, step, 1)

            run_pass(STEM, ACT.Identity)
            with act.Fori(1, LAYERS) as s:
                mix(s)
                run_pass(s, ACT.Gelu)
            mix(LAYERS)
            final_pass(LAYERS)

        @block.vector
        def _(dve):
            for n, tile in enumerate((xin[0], xin[1], zb[0], zb[1], gt[0], gt[1], asb)):
                nc.vector.memset(tile[:], 0.0).then_inc(zeroed, 1)
            dve.wait_ge(const_in, NCONST)
            small = [(cbt[:], cbm), (cw[:].rearrange("p l y c -> p (l y) c"), cwm[:]), (f0[:], f0m[:])]
            for n, (tile, mean) in enumerate(small):
                shape = list(tile.shape)
                nc.vector.tensor_reduce(mean, tile, axis=AX.X, op=ALU.add).then_inc(small_step, 1)
                dve.wait_ge(small_step, 2 * n + 1)
                nc.vector.tensor_scalar(mean, mean, 1.0 / C, None, ALU.mult).then_inc(small_step, 1)
                dve.wait_ge(small_step, 2 * n + 2)
                nc.vector.tensor_tensor(tile, tile, mean.unsqueeze(2).to_broadcast(shape), ALU.subtract
                                        ).then_inc(consts_ready, 1)
            nc.vector.memset(mhalf[:], -0.5).then_inc(consts_ready, 1)
            dve.wait_ge(cb_out, 16)

            def reduce(s, i, p, j):
                q = 4 * rank(s, i, p) + j
                dve.wait_ge(sq_ready, q + 1)
                at_least(dve, rstd_ready, q - 1)
                nc.vector.tensor_reduce(var[j % 2][:], sq[j % 2][:], axis=AX.X, op=ALU.add).then_inc(var_ready, 1)

            def normalise(s, i, p, j):
                q = 4 * rank(s, i, p) + j
                dve.wait_ge(rstd_ready, q + 1)
                at_least(dve, t1_ready, q - 1)
                nc.vector.tensor_tensor(zt[j % 2][:], main_ps[j % 2].rearrange("p (y c) -> p y c", c=C),
                                        rstd[j % 2][:].unsqueeze(2).to_broadcast([128, YC, C]), ALU.mult
                                        ).then_inc(z_ready, 1)

            def z_copy(s, i, p, j):
                idx = 4 * (rank(s, i, p) - PAIRS) + j
                dve.wait_ge(z_psr, idx + 1)
                nc.vector.tensor_copy(zb[p][0:2 * TRIG, :, 8 * j:8 * j + 8].rearrange("k y c -> k c y"),
                                      z_ps.rearrange("k (c y) -> k c y", c=8)).then_inc(zb_ready, 1)

            def hp_copy(s, i, p, j):
                q = 4 * rank(s, i, p) + j
                dve.wait_ge(t2_ready, q + 1)
                nc.vector.tensor_copy(hp[p][:, :, YC * j:YC * j + YC], t2_ps.rearrange("p (y c) -> p c y", c=C)
                                      ).then_inc(hp_ready, 1)

            def w_sum(s, i):
                dve.wait_ge(w_in, 16 * (COUPLES * s + i + 1))
                if not (isinstance(i, int) and i == 0 and s is STEM):
                    dve.wait_ge(w_cent, COUPLES * s + i)
                nc.vector.tensor_reduce(wmean[:], wsb[:, bass.ds(i * WCH, WCH)].rearrange("p m s c -> p (m s) c"),
                                        axis=AX.X, op=ALU.add).then_inc(w_mean, 1)

            def a_copy(s, i, p, j):
                dve.wait_ge(a_psr, 4 * rank(s, i, p) + j + 1)
                for a in range(2):
                    last = nc.vector.tensor_copy(asb[0:Y, a, :, :, 8 * j + 4:8 * j + 8].rearrange("p x s g -> p g x s"),
                                                 a_ps[:, 1].rearrange("p (g x s) -> p g x s", g=4, s=3)[:, :, :, a:a + 2])
                last.then_inc(a_ready[1], 1)

            def run_pass(s, final=False):
                def step(i, p, j):
                    if not final and (c := behind(i, p, j, 3)):
                        hp_copy(s, *c)
                    if c := behind(i, p, j, 1):
                        normalise(s, *c)
                    if behind(i, p, j, 0):
                        reduce(s, i, p, j)
                    prev = None if final else behind(i, p, j, CHUNKS)
                    if prev and j >= 2:
                        a_copy(s, prev[0], prev[1], 2 * (j - 2))
                    if s is not STEM and (c := behind(i, p, j, -CHUNKS)):
                        z_copy(s, *c)
                    if prev and j >= 2:
                        a_copy(s, prev[0], prev[1], 2 * (j - 2) + 1)
                    if final and (c := behind(i, p, j, 3)):
                        out_copy(*c)
                    if not final and p == 0 and j == 1 and behind(i, p, j, 0):
                        w_sum(s, i)
                each_step(dve, step, 2)

            def out_copy(i, p, j):
                c = 4 * (2 * i + p) + j
                dve.wait_ge(f3_psr, 2 * c + 2)
                if j == 0 and not (isinstance(i, int) and i == 0):
                    dve.wait_ge(tok_out[p], 32 * i)
                nc.vector.tensor_scalar(hst[p][:, 4 * j:4 * j + 4, :].rearrange("k a n -> k (a n)"), f3_ps,
                                        fc3b[:], None, ALU.add).then_inc(hst_ready, 1)

            def mix(s):
                for r in range(KY):
                    stored(dve, s, r)
                    dve.wait_ge(mix_ready, (s - 1) * KY + r + 1)
                    nc.vector.tensor_copy(gs[r % 2][:, 0].rearrange("i (a b) s c -> i b a (s c)", b=2),
                                          ps[0:IMGS, 4 * (r % 2):4 * (r % 2) + 2, 0:384].rearrange("i b (a n) -> i b a n", a=6)
                                          ).then_inc(gs_a, 1)

            run_pass(STEM)
            with dve.Fori(1, LAYERS) as s:
                mix(s)
                for j in range(CHUNKS):
                    z_copy(s, 0, 0, j)
                run_pass(s)
            mix(LAYERS)
            for j in range(CHUNKS):
                z_copy(LAYERS, 0, 0, j)
            run_pass(LAYERS, final=True)

        @block.gpsimd
        def _(pool):
            pool.wait_ge(const_in, NCONST)
            pool.wait_ge(consts_ready, 4)

            def rstds(s, i, p, j):
                q = 4 * rank(s, i, p) + j
                pool.wait_ge(var_ready, q + 1)
                waits_apart(pool, passed)
                nc.gpsimd.tensor_scalar(ve[j % 2][:], var[j % 2][:], 1.0 / C, EPS, ALU.mult, ALU.add).then_inc(ve_ready, 1)
                pool.wait_ge(ve_ready, q + 1)
                nc.gpsimd.tensor_tensor(rstd[j % 2][:], ve[j % 2][:], mhalf[:], ALU.pow).then_inc(rstd_ready, 1)

            def w_centre(s, i):
                k = COUPLES * s + i
                chunk = wsb[:, bass.ds(i * WCH, WCH)]
                pool.wait_ge(w_mean, k + 1)
                waits_apart(pool, passed)
                nc.gpsimd.tensor_scalar(wmean[:], wmean[:], 1.0 / C, None, ALU.mult).then_inc(w_sub, 1)
                pool.wait_ge(w_sub, 2 * k + 1)
                flat = chunk.rearrange("p m s c -> p (m s) c")
                nc.gpsimd.tensor_tensor(flat, flat, wmean[:].unsqueeze(2).to_broadcast([128, 2 * WCH, C]),
                                        ALU.subtract).then_inc(w_sub, 1)
                pool.wait_ge(w_sub, 2 * k + 2)
                waits_apart(pool, passed)
                nc.gpsimd.tensor_tensor(chunk[:, :, 0, :], chunk[:, :, 0, :], sgn[:].unsqueeze(2).to_broadcast([128, WCH, C]),
                                        ALU.mult).then_inc(w_cent, 1)

            def run_pass(s, final=False):
                def step(i, p, j):
                    if behind(i, p, j, 0):
                        rstds(s, i, p, j)
                        if p == 0 and j == 1 and not final:
                            w_centre(s, i)
                each_step(pool, step, 0)

            run_pass(STEM)
            with pool.Fori(1, LAYERS) as s:
                run_pass(s)
            run_pass(LAYERS, final=True)



TH = (TXT + 1) // 2


def text_embedding(nc, t, tokens):
    with ExitStack() as ctx:
        def sb(name, shape, dt=F32):
            return ctx.enter_context(nc.sbuf_tensor(name, shape, dt))

        def sem(name):
            return ctx.enter_context(nc.semaphore(name))

        PAD = 64
        state = sb("state", [128, TXT], I32)
        pos = sb("pos", [128, TXT])
        add = [sb(f"add{b}", [128, PAD + TXT]) for b in range(2)]
        top = [sb(f"top{b}", [128, PAD + TXT]) for b in range(2)]
        args = sb("args", [128, TXT])
        idx = sb("idx", [128, 3, TH], I32)
        emb = sb("emb", [128, 3, TH, 64])
        mean = sb("mean", [128, TH])
        sq = sb("esq", [128, TH, 64])
        mhalf = sb("emh", [128, TH])
        gb = sb("gb", [128, 2, 64])
        landed = sem("txt_landed")
        scan = sem("txt_scan")
        idx_ready = sem("idx_ready")
        gathered = sem("gathered")
        var_sum = sem("txt_var")
        rstd_done = sem("txt_rstd")
        txt_ready = sem("txt_ready")
        txt_out = sem("txt_out")
        block = ctx.enter_context(nc.Block())

        @block.sync
        def _(sp):
            sp.dma_start(state[:], t["state"]).then_inc(landed, 16)
            sp.dma_start(pos[:], t["pos"]).then_inc(landed, 16)
            sp.dma_start(gb[:], t["txt_gb"]).then_inc(landed, 16)
            sp.wait_ge(txt_ready, 1)
            sp.dma_start(tokens[:, Y:Y + TH, :], emb[0:64, 0]).then_inc(txt_out, 16)
            sp.dma_start(tokens[:, Y + TH:TOK, :], emb[64:128, 0, 0:TXT - TH]).then_inc(txt_out, 16)
            sp.wait_ge(txt_out, 32)

        @block.gpsimd
        def _(pool):
            pool.wait_ge(idx_ready, 1)
            for k, name in enumerate(("token_emb", "instr_emb", "arg_emb")):
                for c in range(TH):
                    nc.gpsimd.indirect_dma_start(
                        out=emb[:, k, c, :], out_offset=None, in_=t[name],
                        in_offset=bass.IndirectOffsetOnAxis(ap=idx[:, k, c:c + 1], axis=0)).then_inc(gathered, 16)
            pool.wait_ge(var_sum, 2)
            nc.gpsimd.tensor_tensor(mean[:], mean[:], mhalf[:], ALU.pow).then_inc(rstd_done, 1)

        @block.vector
        def _(dve):
            n = 0

            def link(ins):
                nonlocal n
                n += 1
                ins.then_inc(scan, 1)
                dve.wait_ge(scan, n)

            for b in range(2):
                nc.vector.memset(add[b][:], 0.0).then_inc(scan, 1)
                nc.vector.memset(top[b][:], 0.0).then_inc(scan, 1)
            nc.vector.memset(idx[:], 0).then_inc(scan, 1)
            nc.vector.memset(mhalf[:], -0.5).then_inc(scan, 1)
            n = 6
            dve.wait_ge(scan, n)
            dve.wait_ge(landed, 48)
            link(nc.vector.tensor_scalar(add[0][:, PAD + 1:], state[:, 0:TXT - 1], 5.0, None, ALU.is_equal))
            link(nc.vector.tensor_tensor(top[0][:, PAD:], add[0][:, PAD:], pos[:], ALU.mult))
            b = 0
            for s in (1, 2, 4, 8, 16, 32, 64):
                nc.vector.tensor_tensor(add[1 - b][:, PAD:], add[b][:, PAD:], add[b][:, PAD - s:PAD - s + TXT],
                                        ALU.add).then_inc(scan, 1)
                nc.vector.tensor_tensor(top[1 - b][:, PAD:], top[b][:, PAD:], top[b][:, PAD - s:PAD - s + TXT],
                                        ALU.max).then_inc(scan, 1)
                n += 2
                dve.wait_ge(scan, n)
                b = 1 - b
            link(nc.vector.tensor_tensor(args[:], pos[:], top[b][:, PAD:], ALU.subtract))
            for half in range(2):
                k, r, w = TH * half, slice(64 * half, 64 * half + 64), TH if half == 0 else TXT - TH
                for m, src in enumerate((state[r, k:k + w], add[b][r, PAD + k:PAD + k + w], args[r, k:k + w])):
                    link(nc.vector.tensor_copy(idx[r, m, 0:w], src))
            nc.vector.tensor_copy(mean[:, 0:1], args[:, 0:1]).then_inc(idx_ready, 1)
            dve.wait_ge(gathered, 16 * 3 * TH)
            e = emb[:, 0]
            wide = [128, TH, 64]
            link(nc.vector.tensor_tensor(e, e, emb[:, 1], ALU.add))
            link(nc.vector.tensor_tensor(e, e, emb[:, 2], ALU.add))
            link(nc.vector.tensor_reduce(mean[:], e, axis=AX.X, op=ALU.add))
            link(nc.vector.tensor_scalar(mean[:], mean[:], 1.0 / 64, None, ALU.mult))
            link(nc.vector.tensor_tensor(e, e, mean[:].unsqueeze(2).to_broadcast(wide), ALU.subtract))
            link(nc.vector.tensor_tensor(sq[:], e, e, ALU.mult))
            nc.vector.tensor_reduce(mean[:], sq[:], axis=AX.X, op=ALU.add).then_inc(var_sum, 1)
            dve.wait_ge(var_sum, 1)
            nc.vector.tensor_scalar(mean[:], mean[:], 1.0 / 64, EPS, ALU.mult, ALU.add).then_inc(var_sum, 1)
            dve.wait_ge(rstd_done, 1)
            link(nc.vector.tensor_tensor(e, e, mean[:].unsqueeze(2).to_broadcast(wide), ALU.mult))
            link(nc.vector.tensor_tensor(e, e, gb[:, 0:1, :].to_broadcast(wide), ALU.mult))
            nc.vector.tensor_tensor(e, e, gb[:, 1:2, :].to_broadcast(wide), ALU.add).then_inc(txt_ready, 1)


BLK = TOK // 3
KEYS = 119
KEY0 = [0, 11, 22]
HEADS, HD = 8, 8
HID, EXPERTS = 128, 16
QPAD = 160
assert 3 * BLK == TOK and KEY0[2] + KEYS == TOK


def attention_and_experts(nc, t, tokens, out):
    with ExitStack() as ctx:
        def sb(name, shape, dt=F32):
            return ctx.enter_context(nc.sbuf_tensor(name, shape, dt))

        def sem(name):
            return ctx.enter_context(nc.semaphore(name))

        xs = [sb(f"xs{p}", [128, 3, 64]) for p in range(2)]
        xr = [sb(f"xr{p}", [128, 3, 64]) for p in range(2)]
        xn = sb("xn", [128, 3, 64])
        xsq = sb("xsq", [128, 3, 64])
        st1 = sb("st1", [128, 3])
        mu1 = sb("mu1", [128, 3])
        va1 = sb("va1", [128, 3])
        rs1 = sb("rs1", [128, 3])
        xT = sb("xT", [128, 2, QPAD])
        qT = [sb(f"qT{p}", [128, 2, QPAD]) for p in range(2)]
        kT = sb("kT", [64, 2, TOK])
        km = [sb(f"km{p}", [128, 2, HEADS, TOK]) for p in range(2)]
        vv = [sb(f"vv{p}", [KEYS, 2, 3, 64]) for p in range(2)]
        sm = [sb(f"sm{b}", [128, HEADS, KEYS]) for b in range(2)]
        mx = [sb(f"mx{b}", [128, HEADS]) for b in range(2)]
        den = [sb(f"den{p}", [128, 3, HEADS]) for p in range(2)]
        rden = sb("rden", [128, 3, HEADS])
        pT = sb("pT", [KEYS, HEADS, 128])
        osb = sb("osb", [128, 3, 64])
        oT = sb("oT", [128, 3, 128])
        h1 = [sb(f"h1{p}", [128, 3, 64]) for p in range(2)]
        h1b = [sb(f"h1b{p}", [128, 3, 64]) for p in range(2)]
        yn = sb("yn", [128, 3, 64])
        ysq = sb("ysq", [128, 3, 64])
        st2 = sb("st2", [128, 3])
        mu2 = sb("mu2", [128, 3])
        va2 = sb("va2", [128, 3])
        rs2 = sb("rs2", [128, 3])
        yT = sb("yT", [128, 3, 128])
        ff = [sb(f"ff{k}", [128, 3, 2, 64]) for k in range(3)]
        wc = [sb(f"wc{p}", [128, 2, 2, HID]) for p in range(2)]
        bc = [sb(f"bc{p}", [128, 2, 2]) for p in range(2)]
        fin = [sb(f"fin{p}", [128, 3, 64]) for p in range(2)]

        ident = sb("identt", [128, 128])
        mask = sb("mask", [128, 3, KEYS])
        hmask = sb("hmask", [64, HEADS])
        temp = sb("temp", [64, 1])
        mh = sb("mh", [128, 3])
        wq = sb("wq", [128, 64])
        wk = sb("wk", [128, 64])
        wv = sb("wv", [128, 64])
        wp = sb("wp", [128, 64])
        wi = sb("wi", [128, HID])
        bi = sb("bi", [128, 1])
        wr = sb("wr", [128, 2, EXPERTS, HID])
        ws = sb("ws", [128, 2, HID])
        br = sb("br", [128, 2, EXPERTS])
        bs = sb("bs", [128, 2])
        wo = sb("wo", [128, 64])
        bo = sb("bo", [128, 64])
        route = sb("route", [1, IMGS], I32)

        ps = ctx.enter_context(nc.psum_tensor("pst", [128, 8, 512], F32))
        s_ps = ps[:, 0:2, 0:4 * KEYS]
        p_ps = ps[0:KEYS, 2:4, :]
        o_ps = ps[:, 4, 0:192]
        fr_ps = [ps[:, 5, :], ps[:, 6, :]]
        ff_ps = ps[:, 7, :]

        t_const = sem("t_const")
        t_zero = sem("t_zero")
        t_passed = sem("t_passed")
        t_setup = sem("t_setup")
        xs_in = [sem(f"xs_in{p}") for p in range(2)]
        xr_in = [sem(f"xr_in{p}") for p in range(2)]
        c1 = sem("c1")
        va1_ready = sem("va1_ready")
        rs1_ready = sem("rs1_ready")
        xn_ready = sem("xn_ready")
        xT_psr = sem("xT_psr")
        xT_ready = sem("xT_ready")
        q_psr = sem("q_psr")
        k_psr = sem("k_psr")
        q_ready = sem("q_ready")
        k_ready = sem("k_ready")
        km_ready = sem("km_ready")
        v_psr = sem("v_psr")
        v_ready = sem("v_ready")
        s_psr = sem("s_psr")
        sm_ready = sem("sm_ready")
        mx_ready = sem("mx_ready")
        sub_ready = sem("sub_ready")
        exp_ready = sem("exp_ready")
        den_ready = sem("den_ready")
        p_psr = sem("p_psr")
        pT_ready = sem("pT_ready")
        o_psr = sem("o_psr")
        rden_ready = sem("rden_ready")
        osb_ready = sem("osb_ready")
        oT_psr = sem("oT_psr")
        oT_ready = sem("oT_ready")
        pr_psr = sem("pr_psr")
        h1_ready = sem("h1_ready")
        h1b_ready = sem("h1b_ready")
        c2 = sem("c2")
        va2_ready = sem("va2_ready")
        rs2_ready = sem("rs2_ready")
        yn_ready = sem("yn_ready")
        yT_psr = sem("yT_psr")
        yT_ready = sem("yT_ready")
        f_psr = sem("f_psr")
        f_ready = sem("f_ready")
        wc_ready = sem("wc_ready")
        y_psr = sem("y_psr")
        fin_ready = sem("fin_ready")
        fin_out = [sem(f"fin_out{p}") for p in range(2)]

        loads = [(ident, "ident"), (mask, "mask"), (hmask, "hmask"), (temp, "temp"), (wq, "wq"), (wk, "wk"),
                 (wv, "wv"), (wp, "wp"), (wi, "wi"), (bi, "bi"), (wr, "wr"), (ws, "ws"), (br, "br"), (bs, "bs"),
                 (wo, "wo"), (bo, "bo"), (route, "route")]
        block = ctx.enter_context(nc.Block())

        def at(i, p, b, lag):
            return behind(i, p, b, lag, 3)

        def num(i, p):
            return 2 * i + p

        @block.sync
        def _(sp):
            for dst, name in loads:
                sp.dma_start(dst[:], t[name]).then_inc(t_const, 16)
            sp.wait_ge(t_zero, 8)
            sp.wait_ge(t_setup, 2)

            def load(dst, i, p, done):
                for m in range(2):
                    sp.dma_start(dst[64 * m:64 * m + BLK], tokens[bass.ds(2 * num(i, p) + m, 1)]
                                 .rearrange("a (b r) d -> (a r) b d", b=3)).then_inc(done, 16)
            for p in range(2):
                load(xs[p], 0, p, xs_in[p])

            def step(i, p, b):
                if b == 0 and at(i, p, 0, 0):
                    if not (isinstance(i, int) and i == 0):
                        sp.wait_ge(h1_ready, num(i, p) - 1)
                        waits_apart(sp, t_passed)
                    load(xr[p], i, p, xr_in[p])
                if b == 0 and at(i, p, 0, 0) and (c := at(i, p, 0, -6)):
                    sp.wait_ge(xn_ready, num(i, p) + 1)
                    waits_apart(sp, t_passed)
                    load(xs[p], c[0], c[1], xs_in[p])
                if b == 2 and (c := at(i, p, 0, 6)):
                    sp.wait_ge(fin_ready, num(c[0], c[1]) + 1)
                    waits_apart(sp, t_passed)
                    for m in range(2):
                        sp.dma_start(out[bass.ds(2 * num(c[0], c[1]) + m, 1)].rearrange("a (b r) d -> (a r) b d", b=3),
                                     fin[c[1]][64 * m:64 * m + BLK]).then_inc(fin_out[c[1]], 16)
            each_step(sp, step, 2, 3)
            for p in range(2):
                sp.wait_ge(fin_out[p], 32 * COUPLES)

        @block.tensor
        def _(pe):
            pe.wait_ge(t_const, 16 * len(loads))
            pe.wait_ge(t_zero, 8)
            pe.wait_ge(t_setup, 6)

            def front1(i, p):
                g = num(i, p)
                pe.wait_ge(xn_ready, g + 1)
                at_least(pe, q_ready, g)
                waits_apart(pe, t_passed)
                for b in range(3):
                    last = nc.tensor.transpose(fr_ps[0][0:64, 128 * b:128 * b + 128], xn[:, b, :], ident[:])
                last.then_inc(xT_psr, 1)

            def front2(i, p):
                g = num(i, p)
                pe.wait_ge(xT_ready, g + 1)
                at_least(pe, v_ready, g)
                nc.tensor.matmul(fr_ps[1][0:64, 0:2 * TOK], wk[:], xT[:, :, 0:TOK], start=True, stop=True).then_inc(k_psr, 1)
                nc.tensor.matmul(fr_ps[0][0:64, 0:2 * TOK], wq[:], xT[:, :, 0:TOK], start=True, stop=True).then_inc(q_psr, 1)

            def front3(i, p):
                pe.wait_ge(k_ready, num(i, p) + 1)
                for m in range(2):
                    for b in range(3):
                        o = 64 * (3 * m + b)
                        last = nc.tensor.matmul(fr_ps[1][0:KEYS, o:o + 64], xT[:, m, KEY0[b]:KEY0[b] + KEYS], wv[:],
                                                start=True, stop=True)
                last.then_inc(v_psr, 1)

            def scores(i, p, b):
                k = 3 * num(i, p) + b
                if b == 0:
                    pe.wait_ge(km_ready, num(i, p) + 1)
                    pe.wait_ge(q_ready, num(i, p) + 1)
                at_least(pe, sm_ready, k)
                for h in range(2):
                    for m in range(2):
                        last = nc.tensor.matmul(s_ps[64 * m:64 * m + 64, h, :], qT[p][:, m, BLK * b:BLK * b + 64],
                                                km[p][:, m, 4 * h:4 * h + 4, KEY0[b]:KEY0[b] + KEYS],
                                                start=True, stop=True)
                last.then_inc(s_psr, 1)

            def turn(i, p, b):
                k = 3 * num(i, p) + b
                pe.wait_ge(exp_ready, k + 1)
                at_least(pe, pT_ready, k)
                for h in range(HEADS):
                    last = nc.tensor.transpose(p_ps[:, h // 4, 128 * (h % 4):128 * (h % 4) + 128],
                                               sm[(3 * p + b) % 2][:, h, :], ident[:])
                last.then_inc(p_psr, 1)

            def values(i, p, b):
                k = 3 * num(i, p) + b
                pe.wait_ge(pT_ready, k + 1)
                if b == 0:
                    pe.wait_ge(v_ready, num(i, p) + 1)
                    at_least(pe, osb_ready, num(i, p))
                for h in range(HEADS):
                    for m in range(2):
                        last = nc.tensor.matmul(o_ps[64 * m:64 * m + 64, 64 * b + HD * h:64 * b + HD * h + HD],
                                                pT[:, h, 64 * m:64 * m + 64], vv[p][:, m, b, HD * h:HD * h + HD],
                                                start=True, stop=True)
                last.then_inc(o_psr, 1)

            def back_o(i, p):
                g = num(i, p)
                pe.wait_ge(osb_ready, g + 1)
                at_least(pe, fin_ready, g)
                waits_apart(pe, t_passed)
                for b in range(3):
                    last = nc.tensor.transpose(ff_ps[0:64, 128 * b:128 * b + 128], osb[:, b, :], ident[:])
                last.then_inc(oT_psr, 1)

            def back_proj(i, p):
                pe.wait_ge(oT_ready, num(i, p) + 1)
                for b in range(3):
                    last = nc.tensor.matmul(ff_ps[:, 64 * b:64 * b + 64], oT[:, b, :], wp[:], start=True, stop=True)
                last.then_inc(pr_psr, 1)

            def back_y(i, p):
                g = num(i, p)
                pe.wait_ge(yn_ready, g + 1)
                pe.wait_ge(h1_ready, g + 1)
                waits_apart(pe, t_passed)
                for b in range(3):
                    last = nc.tensor.transpose(ff_ps[0:64, 128 * b:128 * b + 128], yn[:, b, :], ident[:])
                last.then_inc(yT_psr, 1)

            def back_in(i, p):
                pe.wait_ge(yT_ready, num(i, p) + 1)
                nc.tensor.matmul(ff_ps[:, 0:384], wi[:], yT[:].rearrange("d b n -> d (b n)"),
                                 start=True, stop=True).then_inc(f_psr, 1)

            def back_layer(i, p, l):
                g = num(i, p)
                pe.wait_ge(f_ready, 3 * g + l + 1)
                if l == 0:
                    pe.wait_ge(wc_ready, g + 1)
                for m in range(2):
                    last = nc.tensor.matmul(ff_ps[:, 192 * m:192 * m + 192], wc[p][:, l, m, :], ff[l][:, :, m, :],
                                            start=True, stop=True)
                last.then_inc(f_psr, 1)

            def back_out(i, p):
                pe.wait_ge(f_ready, 3 * num(i, p) + 3)
                for b in range(3):
                    last = nc.tensor.matmul(ff_ps[:, 64 * b:64 * b + 64], ff[2][:, b].rearrange("k m n -> k (m n)"), wo[:],
                                            start=True, stop=True)
                last.then_inc(y_psr, 1)

            front1(0, 0)
            front2(0, 0)
            front3(0, 0)

            def step(i, p, b):
                here, prev, old = at(i, p, 0, 0), at(i, p, 0, 3), at(i, p, 0, 6)
                nxt = here and at(i, p, 0, -3)
                if here:
                    scores(i, p, b)
                if b == 0 and nxt:
                    front1(*nxt[0:2])
                if b == 0 and old:
                    back_layer(old[0], old[1], 0)
                if b == 1 and prev:
                    back_o(*prev[0:2])
                if b == 2 and prev:
                    back_y(*prev[0:2])
                if c := at(i, p, b, 1):
                    turn(*c)
                if b == 0 and nxt:
                    front2(*nxt[0:2])
                if b == 0 and old:
                    back_layer(old[0], old[1], 1)
                if b == 1 and nxt:
                    front3(*nxt[0:2])
                if b == 1 and prev:
                    back_proj(*prev[0:2])
                if b == 2 and prev:
                    back_in(*prev[0:2])
                if c := at(i, p, b, 1):
                    values(*c)
                if b == 0 and old:
                    back_out(*old[0:2])
            each_step(pe, step, 2, 3)

        @block.scalar
        def _(act):
            act.wait_ge(t_zero, 8)
            act.wait_ge(t_const, 16 * len(loads))

            def xT_copy(i, p):
                g = num(i, p)
                act.wait_ge(xT_psr, g + 1)
                at_least(act, v_psr, g)
                nc.scalar.copy(xT[0:64, :, 0:TOK].rearrange("d m (b r) -> d b m r", b=3),
                               fr_ps[0][0:64, 0:384].rearrange("d (b m r) -> d b m r", b=3, m=2)[:, :, :, 0:BLK]
                               ).then_inc(xT_ready, 1)

            def qk_copy(i, p):
                g = num(i, p)
                act.wait_ge(k_psr, g + 1)
                at_least(act, km_ready, g)
                nc.scalar.copy(kT[:].rearrange("d m n -> d (m n)"), fr_ps[1][0:64, 0:2 * TOK]).then_inc(k_ready, 1)
                act.wait_ge(q_psr, g + 1)
                nc.scalar.copy(qT[p][0:64, :, 0:TOK], fr_ps[0][0:64, 0:2 * TOK].rearrange("d (m n) -> d m n", m=2)
                               ).then_inc(q_ready, 1)

            def v_copy(i, p):
                act.wait_ge(v_psr, num(i, p) + 1)
                nc.scalar.copy(vv[p][:].rearrange("k m b d -> k (m b d)"), fr_ps[1][0:KEYS, 0:384]).then_inc(v_ready, 1)

            def exp(i, p, b):
                act.wait_ge(sub_ready, 3 * num(i, p) + b + 1)
                tile = sm[(3 * p + b) % 2][:].rearrange("p h k -> p (h k)")
                nc.scalar.activation(tile, tile, ACT.Exp).then_inc(exp_ready, 1)

            def pT_copy(i, p, b):
                k = 3 * num(i, p) + b
                act.wait_ge(p_psr, k + 1)
                at_least(act, o_psr, k)
                nc.scalar.copy(pT[:].rearrange("k h n -> k (h n)"), p_ps.rearrange("k a n -> k (a n)")).then_inc(pT_ready, 1)

            def oT_copy(i, p):
                act.wait_ge(oT_psr, num(i, p) + 1)
                nc.scalar.copy(oT[0:64].rearrange("d b n -> d (b n)"), ff_ps[0:64, 0:384]).then_inc(oT_ready, 1)

            def yT_copy(i, p):
                act.wait_ge(yT_psr, num(i, p) + 1)
                nc.scalar.copy(yT[0:64].rearrange("d b n -> d (b n)"), ff_ps[0:64, 0:384]).then_inc(yT_ready, 1)

            def relu_in(i, p):
                act.wait_ge(f_psr, 3 * num(i, p) + 1)
                nc.scalar.activation(ff[0][:].rearrange("k b m n -> k (b m n)"), ff_ps[:, 0:384], ACT.Relu, bias=bi[:]
                                     ).then_inc(f_ready, 1)

            def relu_layer(i, p, l):
                act.wait_ge(f_psr, 3 * num(i, p) + l + 2)
                for m in range(2):
                    last = nc.scalar.activation(ff[l + 1][:, :, m, :], ff_ps[:, 192 * m:192 * m + 192]
                                                .rearrange("k (b n) -> k b n", b=3), ACT.Relu, bias=bc[p][:, m, l:l + 1])
                last.then_inc(f_ready, 1)

            xT_copy(0, 0)
            qk_copy(0, 0)
            v_copy(0, 0)

            def step(i, p, b):
                here, prev, old = at(i, p, 0, 0), at(i, p, 0, 3), at(i, p, 0, 6)
                nxt = here and at(i, p, 0, -3)
                if b == 0 and nxt:
                    xT_copy(*nxt[0:2])
                if b == 0 and old:
                    relu_layer(old[0], old[1], 0)
                if b == 1 and prev:
                    oT_copy(*prev[0:2])
                if b == 2 and prev:
                    yT_copy(*prev[0:2])
                if c := at(i, p, b, 1):
                    pT_copy(*c)
                if b == 0 and nxt:
                    qk_copy(*nxt[0:2])
                if b == 0 and old:
                    relu_layer(old[0], old[1], 1)
                if b == 1 and nxt:
                    v_copy(*nxt[0:2])
                if b == 2 and prev:
                    relu_in(*prev[0:2])
                if here:
                    exp(i, p, b)
            each_step(act, step, 2, 3)

        @block.vector
        def _(dve):
            for tile in (xs[0], xs[1], xT, qT[0], qT[1], km[0], km[1], yT):
                nc.vector.memset(tile[:], 0.0).then_inc(t_zero, 1)
            nc.vector.memset(xr[0][:], 0.0).then_inc(t_setup, 1)
            nc.vector.memset(xr[1][:], 0.0).then_inc(t_setup, 1)
            nc.vector.memset(oT[:], 0.0).then_inc(c1, 1)
            nc.vector.memset(mh[:], -0.5)
            dve.wait_ge(c1, 1)
            nc.vector.memset(oT[64:65], 1.0).then_inc(t_setup, 1)
            dve.wait_ge(t_const, 16 * len(loads))
            nc.vector.tensor_tensor(ws[:], ws[:], ident[:].unsqueeze(1).to_broadcast([128, 2, 128]), ALU.add).then_inc(t_setup, 1)
            nc.vector.tensor_tensor(br[:], br[:], bs[:].unsqueeze(2).to_broadcast([128, 2, EXPERTS]), ALU.add).then_inc(t_setup, 1)
            nc.vector.tensor_scalar(hmask[:], hmask[:], temp[:], None, ALU.mult).then_inc(t_setup, 1)
            dve.wait_ge(t_setup, 6)

            def norm(x, n, sq, st, mu, va, chain, base, va_ready, g, free):
                wide = [128, 3, 64]
                nc.vector.tensor_reduce(st[:], x[:], axis=AX.X, op=ALU.add).then_inc(chain, 1)
                dve.wait_ge(chain, base + 4 * g + 1)
                nc.vector.tensor_scalar(mu[:], st[:], 1.0 / 64, None, ALU.mult).then_inc(chain, 1)
                dve.wait_ge(chain, base + 4 * g + 2)
                free()
                nc.vector.tensor_tensor(n[:], x[:], mu[:].unsqueeze(2).to_broadcast(wide), ALU.subtract).then_inc(chain, 1)
                dve.wait_ge(chain, base + 4 * g + 3)
                nc.vector.tensor_tensor(sq[:], n[:], n[:], ALU.mult).then_inc(chain, 1)
                dve.wait_ge(chain, base + 4 * g + 4)
                nc.vector.tensor_reduce(va[:], sq[:], axis=AX.X, op=ALU.add).then_inc(va_ready, 1)

            def norm_end(n, rs, rs_ready, n_ready, g):
                dve.wait_ge(rs_ready, 2 * g + 2)
                nc.vector.tensor_tensor(n[:], n[:], rs[:].unsqueeze(2).to_broadcast([128, 3, 64]), ALU.mult).then_inc(n_ready, 1)

            def norm1(i, p):
                g = num(i, p)
                dve.wait_ge(xs_in[p], 32 * (i + 1))
                norm(xs[p], xn, xsq, st1, mu1, va1, c1, 1, va1_ready, g,
                     lambda: at_least(dve, xT_psr, g))

            def norm1_end(i, p):
                norm_end(xn, rs1, rs1_ready, xn_ready, num(i, p))

            def masked(i, p, b):
                k = 3 * num(i, p) + b
                dve.wait_ge(s_psr, k + 1)
                at_least(dve, p_psr, k - 1)
                at_least(dve, den_ready, k - 1)
                tile = sm[(3 * p + b) % 2]
                nc.vector.tensor_tensor(tile[:].rearrange("p (a h) k -> p a h k", a=2),
                                        s_ps.rearrange("p a (h k) -> p a h k", h=4),
                                        mask[:, b, :].unsqueeze(1).unsqueeze(1).to_broadcast([128, 2, 4, KEYS]),
                                        ALU.add).then_inc(sm_ready, 1)
                dve.wait_ge(sm_ready, k + 1)
                at_least(dve, sub_ready, k - 1)
                nc.vector.tensor_reduce(mx[(3 * p + b) % 2][:], tile[:], axis=AX.X, op=ALU.max).then_inc(mx_ready, 1)

            def total(i, p, b):
                k = 3 * num(i, p) + b
                dve.wait_ge(exp_ready, k + 1)
                nc.vector.tensor_reduce(den[p][:, b, :], sm[(3 * p + b) % 2][:], axis=AX.X, op=ALU.add).then_inc(den_ready, 1)

            def o_norm(i, p):
                g = num(i, p)
                dve.wait_ge(den_ready, 3 * g + 3)
                nc.vector.reciprocal(rden[:], den[p][:]).then_inc(rden_ready, 1)
                dve.wait_ge(rden_ready, g + 1)
                dve.wait_ge(o_psr, 3 * g + 3)
                at_least(dve, oT_psr, g)
                nc.vector.tensor_tensor(osb[:].rearrange("p b (h d) -> p (b h) d", h=HEADS),
                                        o_ps.rearrange("p (c d) -> p c d", d=HD),
                                        rden[:].rearrange("p b h -> p (b h)").unsqueeze(2).to_broadcast([128, 24, HD]),
                                        ALU.mult).then_inc(osb_ready, 1)

            def residual(i, p):
                g = num(i, p)
                dve.wait_ge(pr_psr, g + 1)
                dve.wait_ge(xr_in[p], 32 * (i + 1))
                at_least(dve, h1b_ready, g - 1)
                nc.vector.tensor_tensor(h1[p][:], ff_ps[:, 0:192].rearrange("p (b d) -> p b d", b=3), xr[p][:], ALU.add
                                        ).then_inc(h1_ready, 1)
                dve.wait_ge(h1_ready, g + 1)
                norm(h1[p], yn, ysq, st2, mu2, va2, c2, 0, va2_ready, g,
                     lambda: at_least(dve, yT_psr, g))

            def weights(i, p):
                g = num(i, p)
                at_least(dve, y_psr, g - 1)
                for m in range(2):
                    e = dve.value_load(route[0:1, bass.ds(4 * i + 2 * p + m, 1)], min_val=0, max_val=EXPERTS - 1)
                    nc.vector.tensor_tensor(wc[p][:, :, m, :], wr[:, :, bass.ds(e, 1), :].rearrange("p l a n -> p l (a n)"), ws[:], ALU.add)
                    last = nc.vector.tensor_copy(bc[p][:, m, :], br[:, :, bass.ds(e, 1)].rearrange("p l a -> p (l a)"))
                last.then_inc(wc_ready, 1)

            def final(i, p):
                g = num(i, p)
                dve.wait_ge(y_psr, g + 1)
                dve.wait_ge(h1b_ready, g + 1)
                at_least(dve, fin_out[p], 32 * i)
                nc.vector.tensor_tensor(fin[p][:], ff_ps[:, 0:192].rearrange("p (b d) -> p b d", b=3), h1b[p][:], ALU.add
                                        ).then_inc(fin_ready, 1)

            for p in range(2):
                norm1(0, p)
                norm1_end(0, p)

            def step(i, p, b):
                here, prev, old = at(i, p, 0, 0), at(i, p, 0, 3), at(i, p, 0, 6)
                nxt2 = here and at(i, p, 0, -6)
                if here:
                    masked(i, p, b)
                if b == 2 and prev:
                    norm_end(yn, rs2, rs2_ready, yn_ready, num(prev[0], prev[1]))
                if b == 2 and nxt2:
                    norm1(*nxt2[0:2])
                if c := at(i, p, b, 1):
                    total(*c)
                if b == 2 and nxt2:
                    norm1_end(*nxt2[0:2])
                if b == 0 and prev:
                    o_norm(*prev[0:2])
                if b == 0 and old:
                    final(*old[0:2])
                if b == 1 and here:
                    weights(i, p)
                if b == 1 and prev:
                    residual(*prev[0:2])
            each_step(dve, step, 2, 3)

        @block.gpsimd
        def _(pool):
            pool.wait_ge(t_setup, 6)

            def power(va, rs, va_ready, rs_ready, i, p):
                g = num(i, p)
                pool.wait_ge(va_ready, g + 1)
                waits_apart(pool, t_passed)
                nc.gpsimd.tensor_scalar(va[:], va[:], 1.0 / 64, EPS, ALU.mult, ALU.add).then_inc(rs_ready, 1)
                pool.wait_ge(rs_ready, 2 * g + 1)
                nc.gpsimd.tensor_tensor(rs[:], va[:], mh[:], ALU.pow).then_inc(rs_ready, 1)

            def keys(i, p):
                g = num(i, p)
                pool.wait_ge(k_ready, g + 1)
                at_least(pool, s_psr, 3 * (g - 1))
                for m in range(2):
                    last = nc.gpsimd.tensor_tensor(km[p][0:64, m], kT[:, m:m + 1, :].to_broadcast([64, HEADS, TOK]),
                                                   hmask[:].unsqueeze(2).to_broadcast([64, HEADS, TOK]), ALU.mult)
                last.then_inc(km_ready, 1)

            def shift(i, p, b):
                pool.wait_ge(mx_ready, 3 * num(i, p) + b + 1)
                n = (3 * p + b) % 2
                nc.gpsimd.tensor_tensor(sm[n][:], sm[n][:], mx[n][:].unsqueeze(2).to_broadcast([128, HEADS, KEYS]),
                                        ALU.subtract).then_inc(sub_ready, 1)

            def with_bias(i, p):
                g = num(i, p)
                pool.wait_ge(h1_ready, g + 1)
                at_least(pool, fin_ready, g - 1)
                nc.gpsimd.tensor_tensor(h1b[p][:], h1[p][:], bo[:].unsqueeze(1).to_broadcast([128, 3, 64]), ALU.add
                                        ).then_inc(h1b_ready, 1)

            for p in range(2):
                power(va1, rs1, va1_ready, rs1_ready, 0, p)
            keys(0, 0)

            def step(i, p, b):
                here, prev = at(i, p, 0, 0), at(i, p, 0, 3)
                nxt, nxt2 = here and at(i, p, 0, -3), here and at(i, p, 0, -6)
                if here:
                    shift(i, p, b)
                if b == 0 and nxt:
                    keys(*nxt[0:2])
                if b == 1 and prev:
                    power(va2, rs2, va2_ready, rs2_ready, *prev[0:2])
                    with_bias(*prev[0:2])
                if b == 2 and nxt2:
                    power(va1, rs1, va1_ready, rs1_ready, *nxt2[0:2])
            each_step(pool, step, 1, 3)


def layouts(inp):
    f = lambda k: np.asarray(inp[k])
    out = {}
    x = f("x").reshape(PAIRS, 2, CHUNKS, YC, X, 3)
    out["x"] = x.transpose(0, 3, 5, 2, 1, 4).reshape(PAIRS, 48, CHUNKS, 128)
    wr, wi = (np.concatenate([f("L0_tok_w1" + a), f("L0_tok_w2" + a)], axis=3)
              .reshape(LAYERS, C, C, KY, 6, 2).transpose(0, 5, 1, 4, 3, 2) for a in "ri")
    w = np.empty((LAYERS, 2, 2, C, 6, KY, 2, C), np.float32)
    w[:, :, 0, ..., 0, :], w[:, :, 0, ..., 1, :] = wr, wi
    w[:, :, 1, ..., 0, :], w[:, :, 1, ..., 1, :] = wi, wr
    out["w"] = w.reshape(LAYERS, 128, MODES, 2, C)
    cw = np.zeros((4, C, LAYERS, 4, C), np.float32)
    fc0 = np.zeros((128, YC, C), np.float32)
    fc1 = np.zeros((4, C, 4, 128), np.float32)
    for y in range(4):
        cw[y, :, :, y, :] = f("L0_tok_conv_w").transpose(2, 0, 1)
        fc1[y, :, y] = f("L0_tok_fc1_w")
    for y in range(YC):
        fc0[3 * y:3 * y + 3, y] = f("L0_tok_fc0_w")
    fc0[48] = f("L0_tok_fc0_b")
    out["conv_w"] = cw.reshape(128, LAYERS, 4, C)
    out["fc0"] = fc0
    out["conv_b"] = np.repeat(f("L0_tok_conv_b")[:, None, :], Y, axis=1)
    g = np.concatenate([f("L0_tok_ln0_g")[None], f("L0_tok_ln_g")])
    b = np.concatenate([f("L0_tok_ln0_b")[None], f("L0_tok_ln_b")])
    out["lnp"] = np.tile(np.stack([g, b], axis=-1).transpose(1, 0, 2), (4, 1, 1))
    out["fc1_w"] = fc1.reshape(128, 4, 128)
    out["fc1_b"] = f("L0_tok_fc1_b")[:, None]
    out["fc2_w"] = f("L0_tok_fc2_w")
    out["fc2_b"] = np.tile(f("L0_tok_fc2_b"), 2)[:, None]
    fc3 = np.zeros((2, 64, 2, 4), np.float32)
    for b_ in range(2):
        for y in range(2):
            fc3[y, :, b_, 2 * b_ + y] = f("L0_tok_fc3_w")[:, 0]
    out["fc3_w"] = fc3.reshape(128, 2, 4)
    out["fc3_b"] = np.repeat(f("L0_tok_fc3_b")[:, None], 4, axis=0)
    st = f("x_txt")
    out["state"] = np.concatenate([st, st]).astype(np.int32)
    out["pos"] = np.tile(np.arange(TXT, dtype=np.float32), (128, 1))
    out["txt_gb"] = np.tile(np.stack([f("L0_txt_gamma"), f("L0_txt_beta")])[None], (128, 1, 1))
    for k in ("token_emb", "instr_emb", "arg_emb"):
        out[k] = f("L0_txt_" + k)
    rows = lambda a: np.concatenate([a, np.zeros((128 - len(a),) + a.shape[1:])])
    mask = np.zeros((128, 3, KEYS), np.float32)
    for b_ in range(3):
        q, k = (a // 11 * np.array([1]) for a in (BLK * b_ + np.arange(BLK), KEY0[b_] + np.arange(KEYS)))
        qc, kc = (BLK * b_ + np.arange(BLK)) % 11, (KEY0[b_] + np.arange(KEYS)) % 11
        far = (abs(q[:, None] - k[None]) > 3) | (abs(qc[:, None] - kc[None]) > 3)
        for m in range(2):
            mask[64 * m:64 * m + BLK, b_] = np.where(far, -1e30, 0)
    out["mask"] = mask
    out["hmask"] = np.where(np.arange(64)[:, None] // HD == np.arange(HEADS), HD ** -0.5, 0)
    out["temp"] = np.tile(f("L0_attn_temperature"), 64)[:, None]
    for n, k in enumerate(("wq", "wk", "wv")):
        out[k] = rows(f("L0_attn_W_qkv")[64 * n:64 * n + 64].T)
    out["wp"] = rows(np.concatenate([f("L0_attn_W_proj").T, f("L0_attn_b_proj")[None]]))
    out["wi"] = rows(f("L0_ffn_Wi").T)
    out["bi"] = f("L0_ffn_bi")[:, None]
    out["wr"] = f("L0_ffn_Wr").transpose(3, 0, 1, 2)
    out["ws"] = f("L0_ffn_Ws")[:, 0].transpose(2, 0, 1)
    out["br"] = f("L0_ffn_br").transpose(2, 0, 1)
    out["bs"] = f("L0_ffn_bs")[:, 0].T
    out["wo"] = f("L0_ffn_Wo").T
    out["bo"] = np.tile(f("L0_ffn_bo"), (128, 1))
    out["route"] = f("L0_ffn_route_id")[None].astype(np.int32)
    kx, n64 = np.arange(KX), np.arange(64)
    ky = np.concatenate([np.arange(KYH), np.arange(64 - KYH, 64)])
    tx = 2 * np.pi * np.outer(n64, kx) / 64
    ty = 2 * np.pi * np.outer(n64, ky) / 64
    d1 = np.zeros((2, 64, 2, KX, 3))
    ex = np.zeros((2, KX, 2, 2, 64))
    weight = np.where(kx == 0, 1.0, 2.0)[:, None] / (64 * 64)
    for m in range(2):
        d1[m, :, m, :, 0], d1[m, :, m, :, 1], d1[m, :, m, :, 2] = np.cos(tx), -np.sin(tx), -np.cos(tx)
        ex[m, :, 0, m], ex[m, :, 1, m] = weight * np.cos(tx.T), -weight * np.sin(tx.T)
    out["d1"] = d1.reshape(128, 2, KX, 3)
    out["ex"] = rows(np.concatenate([ex.reshape(2 * TRIG, 128), np.ones((1, 128))]))
    out["cy"] = rows(np.stack([np.cos(ty), np.sin(ty)], axis=1))
    out["dyi"] = rows(np.concatenate([np.cos(ty.T), -np.sin(ty.T)]))
    out["sgn"] = np.tile(np.repeat([1.0, -1.0], C), 2)[:, None]
    out["ident"] = np.eye(128)
    out["ones"] = np.ones((1, 512))
    return {k: np.ascontiguousarray(v, dtype=v.dtype if v.dtype.kind == "i" else np.float32) for k, v in out.items()}


def kernel(**inputs):
    import concourse.bacc as bacc
    from concourse.bass_utils import run_bass_kernel_spmd

    nc = bacc.Bacc("TRN2", target_bir_lowering=False, num_devices=1)
    arrays = {f"in_{k}": v for k, v in layouts(inputs).items()}
    t = {k[3:]: nc.dram_tensor(k, v.shape, mybir.dt.from_np(v.dtype), kind="ExternalInput").ap()
         for k, v in arrays.items()}
    out = nc.dram_tensor("out", [IMGS, TOK, 64], F32, kind="ExternalOutput").ap()
    tokens = nc.dram_tensor("tokens", [IMGS, TOK, 64], F32).ap()
    token_network(nc, t, tokens)
    text_embedding(nc, t, tokens)
    attention_and_experts(nc, t, tokens, out)
    r = run_bass_kernel_spmd(nc, [arrays], core_ids=[0])
    return r.results[0]["out"]
```

```python
import numpy as np
import concourse.bass as bass
from concourse import mybir
from contextlib import ExitStack

F32 = mybir.dt.float32
I32 = mybir.dt.int32
ALU = mybir.AluOpType
ACT = mybir.ActivationFunctionType
AX = mybir.AxisListType

IMGS, Y, X, C = 64, 64, 64, 32
PAIRS = IMGS // 2
KX, KYH = 12, 12
KY = 2 * KYH
MODES = KYH * KX
LAYERS = 4
CHUNKS = 4
YC = Y // CHUNKS
YQ = 4
STEM = 0
COUPLES = PAIRS // 2
TRIG = 2 * KX
EPS = 1e-5
TXT, VOCAB = 77, 8000
TOK = Y + TXT
WCH = MODES // COUPLES
ROWBUFS = 4
PART1 = 64


def at_least(eng, sem, value):
    if isinstance(value, int) and value <= 0:
        return
    eng.wait_ge(sem, value)


def waits_apart(eng, passed):
    eng.sem_inc(passed, 1)


def each_step(eng, step, drain, per=CHUNKS):
    def couple(i, pairs=2):
        for p in range(pairs):
            for j in range(per):
                step(i, p, j)
    couple(0)
    couple(1)
    with eng.Fori(2, COUPLES - 1) as i:
        couple(i)
    couple(COUPLES - 1)
    couple(COUPLES, drain)


def behind(i, p, j, lag, per=CHUNKS):
    n, j = divmod(per * p + j - lag, per)
    i, p = i + n // 2, n % 2
    if isinstance(i, int) and not 0 <= i < COUPLES:
        return None
    return i, p, j


def token_network(nc, t, tokens):
    with ExitStack() as ctx:
        def sb(name, shape, dt=F32):
            return ctx.enter_context(nc.sbuf_tensor(name, shape, dt))

        def sem(name):
            return ctx.enter_context(nc.semaphore(name))

        h_dram = nc.dram_tensor("h_scratch", [PAIRS, 128, 16 * 128], F32).ap()
        g_dram = nc.dram_tensor("g_scratch", [IMGS, KY, KX * 2 * C], F32).ap()
        cb_dram = nc.dram_tensor("cb_scratch", [LAYERS, Y * C], F32).ap()

        wsb = sb("wsb", [128, MODES, 2, C])
        xsb = sb("xsb", [128, MODES, IMGS])
        hc = [sb(f"hc{p}", [128, 16, 128]) for p in range(2)]
        hp = [sb(f"hp{p}", [128, C, Y]) for p in range(2)]
        zb = [sb(f"zb{p}", [128, Y, C]) for p in range(2)]
        gt = [sb(f"gt{p}", [128, 2, KX, 2, C]) for p in range(2)]
        asb = sb("asb", [128, 2 * KX, 2, C])
        sq = [sb(f"sq{p}", [128, YC, C + 1]) for p in range(2)]
        zt = [sb(f"zt{p}", [128, YC, C]) for p in range(2)]
        var = [sb(f"var{p}", [128, YC]) for p in range(2)]
        rstd = [sb(f"rstd{p}", [128, YC]) for p in range(2)]
        mhalf = sb("mhalf", [128, YC])
        wmean = sb("wmean", [128, 2 * WCH])
        gs = [sb(f"gs{n}", [2 * IMGS, KX // 2, 2, C]) for n in range(ROWBUFS)]
        xin = [sb(f"xin{p}", [128, CHUNKS, 128]) for p in range(2)]
        a1 = [sb(f"a1{p}", [128, 512]) for p in range(2)]
        a2 = [sb(f"a2{p}", [128, 512]) for p in range(2)]
        hst = [sb(f"hst{p}", [34, 16, 128]) for p in range(2)]

        ident = sb("ident", [128, 128])
        d1 = sb("d1", [128, 2, KX, 3])
        cy = sb("cy", [128, KY])
        gbx = sb("gbx", [128, LAYERS, 2, C])
        dyi = sb("dyi", [128, Y])
        ex = sb("ex", [128, 128])
        sgn = sb("sgn", [128, 1])
        cw = sb("cw", [128, LAYERS, 4, C])
        cwm = sb("cwm", [128, LAYERS * 4])
        cbt = hp[0][0:LAYERS].rearrange("l c y -> l (c y)").rearrange("l (y c) -> l y c", c=C)
        cbm = hp[1][0:LAYERS, 0, :]
        f0 = sb("f0", [128, YC, C])
        f0m = sb("f0m", [128, YC])
        lnp = sb("lnp", [128, 2])
        fc1 = sb("fc1", [128, 4, 128])
        fc1b = sb("fc1b", [128, 1])
        fc2 = sb("fc2", [128, 64])
        fc2b = sb("fc2b", [128, 1])
        fc3 = sb("fc3", [128, 2])
        fc3b = sb("fc3b", [128, 1])

        ps = ctx.enter_context(nc.psum_tensor("ps", [128, 8, 512], F32))
        main_ps = [ps[:, b, :] for b in (0, 1)]
        t_ps, x_ps = ps[:, 2, :], ps[:, 5, 0:MODES * 2]
        z_ps = [ps[64 * h:64 * h + 2 * TRIG, 4, :] for h in range(2)]
        a_ps = [ps[:, 6 + b, 0:4 * 2 * KX * 3] for b in range(2)]
        f1_ps = [ps[:, 6, :], ps[:, 7, :]]
        f2_ps = [ps[:, 3, :], ps[:, 5, :]]
        f3_ps = [ps[64 + 32 * b:66 + 32 * b, 4, :] for b in range(2)]

        const_in = sem("const_in")
        small_step = sem("small_step")
        passed = sem("passed")
        zeroed = sem("zeroed")
        consts_ready = sem("consts_ready")
        cb_out = sem("cb_out")
        zbias_in = sem("zbias_in")
        xin_in = [sem(f"xin_in{p}") for p in range(2)]
        w_in = sem("w_in")
        w_mean = sem("w_mean")
        w_sub = sem("w_sub")
        w_cent = sem("w_cent")
        main_ready = sem("main_ready")
        sq_ready = sem("sq_ready")
        var_ready = sem("var_ready")
        rstd_ready = sem("rstd_ready")
        norm_ready = sem("norm_ready")
        gain_ready = sem("gain_ready")
        zt_ready = sem("zt_ready")
        hp_ready = sem("hp_ready")
        t_ready = sem("t_ready")
        hc_ready = sem("hc_ready")
        a_psr = sem("a_psr")
        a_ready = [sem(f"a_ready{b}") for b in range(2)]
        x_psr = sem("x_psr")
        x_ready = sem("x_ready")
        z_psr = sem("z_psr")
        zb_ready = [sem(f"zb_ready{h}") for h in range(2)]
        h_out = [sem(f"h_out{j}") for j in range(CHUNKS)]
        h_in = [[sem(f"h_in{p}{j}") for j in range(CHUNKS)] for p in range(2)]
        gt_in = [sem(f"gt_in{p}") for p in range(2)]
        mix_ready = sem("mix_ready")
        gs_ready = sem("gs_ready")
        g_out = [sem(f"g_out{n}") for n in range(ROWBUFS)]
        gt_ready = sem("gt_ready")
        f1_psr = sem("f1_psr")
        a1_ready = sem("a1_ready")
        f2_psr = sem("f2_psr")
        a2_ready = sem("a2_ready")
        f3_psr = sem("f3_psr")
        hst_ready = sem("hst_ready")
        tok_out = [sem(f"tok_out{p}") for p in range(2)]

        block = ctx.enter_context(nc.Block())
        loads = [(ident, t["ident"]), (d1, t["d1"]), (cy, t["cy"]), (dyi, t["dyi"]), (ex, t["ex"]),
                 (sgn, t["sgn"]), (cw, t["conv_w"]), (cbt, t["conv_b"]), (f0, t["fc0"]), (lnp, t["lnp"]), (gbx, t["gbx"]),
                 (fc1, t["fc1_w"]), (fc1b, t["fc1_b"]), (fc2, t["fc2_w"]), (fc2b, t["fc2_b"]),
                 (fc3, t["fc3_w"]), (fc3b, t["fc3_b"])]
        CONSTS = 8
        NCONST = 16 * (len(loads) + 2)

        def rank(s, i, p):
            return s * PAIRS + 2 * i + p

        def stored(eng, s, r):
            if r >= ROWBUFS:
                eng.wait_ge(g_out[r % ROWBUFS], 32 * (KY // ROWBUFS * (s - 1) + r // ROWBUFS))

        def copy_parts(copy, eng, s, i, p, j):
            eng.wait_ge(a_psr, 4 * rank(s, i, p) + j + 1)
            for a in range(2):
                for h in range(2):
                    last = copy(asb[64 * a:64 * a + 64, :, :, 8 * j + h:8 * j + 8:2].rearrange("p x s g -> p g x s"),
                                a_ps[j % 2][64 * h:64 * h + 64].rearrange("p (g x s) -> p g x s", g=4, s=3)[:, :, :, a:a + 2])
            last.then_inc(a_ready[j % 2], 1)

        def z_halves(s):
            return range(1) if isinstance(s, int) and s == LAYERS else range(2)

        def z_half(p, j, h):
            return zb[p][0:2 * TRIG, :, 8 * j + h:8 * j + 8:2].rearrange("k y c -> k c y")

        @block.sync
        def _(sp):
            for dst, src in loads:
                sp.dma_start(dst[:], src[:]).then_inc(const_in, 16)
            sp.wait_ge(zeroed, 6)
            for p in range(2):
                sp.dma_start(xin[p][48:49], t["ones"][:, 0:512].rearrange("a (j n) -> a j n", j=CHUNKS)).then_inc(const_in, 16)
            for p in range(2):
                sp.dma_start(xin[p][0:48], t["x"][p]).then_inc(xin_in[p], 16)
            sp.wait_ge(consts_ready, 1)
            sp.dma_start(cb_dram.rearrange("l (y c) -> l y c", c=C), cbt[:]).then_inc(cb_out, 16)
            sp.wait_ge(cb_out, 16)

            def load_w(s, i):
                if not (isinstance(i, int) and i == 0 and isinstance(s, int) and s == 0):
                    sp.wait_ge(w_cent, s * COUPLES + i)
                    waits_apart(sp, passed)
                sp.dma_start(wsb[:, bass.ds(i * WCH, WCH)], t["w"][bass.ds(s, 1), :, bass.ds(i * WCH, WCH)]
                             .rearrange("a p m s c -> (a p) m s c")).then_inc(w_in, 16)

            def h_chunk(i, p, j):
                return h_dram[bass.ds(2 * i + p, 1), :, 512 * j:512 * j + 512].rearrange("a p n -> (a p) n")

            def hc_chunk(p, j):
                return hc[p][:, 4 * j:4 * j + 4, :].rearrange("p a n -> p (a n)")

            def store_h(s, i, p, j):
                sp.wait_ge(hc_ready, 4 * rank(s, i, p) + j + 1)
                waits_apart(sp, passed)
                sp.dma_start(h_chunk(i, p, j), hc_chunk(p, j)).then_inc(h_out[j], 16)

            def load_h(i, p, j):
                sp.dma_start(hc_chunk(p, j), h_chunk(i, p, j)).then_inc(h_in[p][j], 16)

            def load_gt(i, p):
                sp.dma_start(gt[p][0:KY].rearrange("k m x s c -> k m (x s c)"),
                             g_dram[bass.ds(4 * i + 2 * p, 2)].rearrange("m k n -> k m n")).then_inc(gt_in[p], 16)

            def stem_step(i, p, j):
                if behind(i, p, j, 0):
                    if p == 0 and j == 0:
                        load_w(0, i)
                if c := behind(i, p, j, 2):
                    store_h(0, *c)
                    if c[2] == 3 and (nxt := behind(*c, -2 * CHUNKS)):
                        sp.wait_ge(main_ready, 4 * rank(0, c[0], c[1]) + 4)
                        waits_apart(sp, passed)
                        sp.dma_start(xin[c[1]][0:48], t["x"][bass.ds(2 * nxt[0] + nxt[1], 1)]
                                     .rearrange("a k j n -> (a k) j n")).then_inc(xin_in[c[1]], 16)
            each_step(sp, stem_step, 1)

            def between(s):
                for j in range(CHUNKS):
                    sp.wait_ge(h_out[j], 16 * PAIRS * s)
                waits_apart(sp, passed)
                for p in range(2):
                    for j in range(CHUNKS):
                        load_h(0, p, j)
                    sp.dma_start(zb[p][2 * TRIG:2 * TRIG + 1].rearrange("a y c -> a (y c)"),
                                 cb_dram[bass.ds(s - 1, 1)]).then_inc(zbias_in, 16)
                for r in range(KY):
                    row = (s - 1) * KY + r
                    sp.wait_ge(gs_ready, row + 1)
                    waits_apart(sp, passed)
                    for b in range(2):
                        sp.dma_start(g_dram[:, r, KX * C * b:KX * C * (b + 1)],
                                     gs[r % ROWBUFS][64 * b:64 * b + IMGS].rearrange("i x s c -> i (x s c)")
                                     ).then_inc(g_out[r % ROWBUFS], 16)
                for n in range(ROWBUFS):
                    sp.wait_ge(g_out[n], 32 * (KY // ROWBUFS) * s)
                    waits_apart(sp, passed)
                for p in range(2):
                    load_gt(0, p)

            def layer_pass(s, final):
                between(s)

                def step(i, p, j):
                    if behind(i, p, j, 0) and j == 0:
                        if p == 0 and not final:
                            load_w(s, i)
                        if nxt := behind(i, p, 0, -2 * CHUNKS):
                            sp.wait_ge(z_psr, 4 * (rank(s, i, p) - PAIRS) + 4)
                            waits_apart(sp, passed)
                            load_gt(*nxt[0:2])
                    if not final and (c := behind(i, p, j, 2)):
                        store_h(s, *c)
                    if c := behind(i, p, j, 3):
                        if nxt := behind(*c, -2 * CHUNKS):
                            if final:
                                sp.wait_ge(hst_ready, 4 * (2 * c[0] + c[1]) + c[2] + 1)
                                waits_apart(sp, passed)
                            else:
                                sp.wait_ge(h_out[c[2]], 16 * (PAIRS * s + 2 * c[0] + c[1] + 1))
                                waits_apart(sp, passed)
                            load_h(*nxt)
                        if final and c[2] == 3:
                            n = 2 * c[0] + c[1]
                            sp.wait_ge(hst_ready, 4 * n + 4)
                            waits_apart(sp, passed)
                            for m in range(2):
                                for b in range(2):
                                    sp.dma_start(tokens[bass.ds(2 * n + m, 1), 32 * b:32 * b + 32, :]
                                                 .rearrange("a (q r) x -> (a q) r x", q=2),
                                                 hst[c[1]][32 * b:32 * b + 2, :, 64 * m:64 * m + 64]
                                                 ).then_inc(tok_out[c[1]], 16)
                each_step(sp, step, 1)

            with sp.Fori(1, LAYERS) as s:
                layer_pass(s, False)
            layer_pass(LAYERS, True)
            for p in range(2):
                sp.wait_ge(tok_out[p], 64 * COUPLES)

        @block.tensor
        def _(pe):
            pe.wait_ge(const_in, NCONST)
            pe.wait_ge(consts_ready, CONSTS)

            def main(s, i, p, j):
                g = rank(s, i, p)
                q = 4 * g + j
                m = main_ps[j % 2]
                at_least(pe, norm_ready, q - 1)
                if s is STEM:
                    if j == 0:
                        pe.wait_ge(xin_in[p], 16 * (i + 1))
                    nc.tensor.matmul(m, xin[p][:, j, :], f0[:].rearrange("k y c -> k (y c)"),
                                     start=True, stop=True).then_inc(main_ready, 1)
                    return
                pe.wait_ge(h_in[p][j], 16 * (COUPLES * (s - 1) + i + 1))
                if j == 0:
                    for h in z_halves(s):
                        pe.wait_ge(zb_ready[h], 4 * (g - PAIRS) + 4)
                    if isinstance(i, int) and i == 0 and p == 0:
                        pe.wait_ge(zbias_in, 32 * s)
                nc.tensor.matmul(m, ex[:], zb[p][:].rearrange("k (q r) c -> k r q c", q=YQ)[:, 4 * j:4 * j + 4],
                                 start=True, stop=False, skip_group_check=True)
                for k in range(4):
                    last = nc.tensor.matmul(m[:, 128 * k:128 * k + 128], hc[p][:, 4 * j + k, :],
                                            cw[:, bass.ds(s - 1, 1)].rearrange("p a y c -> p (a y c)"),
                                            start=False, stop=True, skip_group_check=True)
                last.then_inc(main_ready, 1)

            def i1(s, i, p, j):
                idx = 4 * (rank(s, i, p) - PAIRS) + j
                if j == 0:
                    pe.wait_ge(gt_ready, rank(s, i, p) - PAIRS + 1)
                if not (isinstance(i, int) and i == 0 and p == 0 and j == 0):
                    for h in z_halves(s):
                        pe.wait_ge(zb_ready[h], idx)
                for k in range(8):
                    w = len(z_halves(s))
                    h, n = k % w, k // w
                    last = nc.tensor.matmul(z_ps[h][:, 64 * n:64 * n + 64],
                                            gt[p][:, :, :, :, 8 * j + k].rearrange("k m x s -> k (m x s)"),
                                            dyi[:], start=True, stop=True)
                last.then_inc(z_psr, 1)

            def turn(s, i, p, j, final=False):
                q = 4 * rank(s, i, p) + j
                at_least(pe, hc_ready, q)
                if final:
                    pe.wait_ge(norm_ready, q + 1)
                else:
                    pe.wait_ge(hp_ready, q + 1)
                for k in range(4):
                    if final:
                        src = zt[j % 2][:, 4 * k:4 * k + 4, :].rearrange("p y c -> p (y c)")
                    else:
                        src = hp[p][:].rearrange("p c (q r) -> p (c q) r", q=YQ)[:, :, 4 * j + k]
                    last = nc.tensor.transpose(t_ps[:, 128 * k:128 * k + 128], src, ident[:])
                last.then_inc(t_ready, 1)

            def f1(s, i, p, j):
                g = rank(s, i, p)
                if j == 0:
                    pe.wait_ge(hp_ready, 4 * g + 4)
                at_least(pe, a_ready[j % 2], 2 * g + j // 2)
                for k in range(8):
                    h, n = k % 2, k // 2
                    last = nc.tensor.matmul(a_ps[j % 2][64 * h:64 * h + 64, 72 * n:72 * n + 72], hp[p][:, 8 * j + k, :],
                                            d1[:].rearrange("p m x s -> p (m x s)"), start=True, stop=True)
                last.then_inc(a_psr, 1)

            def f2(s, i, p, half):
                g = rank(s, i, p)
                if half == 0:
                    for b in range(2):
                        pe.wait_ge(a_ready[b], 2 * g + 2)
                    at_least(pe, x_ready, g)
                for k in range(KX // 2 * half, KX // 2 * half + KX // 2):
                    last = nc.tensor.matmul(x_ps[:, KY * k:KY * k + KY],
                                            asb[:, 2 * k:2 * k + 2].rearrange("y x s c -> y (x s c)"),
                                            cy[:], start=True, stop=True)
                if half:
                    last.then_inc(x_psr, 1)

            def run_pass(s):
                def step(i, p, j):
                    if behind(i, p, j, 0):
                        main(s, i, p, j)
                    prev = behind(i, p, j, CHUNKS)
                    if prev and j >= 2:
                        f1(s, prev[0], prev[1], 2 * (j - 2))
                    if c := behind(i, p, j, 2):
                        turn(s, *c)
                    if s is not STEM and (c := behind(i, p, j, -CHUNKS)):
                        i1(s, *c)
                    if prev and j >= 2:
                        f1(s, prev[0], prev[1], 2 * (j - 2) + 1)
                    if j < 2 and (c := behind(i, p, j, 2 * CHUNKS)):
                        f2(s, c[0], c[1], j)
                each_step(pe, step, 2)

            def mix(s):
                pe.wait_ge(x_ready, PAIRS * s)
                pe.wait_ge(w_cent, COUPLES * s)
                waits_apart(pe, passed)
                for r in range(KY):
                    row = (s - 1) * KY + r
                    if r >= ROWBUFS:
                        pe.wait_ge(gs_ready, row - ROWBUFS + 1)
                        waits_apart(pe, passed)
                    for a in range(6):
                        for b in range(2):
                            k = slice(64 * b, 64 * b + 64)
                            last = nc.tensor.matmul(
                                ps[64 * b:64 * b + IMGS, r % ROWBUFS, 64 * a:64 * a + 64],
                                xsb[k, KY * a + r, :], wsb[k, KY * a + r].rearrange("k s c -> k (s c)"),
                                start=True, stop=True, tile_position=(64 * b, 64 * b))
                    last.then_inc(mix_ready, 1)
                pe.wait_ge(gs_ready, KY * s)

            def head(i, p, j):
                c = 4 * (2 * i + p) + j
                pe.wait_ge(hc_ready, 4 * rank(LAYERS, i, p) + j + 1)

                def fc1_row(y):
                    at_least(pe, a1_ready, 4 * c + y - 1)
                    nc.tensor.matmul(f1_ps[y % 2], fc1[:, y, :],
                                     hc[p][:, 4 * j:4 * j + 4, :].rearrange("c a n -> c (a n)"),
                                     start=True, stop=True).then_inc(f1_psr, 1)

                def fc2_row(y):
                    pe.wait_ge(a1_ready, 4 * c + y + 1)
                    if y % 2 == 0:
                        at_least(pe, a2_ready, 2 * c + y // 2 - 1)
                    nc.tensor.matmul(f2_ps[y // 2][64 * (y % 2):64 * (y % 2) + 64], fc2[:], a1[y % 2][:],
                                     start=True, stop=True).then_inc(f2_psr, 1)

                def fc3_rows(b):
                    pe.wait_ge(a2_ready, 2 * c + b + 1)
                    if b == 0:
                        at_least(pe, hst_ready, c)
                    nc.tensor.matmul(f3_ps[b], fc3[:], a2[b][:], start=True, stop=True).then_inc(f3_psr, 1)

                fc1_row(0)
                fc1_row(1)
                fc2_row(0)
                fc1_row(2)
                fc2_row(1)
                fc1_row(3)
                fc2_row(2)
                fc2_row(3)
                fc3_rows(0)
                fc3_rows(1)

            def final_pass(s):
                def step(i, p, j):
                    if c := behind(i, p, j, 2):
                        turn(s, *c, final=True)
                    if behind(i, p, j, 0):
                        main(s, i, p, j)
                    if c := behind(i, p, j, -CHUNKS):
                        i1(s, *c)
                    if c := behind(i, p, j, 3):
                        head(*c)
                each_step(pe, step, 1)

            run_pass(STEM)
            with pe.Fori(1, LAYERS) as s:
                mix(s)
                for j in range(CHUNKS):
                    i1(s, 0, 0, j)
                run_pass(s)
            mix(LAYERS)
            for j in range(CHUNKS):
                i1(LAYERS, 0, 0, j)
            final_pass(LAYERS)

        @block.scalar
        def _(act):
            act.wait_ge(const_in, NCONST)
            act.wait_ge(consts_ready, CONSTS)

            def square(s, i, p, j):
                q = 4 * rank(s, i, p) + j
                act.wait_ge(main_ready, q + 1)
                at_least(act, var_ready, q - 1)
                nc.scalar.activation(sq[j % 2][:, :, 0:C], main_ps[j % 2].rearrange("p (y c) -> p y c", c=C), ACT.Square
                                     ).then_inc(sq_ready, 1)

            def chunk_of_hc(p, j):
                return hc[p][:, 4 * j:4 * j + 4, :].rearrange("p a n -> p (a n)")

            def activate(s, i, p, j, func):
                g = rank(s, i, p)
                if j == 0:
                    at_least(act, a_psr, 4 * (g - 1))
                act.wait_ge(zt_ready, 4 * g + j + 1)
                nc.scalar.activation(hp[p][:].rearrange("p c (q r) -> p c q r", q=YQ)[:, :, :, 4 * j:4 * j + 4],
                                     zt[j % 2][:].rearrange("p (k q) c -> p c q k", k=4), func).then_inc(hp_ready, 1)

            def hc_copy(s, i, p, j):
                if s is STEM:
                    at_least(act, h_out[j], 16 * (2 * i + p - 1))
                act.wait_ge(t_ready, 4 * rank(s, i, p) + j + 1)
                nc.scalar.copy(chunk_of_hc(p, j), t_ps).then_inc(hc_ready, 1)

            def affine(s, i, p, j):
                act.wait_ge(t_ready, 4 * rank(s, i, p) + j + 1)
                nc.scalar.activation(chunk_of_hc(p, j), t_ps, ACT.Identity, bias=lnp[:, 1:2], scale=lnp[:, 0:1]
                                     ).then_inc(hc_ready, 1)

            def a_copy(s, i, p, j):
                copy_parts(nc.scalar.copy, act, s, i, p, j)

            def z_copy(s, i, p, j):
                idx = 4 * (rank(s, i, p) - PAIRS) + j
                act.wait_ge(z_psr, idx + 1)
                nc.scalar.copy(z_half(p, j, 1), z_ps[1][:, 0:256].rearrange("k (c y) -> k c y", c=4)
                               ).then_inc(zb_ready[1], 1)

            def x_copy(s, i, p):
                act.wait_ge(x_psr, rank(s, i, p) + 1)
                nc.scalar.copy(xsb[:, :, bass.ds(4 * i + 2 * p, 2)].rearrange("p k m -> p m k"),
                               x_ps.rearrange("p (m k) -> p m k", m=2)).then_inc(x_ready, 1)

            def run_pass(s, func):
                def step(i, p, j):
                    if behind(i, p, j, 0):
                        square(s, i, p, j)
                    prev = behind(i, p, j, CHUNKS)
                    if prev and j >= 2:
                        a_copy(s, prev[0], prev[1], 2 * (j - 2))
                    if c := behind(i, p, j, 2):
                        hc_copy(s, *c)
                    if s is not STEM and (c := behind(i, p, j, -CHUNKS)):
                        z_copy(s, *c)
                    if c := behind(i, p, j, 1):
                        activate(s, *c, func)
                    if s is not STEM and j == 3 and (c := behind(i, p, 0, -2 * CHUNKS)):
                        gt_part1(s, c[0], c[1])
                    if j == 1 and (c := behind(i, p, j, 2 * CHUNKS)):
                        x_copy(s, c[0], c[1])
                each_step(act, step, 2)

            def gt_part1(s, i, p):
                act.wait_ge(gt_in[p], 16 * (COUPLES * (s - 1) + i + 1))
                re, im = gt[p][0:KY, :, :, 0, :], gt[p][0:KY, :, :, 1, :]
                nc.scalar.copy(gt[p][PART1:PART1 + KY, :, :, 0, :], im)
                nc.scalar.mul(gt[p][PART1:PART1 + KY, :, :, 1, :], re, -1.0).then_inc(gt_ready, 1)

            def head(i, p, j):
                c = 4 * (2 * i + p) + j

                def gelu1(y):
                    act.wait_ge(f1_psr, 4 * c + y + 1)
                    at_least(act, f2_psr, 4 * c + y - 1)
                    nc.scalar.activation(a1[y % 2][:], f1_ps[y % 2], ACT.Gelu, bias=fc1b[:]).then_inc(a1_ready, 1)

                def gelu2(b):
                    act.wait_ge(f2_psr, 4 * c + 2 * b + 2)
                    at_least(act, f3_psr, 2 * c + b - 1)
                    nc.scalar.activation(a2[b][:], f2_ps[b], ACT.Gelu, bias=fc2b[:]).then_inc(a2_ready, 1)

                gelu1(0)
                gelu1(1)
                gelu1(2)
                gelu2(0)
                gelu1(3)
                gelu2(1)

            def final_pass(s):
                def step(i, p, j):
                    if c := behind(i, p, j, 2):
                        affine(s, *c)
                    if behind(i, p, j, 0):
                        square(s, i, p, j)
                    if j == 3 and (c := behind(i, p, 0, -2 * CHUNKS)):
                        gt_part1(s, c[0], c[1])
                    if c := behind(i, p, j, 3):
                        head(*c)
                each_step(act, step, 1)

            run_pass(STEM, ACT.Identity)
            with act.Fori(1, LAYERS) as s:
                gt_part1(s, 0, 0)
                for j in range(CHUNKS):
                    z_copy(s, 0, 0, j)
                gt_part1(s, 0, 1)
                run_pass(s, ACT.Gelu)
            for p in range(2):
                gt_part1(LAYERS, 0, p)
            final_pass(LAYERS)

        @block.vector
        def _(dve):
            for n, tile in enumerate((xin[0], xin[1], zb[0], zb[1], gt[0], gt[1])):
                nc.vector.memset(tile[:], 0.0).then_inc(zeroed, 1)
            dve.wait_ge(const_in, NCONST)
            small = [(cbt[:], cbm), (cw[:].rearrange("p l y c -> p (l y) c"), cwm[:]), (f0[:], f0m[:])]
            for n, (tile, mean) in enumerate(small):
                shape = list(tile.shape)
                nc.vector.tensor_reduce(mean, tile, axis=AX.X, op=ALU.add).then_inc(small_step, 1)
                dve.wait_ge(small_step, 2 * n + 1)
                nc.vector.tensor_scalar(mean, mean, 1.0 / C, None, ALU.mult).then_inc(small_step, 1)
                dve.wait_ge(small_step, 2 * n + 2)
                nc.vector.tensor_tensor(tile, tile, mean.unsqueeze(2).to_broadcast(shape), ALU.subtract
                                        ).then_inc(consts_ready, 1)
            nc.vector.memset(mhalf[:], -0.5).then_inc(consts_ready, 1)
            for p in range(2):
                nc.vector.memset(sq[p][:, :, C:C + 1], C * EPS).then_inc(consts_ready, 1)
            for gain in (gbx[:, :, 0, :], lnp[:, 0:1]):
                nc.vector.tensor_scalar(gain, gain, float(np.sqrt(C)), None, ALU.mult).then_inc(consts_ready, 1)
            dve.wait_ge(consts_ready, CONSTS)
            dve.wait_ge(cb_out, 16)

            def reduce(s, i, p, j):
                q = 4 * rank(s, i, p) + j
                dve.wait_ge(sq_ready, q + 1)
                at_least(dve, rstd_ready, q - 1)
                nc.vector.tensor_reduce(var[j % 2][:], sq[j % 2][:], axis=AX.X, op=ALU.add).then_inc(var_ready, 1)

            def normalise(s, i, p, j, final=False):
                q = 4 * rank(s, i, p) + j
                dve.wait_ge(rstd_ready, q + 1)
                if final:
                    dve.wait_ge(t_ready, q - 1)
                else:
                    at_least(dve, hp_ready, q - 1)
                nc.vector.tensor_tensor(zt[j % 2][:], main_ps[j % 2].rearrange("p (y c) -> p y c", c=C),
                                        rstd[j % 2][:].unsqueeze(2).to_broadcast([128, YC, C]), ALU.mult
                                        ).then_inc(norm_ready, 1)

            def affine(s, i, p, j):
                q = 4 * rank(s, i, p) + j
                z = zt[j % 2][:]
                for which, op, before, after in ((0, ALU.mult, norm_ready, gain_ready), (1, ALU.add, gain_ready, zt_ready)):
                    dve.wait_ge(before, q + 1)
                    nc.vector.tensor_tensor(z, z, gbx[:, bass.ds(s, 1), which, :].to_broadcast([128, YC, C]), op
                                            ).then_inc(after, 1)

            def z_copy(s, i, p, j, final=False):
                idx = 4 * (rank(s, i, p) - PAIRS) + j
                dve.wait_ge(z_psr, idx + 1)
                if final:
                    nc.vector.tensor_copy(zb[p][0:2 * TRIG, :, 8 * j:8 * j + 8].rearrange("k y c -> k c y"),
                                          z_ps[0].rearrange("k (c y) -> k c y", c=8)).then_inc(zb_ready[0], 1)
                else:
                    nc.vector.tensor_copy(z_half(p, j, 0), z_ps[0][:, 0:256].rearrange("k (c y) -> k c y", c=4)
                                          ).then_inc(zb_ready[0], 1)

            def w_sum(s, i):
                dve.wait_ge(w_in, 16 * (COUPLES * s + i + 1))
                if not (isinstance(i, int) and i == 0 and s is STEM):
                    dve.wait_ge(w_cent, COUPLES * s + i)
                nc.vector.tensor_reduce(wmean[:], wsb[:, bass.ds(i * WCH, WCH)].rearrange("p m s c -> p (m s) c"),
                                        axis=AX.X, op=ALU.add).then_inc(w_mean, 1)

            def a_copy(s, i, p, j):
                copy_parts(nc.vector.tensor_copy, dve, s, i, p, j)

            def run_pass(s, final=False):
                def step(i, p, j):
                    if behind(i, p, j, 0):
                        reduce(s, i, p, j)
                    c = behind(i, p, j, 1)
                    if c:
                        normalise(s, *c, final)
                    if c and not final:
                        affine(s, *c)
                    prev = None if final else behind(i, p, j, CHUNKS)
                    if prev and j >= 2:
                        a_copy(s, prev[0], prev[1], 2 * (j - 2) + 1)
                    if s is not STEM and (c := behind(i, p, j, -CHUNKS)):
                        z_copy(s, *c, final)
                    if final and (c := behind(i, p, j, 3)):
                        out_copy(*c)
                    if not final and p == 0 and j == 1 and behind(i, p, j, 0):
                        w_sum(s, i)
                each_step(dve, step, 2)

            def out_copy(i, p, j):
                c = 4 * (2 * i + p) + j
                dve.wait_ge(f3_psr, 2 * c + 2)
                if j == 0 and not (isinstance(i, int) and i == 0):
                    dve.wait_ge(tok_out[p], 64 * i)
                for b in range(2):
                    last = nc.vector.tensor_scalar(hst[p][32 * b:32 * b + 2, 4 * j:4 * j + 4, :].rearrange("k a n -> k (a n)"),
                                                   f3_ps[b], fc3b[64 + 32 * b:66 + 32 * b], None, ALU.add)
                last.then_inc(hst_ready, 1)

            def mix(s):
                for r in range(KY):
                    stored(dve, s, r)
                    dve.wait_ge(mix_ready, (s - 1) * KY + r + 1)
                    nc.vector.tensor_copy(gs[r % ROWBUFS][:].rearrange("i a s c -> i (a s c)"), ps[:, r % ROWBUFS, 0:KX * C]
                                          ).then_inc(gs_ready, 1)

            run_pass(STEM)
            with dve.Fori(1, LAYERS) as s:
                mix(s)
                for j in range(CHUNKS):
                    z_copy(s, 0, 0, j)
                run_pass(s)
            mix(LAYERS)
            for j in range(CHUNKS):
                z_copy(LAYERS, 0, 0, j, final=True)
            run_pass(LAYERS, final=True)

        @block.gpsimd
        def _(pool):
            pool.wait_ge(const_in, NCONST)
            pool.wait_ge(consts_ready, CONSTS)

            def rstds(s, i, p, j):
                q = 4 * rank(s, i, p) + j
                pool.wait_ge(var_ready, q + 1)
                nc.gpsimd.tensor_tensor(rstd[j % 2][:], var[j % 2][:], mhalf[:], ALU.pow).then_inc(rstd_ready, 1)

            def w_centre(s, i):
                k = COUPLES * s + i
                chunk = wsb[:, bass.ds(i * WCH, WCH)]
                pool.wait_ge(w_mean, k + 1)
                waits_apart(pool, passed)
                nc.gpsimd.tensor_scalar(wmean[:], wmean[:], 1.0 / C, None, ALU.mult).then_inc(w_sub, 1)
                pool.wait_ge(w_sub, 2 * k + 1)
                flat = chunk.rearrange("p m s c -> p (m s) c")
                nc.gpsimd.tensor_tensor(flat, flat, wmean[:].unsqueeze(2).to_broadcast([128, 2 * WCH, C]),
                                        ALU.subtract).then_inc(w_sub, 1)
                pool.wait_ge(w_sub, 2 * k + 2)
                waits_apart(pool, passed)
                nc.gpsimd.tensor_tensor(chunk[:, :, 0, :], chunk[:, :, 0, :], sgn[:].unsqueeze(2).to_broadcast([128, WCH, C]),
                                        ALU.mult).then_inc(w_cent, 1)

            def run_pass(s, final=False):
                def step(i, p, j):
                    if behind(i, p, j, 0):
                        rstds(s, i, p, j)
                        if p == 0 and j == 1 and not final:
                            w_centre(s, i)
                each_step(pool, step, 0)

            run_pass(STEM)
            with pool.Fori(1, LAYERS) as s:
                run_pass(s)
            run_pass(LAYERS, final=True)



TH = (TXT + 1) // 2


def text_embedding(nc, t, tokens):
    with ExitStack() as ctx:
        def sb(name, shape, dt=F32):
            return ctx.enter_context(nc.sbuf_tensor(name, shape, dt))

        def sem(name):
            return ctx.enter_context(nc.semaphore(name))

        PAD = 64
        state = sb("state", [128, TXT], I32)
        pos = sb("pos", [128, TXT])
        add = [sb(f"add{b}", [128, PAD + TXT]) for b in range(2)]
        top = [sb(f"top{b}", [128, PAD + TXT]) for b in range(2)]
        args = sb("args", [128, TXT])
        idx = sb("idx", [128, 3, TH], I32)
        emb = sb("emb", [128, 3, TH, 64])
        mean = sb("mean", [128, TH])
        sq = sb("esq", [128, TH, 64])
        mhalf = sb("emh", [128, TH])
        gb = sb("gb", [128, 2, 64])
        landed = sem("txt_landed")
        scan = sem("txt_scan")
        idx_ready = sem("idx_ready")
        gathered = sem("gathered")
        var_sum = sem("txt_var")
        rstd_done = sem("txt_rstd")
        txt_ready = sem("txt_ready")
        txt_out = sem("txt_out")
        block = ctx.enter_context(nc.Block())

        @block.sync
        def _(sp):
            sp.dma_start(state[:], t["state"]).then_inc(landed, 16)
            sp.dma_start(pos[:], t["pos"]).then_inc(landed, 16)
            sp.dma_start(gb[:], t["txt_gb"]).then_inc(landed, 16)
            sp.wait_ge(txt_ready, 1)
            sp.dma_start(tokens[:, Y:Y + TH, :], emb[0:64, 0]).then_inc(txt_out, 16)
            sp.dma_start(tokens[:, Y + TH:TOK, :], emb[64:128, 0, 0:TXT - TH]).then_inc(txt_out, 16)
            sp.wait_ge(txt_out, 32)

        @block.gpsimd
        def _(pool):
            pool.wait_ge(idx_ready, 1)
            for k, name in enumerate(("token_emb", "instr_emb", "arg_emb")):
                for c in range(TH):
                    nc.gpsimd.indirect_dma_start(
                        out=emb[:, k, c, :], out_offset=None, in_=t[name],
                        in_offset=bass.IndirectOffsetOnAxis(ap=idx[:, k, c:c + 1], axis=0)).then_inc(gathered, 16)
            pool.wait_ge(var_sum, 2)
            nc.gpsimd.tensor_tensor(mean[:], mean[:], mhalf[:], ALU.pow).then_inc(rstd_done, 1)

        @block.vector
        def _(dve):
            n = 0

            def link(ins):
                nonlocal n
                n += 1
                ins.then_inc(scan, 1)
                dve.wait_ge(scan, n)

            for b in range(2):
                nc.vector.memset(add[b][:], 0.0).then_inc(scan, 1)
                nc.vector.memset(top[b][:], 0.0).then_inc(scan, 1)
            nc.vector.memset(idx[:], 0).then_inc(scan, 1)
            nc.vector.memset(mhalf[:], -0.5).then_inc(scan, 1)
            n = 6
            dve.wait_ge(scan, n)
            dve.wait_ge(landed, 48)
            link(nc.vector.tensor_scalar(add[0][:, PAD + 1:], state[:, 0:TXT - 1], 5.0, None, ALU.is_equal))
            link(nc.vector.tensor_tensor(top[0][:, PAD:], add[0][:, PAD:], pos[:], ALU.mult))
            b = 0
            for s in (1, 2, 4, 8, 16, 32, 64):
                nc.vector.tensor_tensor(add[1 - b][:, PAD:], add[b][:, PAD:], add[b][:, PAD - s:PAD - s + TXT],
                                        ALU.add).then_inc(scan, 1)
                nc.vector.tensor_tensor(top[1 - b][:, PAD:], top[b][:, PAD:], top[b][:, PAD - s:PAD - s + TXT],
                                        ALU.max).then_inc(scan, 1)
                n += 2
                dve.wait_ge(scan, n)
                b = 1 - b
            link(nc.vector.tensor_tensor(args[:], pos[:], top[b][:, PAD:], ALU.subtract))
            for half in range(2):
                k, r, w = TH * half, slice(64 * half, 64 * half + 64), TH if half == 0 else TXT - TH
                for m, src in enumerate((state[r, k:k + w], add[b][r, PAD + k:PAD + k + w], args[r, k:k + w])):
                    link(nc.vector.tensor_copy(idx[r, m, 0:w], src))
            nc.vector.tensor_copy(mean[:, 0:1], args[:, 0:1]).then_inc(idx_ready, 1)
            dve.wait_ge(gathered, 16 * 3 * TH)
            e = emb[:, 0]
            wide = [128, TH, 64]
            link(nc.vector.tensor_tensor(e, e, emb[:, 1], ALU.add))
            link(nc.vector.tensor_tensor(e, e, emb[:, 2], ALU.add))
            link(nc.vector.tensor_reduce(mean[:], e, axis=AX.X, op=ALU.add))
            link(nc.vector.tensor_scalar(mean[:], mean[:], 1.0 / 64, None, ALU.mult))
            link(nc.vector.tensor_tensor(e, e, mean[:].unsqueeze(2).to_broadcast(wide), ALU.subtract))
            link(nc.vector.tensor_tensor(sq[:], e, e, ALU.mult))
            nc.vector.tensor_reduce(mean[:], sq[:], axis=AX.X, op=ALU.add).then_inc(var_sum, 1)
            dve.wait_ge(var_sum, 1)
            nc.vector.tensor_scalar(mean[:], mean[:], 1.0 / 64, EPS, ALU.mult, ALU.add).then_inc(var_sum, 1)
            dve.wait_ge(rstd_done, 1)
            link(nc.vector.tensor_tensor(e, e, mean[:].unsqueeze(2).to_broadcast(wide), ALU.mult))
            link(nc.vector.tensor_tensor(e, e, gb[:, 0:1, :].to_broadcast(wide), ALU.mult))
            nc.vector.tensor_tensor(e, e, gb[:, 1:2, :].to_broadcast(wide), ALU.add).then_inc(txt_ready, 1)


BLK = TOK // 3
KEYS = 119
KEY0 = [0, 11, 22]
HEADS, HD = 8, 8
HID, EXPERTS = 128, 16
QPAD = 160
assert 3 * BLK == TOK and KEY0[2] + KEYS == TOK


def attention_and_experts(nc, t, tokens, out):
    with ExitStack() as ctx:
        def sb(name, shape, dt=F32):
            return ctx.enter_context(nc.sbuf_tensor(name, shape, dt))

        def sem(name):
            return ctx.enter_context(nc.semaphore(name))

        xs = [sb(f"xs{p}", [128, 3, 64]) for p in range(2)]
        xr = [sb(f"xr{p}", [128, 3, 64]) for p in range(2)]
        xn = sb("xn", [128, 3, 64])
        xsq = sb("xsq", [128, 3, 64])
        st1 = sb("st1", [128, 3])
        mu1 = sb("mu1", [128, 3])
        va1 = sb("va1", [128, 3])
        rs1 = sb("rs1", [128, 3])
        xT = sb("xT", [128, 2, QPAD])
        qT = [sb(f"qT{p}", [128, 2, QPAD]) for p in range(2)]
        kT = sb("kT", [64, 2, TOK])
        km = [sb(f"km{p}", [128, 2, HEADS, TOK]) for p in range(2)]
        vv = [sb(f"vv{p}", [KEYS, 2, 3, 64]) for p in range(2)]
        sm = [sb(f"sm{b}", [128, HEADS, KEYS]) for b in range(2)]
        mx = [sb(f"mx{b}", [128, HEADS]) for b in range(2)]
        den = [sb(f"den{p}", [128, 3, HEADS]) for p in range(2)]
        rden = sb("rden", [128, 3, HEADS])
        pT = sb("pT", [KEYS, HEADS, 128])
        osb = sb("osb", [128, 3, 64])
        oT = sb("oT", [128, 3, 128])
        h1 = [sb(f"h1{p}", [128, 3, 64]) for p in range(2)]
        h1b = [sb(f"h1b{p}", [128, 3, 64]) for p in range(2)]
        yn = sb("yn", [128, 3, 64])
        ysq = sb("ysq", [128, 3, 64])
        st2 = sb("st2", [128, 3])
        mu2 = sb("mu2", [128, 3])
        va2 = sb("va2", [128, 3])
        rs2 = sb("rs2", [128, 3])
        yT = sb("yT", [128, 3, 128])
        ff = [sb(f"ff{k}", [128, 3, 2, 64]) for k in range(3)]
        wc = [sb(f"wc{p}", [128, 2, 2, HID]) for p in range(2)]
        bc = [sb(f"bc{p}", [128, 2, 2]) for p in range(2)]
        fin = [sb(f"fin{p}", [128, 3, 64]) for p in range(2)]

        ident = sb("identt", [128, 128])
        mask = sb("mask", [128, 3, KEYS])
        hmask = sb("hmask", [64, HEADS])
        temp = sb("temp", [64, 1])
        mh = sb("mh", [128, 3])
        wq = sb("wq", [128, 64])
        wk = sb("wk", [128, 64])
        wv = sb("wv", [128, 64])
        wp = sb("wp", [128, 64])
        wi = sb("wi", [128, HID])
        bi = sb("bi", [128, 1])
        wr = sb("wr", [128, 2, EXPERTS, HID])
        ws = sb("ws", [128, 2, HID])
        br = sb("br", [128, 2, EXPERTS])
        bs = sb("bs", [128, 2])
        wo = sb("wo", [128, 64])
        bo = sb("bo", [128, 64])
        route = sb("route", [1, IMGS], I32)

        ps = ctx.enter_context(nc.psum_tensor("pst", [128, 8, 512], F32))
        s_ps = ps[:, 0:2, 0:4 * KEYS]
        p_ps = ps[0:KEYS, 2:4, :]
        o_ps = ps[:, 4, 0:192]
        fr_ps = [ps[:, 5, :], ps[:, 6, :]]
        ff_ps = ps[:, 7, :]

        t_const = sem("t_const")
        t_zero = sem("t_zero")
        t_passed = sem("t_passed")
        t_setup = sem("t_setup")
        xs_in = [sem(f"xs_in{p}") for p in range(2)]
        xr_in = [sem(f"xr_in{p}") for p in range(2)]
        c1 = sem("c1")
        va1_ready = sem("va1_ready")
        rs1_ready = sem("rs1_ready")
        xn_ready = sem("xn_ready")
        xT_psr = sem("xT_psr")
        xT_ready = sem("xT_ready")
        q_psr = sem("q_psr")
        k_psr = sem("k_psr")
        q_ready = sem("q_ready")
        k_ready = sem("k_ready")
        km_ready = sem("km_ready")
        v_psr = sem("v_psr")
        v_ready = sem("v_ready")
        s_psr = sem("s_psr")
        sm_ready = sem("sm_ready")
        mx_ready = sem("mx_ready")
        sub_ready = sem("sub_ready")
        exp_ready = sem("exp_ready")
        den_ready = sem("den_ready")
        p_psr = sem("p_psr")
        pT_ready = sem("pT_ready")
        o_psr = sem("o_psr")
        rden_ready = sem("rden_ready")
        osb_ready = sem("osb_ready")
        oT_psr = sem("oT_psr")
        oT_ready = sem("oT_ready")
        pr_psr = sem("pr_psr")
        h1_ready = sem("h1_ready")
        h1b_ready = sem("h1b_ready")
        c2 = sem("c2")
        va2_ready = sem("va2_ready")
        rs2_ready = sem("rs2_ready")
        yn_ready = sem("yn_ready")
        yT_psr = sem("yT_psr")
        yT_ready = sem("yT_ready")
        f_psr = sem("f_psr")
        f_ready = sem("f_ready")
        wc_ready = sem("wc_ready")
        y_psr = sem("y_psr")
        fin_ready = sem("fin_ready")
        fin_out = [sem(f"fin_out{p}") for p in range(2)]

        loads = [(ident, "ident"), (mask, "mask"), (hmask, "hmask"), (temp, "temp"), (wq, "wq"), (wk, "wk"),
                 (wv, "wv"), (wp, "wp"), (wi, "wi"), (bi, "bi"), (wr, "wr"), (ws, "ws"), (br, "br"), (bs, "bs"),
                 (wo, "wo"), (bo, "bo"), (route, "route")]
        block = ctx.enter_context(nc.Block())

        def at(i, p, b, lag):
            return behind(i, p, b, lag, 3)

        def num(i, p):
            return 2 * i + p

        @block.sync
        def _(sp):
            for dst, name in loads:
                sp.dma_start(dst[:], t[name]).then_inc(t_const, 16)
            sp.wait_ge(t_zero, 8)
            sp.wait_ge(t_setup, 2)

            def load(dst, i, p, done):
                for m in range(2):
                    sp.dma_start(dst[64 * m:64 * m + BLK], tokens[bass.ds(2 * num(i, p) + m, 1)]
                                 .rearrange("a (b r) d -> (a r) b d", b=3)).then_inc(done, 16)
            for p in range(2):
                load(xs[p], 0, p, xs_in[p])

            def step(i, p, b):
                if b == 0 and at(i, p, 0, 0):
                    if not (isinstance(i, int) and i == 0):
                        sp.wait_ge(h1_ready, num(i, p) - 1)
                        waits_apart(sp, t_passed)
                    load(xr[p], i, p, xr_in[p])
                if b == 0 and at(i, p, 0, 0) and (c := at(i, p, 0, -6)):
                    sp.wait_ge(xn_ready, num(i, p) + 1)
                    waits_apart(sp, t_passed)
                    load(xs[p], c[0], c[1], xs_in[p])
                if b == 2 and (c := at(i, p, 0, 6)):
                    sp.wait_ge(fin_ready, num(c[0], c[1]) + 1)
                    waits_apart(sp, t_passed)
                    for m in range(2):
                        sp.dma_start(out[bass.ds(2 * num(c[0], c[1]) + m, 1)].rearrange("a (b r) d -> (a r) b d", b=3),
                                     fin[c[1]][64 * m:64 * m + BLK]).then_inc(fin_out[c[1]], 16)
            each_step(sp, step, 2, 3)
            for p in range(2):
                sp.wait_ge(fin_out[p], 32 * COUPLES)

        @block.tensor
        def _(pe):
            pe.wait_ge(t_const, 16 * len(loads))
            pe.wait_ge(t_zero, 8)
            pe.wait_ge(t_setup, 6)

            def front1(i, p):
                g = num(i, p)
                pe.wait_ge(xn_ready, g + 1)
                at_least(pe, q_ready, g)
                waits_apart(pe, t_passed)
                for b in range(3):
                    last = nc.tensor.transpose(fr_ps[0][0:64, 128 * b:128 * b + 128], xn[:, b, :], ident[:])
                last.then_inc(xT_psr, 1)

            def front2(i, p):
                g = num(i, p)
                pe.wait_ge(xT_ready, g + 1)
                at_least(pe, v_ready, g)
                nc.tensor.matmul(fr_ps[1][0:64, 0:2 * TOK], wk[:], xT[:, :, 0:TOK], start=True, stop=True).then_inc(k_psr, 1)
                nc.tensor.matmul(fr_ps[0][0:64, 0:2 * TOK], wq[:], xT[:, :, 0:TOK], start=True, stop=True).then_inc(q_psr, 1)

            def front3(i, p):
                pe.wait_ge(k_ready, num(i, p) + 1)
                for m in range(2):
                    for b in range(3):
                        o = 64 * (3 * m + b)
                        last = nc.tensor.matmul(fr_ps[1][0:KEYS, o:o + 64], xT[:, m, KEY0[b]:KEY0[b] + KEYS], wv[:],
                                                start=True, stop=True)
                last.then_inc(v_psr, 1)

            def scores(i, p, b):
                k = 3 * num(i, p) + b
                if b == 0:
                    pe.wait_ge(km_ready, num(i, p) + 1)
                    pe.wait_ge(q_ready, num(i, p) + 1)
                at_least(pe, sm_ready, k)
                for h in range(2):
                    for m in range(2):
                        last = nc.tensor.matmul(s_ps[64 * m:64 * m + 64, h, :], qT[p][:, m, BLK * b:BLK * b + 64],
                                                km[p][:, m, 4 * h:4 * h + 4, KEY0[b]:KEY0[b] + KEYS],
                                                start=True, stop=True)
                last.then_inc(s_psr, 1)

            def turn(i, p, b):
                k = 3 * num(i, p) + b
                pe.wait_ge(exp_ready, k + 1)
                at_least(pe, pT_ready, k)
                for h in range(HEADS):
                    last = nc.tensor.transpose(p_ps[:, h // 4, 128 * (h % 4):128 * (h % 4) + 128],
                                               sm[(3 * p + b) % 2][:, h, :], ident[:])
                last.then_inc(p_psr, 1)

            def values(i, p, b):
                k = 3 * num(i, p) + b
                pe.wait_ge(pT_ready, k + 1)
                if b == 0:
                    pe.wait_ge(v_ready, num(i, p) + 1)
                    at_least(pe, osb_ready, num(i, p))
                for h in range(HEADS):
                    for m in range(2):
                        last = nc.tensor.matmul(o_ps[64 * m:64 * m + 64, 64 * b + HD * h:64 * b + HD * h + HD],
                                                pT[:, h, 64 * m:64 * m + 64], vv[p][:, m, b, HD * h:HD * h + HD],
                                                start=True, stop=True)
                last.then_inc(o_psr, 1)

            def back_o(i, p):
                g = num(i, p)
                pe.wait_ge(osb_ready, g + 1)
                at_least(pe, fin_ready, g)
                waits_apart(pe, t_passed)
                for b in range(3):
                    last = nc.tensor.transpose(ff_ps[0:64, 128 * b:128 * b + 128], osb[:, b, :], ident[:])
                last.then_inc(oT_psr, 1)

            def back_proj(i, p):
                pe.wait_ge(oT_ready, num(i, p) + 1)
                for b in range(3):
                    last = nc.tensor.matmul(ff_ps[:, 64 * b:64 * b + 64], oT[:, b, :], wp[:], start=True, stop=True)
                last.then_inc(pr_psr, 1)

            def back_y(i, p):
                g = num(i, p)
                pe.wait_ge(yn_ready, g + 1)
                pe.wait_ge(h1_ready, g + 1)
                waits_apart(pe, t_passed)
                for b in range(3):
                    last = nc.tensor.transpose(ff_ps[0:64, 128 * b:128 * b + 128], yn[:, b, :], ident[:])
                last.then_inc(yT_psr, 1)

            def back_in(i, p):
                pe.wait_ge(yT_ready, num(i, p) + 1)
                nc.tensor.matmul(ff_ps[:, 0:384], wi[:], yT[:].rearrange("d b n -> d (b n)"),
                                 start=True, stop=True).then_inc(f_psr, 1)

            def back_layer(i, p, l):
                g = num(i, p)
                pe.wait_ge(f_ready, 3 * g + l + 1)
                if l == 0:
                    pe.wait_ge(wc_ready, g + 1)
                for m in range(2):
                    last = nc.tensor.matmul(ff_ps[:, 192 * m:192 * m + 192], wc[p][:, l, m, :], ff[l][:, :, m, :],
                                            start=True, stop=True)
                last.then_inc(f_psr, 1)

            def back_out(i, p):
                pe.wait_ge(f_ready, 3 * num(i, p) + 3)
                for b in range(3):
                    last = nc.tensor.matmul(ff_ps[:, 64 * b:64 * b + 64], ff[2][:, b].rearrange("k m n -> k (m n)"), wo[:],
                                            start=True, stop=True)
                last.then_inc(y_psr, 1)

            front1(0, 0)
            front2(0, 0)
            front3(0, 0)

            def step(i, p, b):
                here, prev, old = at(i, p, 0, 0), at(i, p, 0, 3), at(i, p, 0, 6)
                nxt = here and at(i, p, 0, -3)
                if here:
                    scores(i, p, b)
                if b == 0 and nxt:
                    front1(*nxt[0:2])
                if b == 0 and old:
                    back_layer(old[0], old[1], 0)
                if b == 1 and prev:
                    back_o(*prev[0:2])
                if b == 2 and prev:
                    back_y(*prev[0:2])
                if c := at(i, p, b, 1):
                    turn(*c)
                if b == 0 and nxt:
                    front2(*nxt[0:2])
                if b == 0 and old:
                    back_layer(old[0], old[1], 1)
                if b == 1 and nxt:
                    front3(*nxt[0:2])
                if b == 1 and prev:
                    back_proj(*prev[0:2])
                if b == 2 and prev:
                    back_in(*prev[0:2])
                if c := at(i, p, b, 1):
                    values(*c)
                if b == 0 and old:
                    back_out(*old[0:2])
            each_step(pe, step, 2, 3)

        @block.scalar
        def _(act):
            act.wait_ge(t_zero, 8)
            act.wait_ge(t_const, 16 * len(loads))

            def xT_copy(i, p):
                g = num(i, p)
                act.wait_ge(xT_psr, g + 1)
                at_least(act, v_psr, g)
                nc.scalar.copy(xT[0:64, :, 0:TOK].rearrange("d m (b r) -> d b m r", b=3),
                               fr_ps[0][0:64, 0:384].rearrange("d (b m r) -> d b m r", b=3, m=2)[:, :, :, 0:BLK]
                               ).then_inc(xT_ready, 1)

            def qk_copy(i, p):
                g = num(i, p)
                act.wait_ge(k_psr, g + 1)
                at_least(act, km_ready, g)
                nc.scalar.copy(kT[:].rearrange("d m n -> d (m n)"), fr_ps[1][0:64, 0:2 * TOK]).then_inc(k_ready, 1)
                act.wait_ge(q_psr, g + 1)
                nc.scalar.copy(qT[p][0:64, :, 0:TOK], fr_ps[0][0:64, 0:2 * TOK].rearrange("d (m n) -> d m n", m=2)
                               ).then_inc(q_ready, 1)

            def v_copy(i, p):
                act.wait_ge(v_psr, num(i, p) + 1)
                nc.scalar.copy(vv[p][:].rearrange("k m b d -> k (m b d)"), fr_ps[1][0:KEYS, 0:384]).then_inc(v_ready, 1)

            def exp(i, p, b):
                act.wait_ge(sub_ready, 3 * num(i, p) + b + 1)
                tile = sm[(3 * p + b) % 2][:].rearrange("p h k -> p (h k)")
                nc.scalar.activation(tile, tile, ACT.Exp).then_inc(exp_ready, 1)

            def pT_copy(i, p, b):
                k = 3 * num(i, p) + b
                act.wait_ge(p_psr, k + 1)
                at_least(act, o_psr, k)
                nc.scalar.copy(pT[:].rearrange("k h n -> k (h n)"), p_ps.rearrange("k a n -> k (a n)")).then_inc(pT_ready, 1)

            def oT_copy(i, p):
                act.wait_ge(oT_psr, num(i, p) + 1)
                nc.scalar.copy(oT[0:64].rearrange("d b n -> d (b n)"), ff_ps[0:64, 0:384]).then_inc(oT_ready, 1)

            def yT_copy(i, p):
                act.wait_ge(yT_psr, num(i, p) + 1)
                nc.scalar.copy(yT[0:64].rearrange("d b n -> d (b n)"), ff_ps[0:64, 0:384]).then_inc(yT_ready, 1)

            def relu_in(i, p):
                act.wait_ge(f_psr, 3 * num(i, p) + 1)
                nc.scalar.activation(ff[0][:].rearrange("k b m n -> k (b m n)"), ff_ps[:, 0:384], ACT.Relu, bias=bi[:]
                                     ).then_inc(f_ready, 1)

            def relu_layer(i, p, l):
                act.wait_ge(f_psr, 3 * num(i, p) + l + 2)
                for m in range(2):
                    last = nc.scalar.activation(ff[l + 1][:, :, m, :], ff_ps[:, 192 * m:192 * m + 192]
                                                .rearrange("k (b n) -> k b n", b=3), ACT.Relu, bias=bc[p][:, m, l:l + 1])
                last.then_inc(f_ready, 1)

            xT_copy(0, 0)
            qk_copy(0, 0)
            v_copy(0, 0)

            def step(i, p, b):
                here, prev, old = at(i, p, 0, 0), at(i, p, 0, 3), at(i, p, 0, 6)
                nxt = here and at(i, p, 0, -3)
                if b == 0 and nxt:
                    xT_copy(*nxt[0:2])
                if b == 0 and old:
                    relu_layer(old[0], old[1], 0)
                if b == 1 and prev:
                    oT_copy(*prev[0:2])
                if b == 2 and prev:
                    yT_copy(*prev[0:2])
                if c := at(i, p, b, 1):
                    pT_copy(*c)
                if b == 0 and nxt:
                    qk_copy(*nxt[0:2])
                if b == 0 and old:
                    relu_layer(old[0], old[1], 1)
                if b == 1 and nxt:
                    v_copy(*nxt[0:2])
                if b == 2 and prev:
                    relu_in(*prev[0:2])
                if here:
                    exp(i, p, b)
            each_step(act, step, 2, 3)

        @block.vector
        def _(dve):
            for tile in (xs[0], xs[1], xT, qT[0], qT[1], km[0], km[1], yT):
                nc.vector.memset(tile[:], 0.0).then_inc(t_zero, 1)
            nc.vector.memset(xr[0][:], 0.0).then_inc(t_setup, 1)
            nc.vector.memset(xr[1][:], 0.0).then_inc(t_setup, 1)
            nc.vector.memset(oT[:], 0.0).then_inc(c1, 1)
            nc.vector.memset(mh[:], -0.5)
            dve.wait_ge(c1, 1)
            nc.vector.memset(oT[64:65], 1.0).then_inc(t_setup, 1)
            dve.wait_ge(t_const, 16 * len(loads))
            nc.vector.tensor_tensor(ws[:], ws[:], ident[:].unsqueeze(1).to_broadcast([128, 2, 128]), ALU.add).then_inc(t_setup, 1)
            nc.vector.tensor_tensor(br[:], br[:], bs[:].unsqueeze(2).to_broadcast([128, 2, EXPERTS]), ALU.add).then_inc(t_setup, 1)
            nc.vector.tensor_scalar(hmask[:], hmask[:], temp[:], None, ALU.mult).then_inc(t_setup, 1)
            dve.wait_ge(t_setup, 6)

            def norm(x, n, sq, st, mu, va, chain, base, va_ready, g, free):
                wide = [128, 3, 64]
                nc.vector.tensor_reduce(st[:], x[:], axis=AX.X, op=ALU.add).then_inc(chain, 1)
                dve.wait_ge(chain, base + 4 * g + 1)
                nc.vector.tensor_scalar(mu[:], st[:], 1.0 / 64, None, ALU.mult).then_inc(chain, 1)
                dve.wait_ge(chain, base + 4 * g + 2)
                free()
                nc.vector.tensor_tensor(n[:], x[:], mu[:].unsqueeze(2).to_broadcast(wide), ALU.subtract).then_inc(chain, 1)
                dve.wait_ge(chain, base + 4 * g + 3)
                nc.vector.tensor_tensor(sq[:], n[:], n[:], ALU.mult).then_inc(chain, 1)
                dve.wait_ge(chain, base + 4 * g + 4)
                nc.vector.tensor_reduce(va[:], sq[:], axis=AX.X, op=ALU.add).then_inc(va_ready, 1)

            def norm_end(n, rs, rs_ready, n_ready, g):
                dve.wait_ge(rs_ready, 2 * g + 2)
                nc.vector.tensor_tensor(n[:], n[:], rs[:].unsqueeze(2).to_broadcast([128, 3, 64]), ALU.mult).then_inc(n_ready, 1)

            def norm1(i, p):
                g = num(i, p)
                dve.wait_ge(xs_in[p], 32 * (i + 1))
                norm(xs[p], xn, xsq, st1, mu1, va1, c1, 1, va1_ready, g,
                     lambda: at_least(dve, xT_psr, g))

            def norm1_end(i, p):
                norm_end(xn, rs1, rs1_ready, xn_ready, num(i, p))

            def masked(i, p, b):
                k = 3 * num(i, p) + b
                dve.wait_ge(s_psr, k + 1)
                at_least(dve, p_psr, k - 1)
                at_least(dve, den_ready, k - 1)
                tile = sm[(3 * p + b) % 2]
                nc.vector.tensor_tensor(tile[:].rearrange("p (a h) k -> p a h k", a=2),
                                        s_ps.rearrange("p a (h k) -> p a h k", h=4),
                                        mask[:, b, :].unsqueeze(1).unsqueeze(1).to_broadcast([128, 2, 4, KEYS]),
                                        ALU.add).then_inc(sm_ready, 1)
                dve.wait_ge(sm_ready, k + 1)
                at_least(dve, sub_ready, k - 1)
                nc.vector.tensor_reduce(mx[(3 * p + b) % 2][:], tile[:], axis=AX.X, op=ALU.max).then_inc(mx_ready, 1)

            def total(i, p, b):
                k = 3 * num(i, p) + b
                dve.wait_ge(exp_ready, k + 1)
                nc.vector.tensor_reduce(den[p][:, b, :], sm[(3 * p + b) % 2][:], axis=AX.X, op=ALU.add).then_inc(den_ready, 1)

            def o_norm(i, p):
                g = num(i, p)
                dve.wait_ge(den_ready, 3 * g + 3)
                nc.vector.reciprocal(rden[:], den[p][:]).then_inc(rden_ready, 1)
                dve.wait_ge(rden_ready, g + 1)
                dve.wait_ge(o_psr, 3 * g + 3)
                at_least(dve, oT_psr, g)
                nc.vector.tensor_tensor(osb[:].rearrange("p b (h d) -> p (b h) d", h=HEADS),
                                        o_ps.rearrange("p (c d) -> p c d", d=HD),
                                        rden[:].rearrange("p b h -> p (b h)").unsqueeze(2).to_broadcast([128, 24, HD]),
                                        ALU.mult).then_inc(osb_ready, 1)

            def residual(i, p):
                g = num(i, p)
                dve.wait_ge(pr_psr, g + 1)
                dve.wait_ge(xr_in[p], 32 * (i + 1))
                at_least(dve, h1b_ready, g - 1)
                nc.vector.tensor_tensor(h1[p][:], ff_ps[:, 0:192].rearrange("p (b d) -> p b d", b=3), xr[p][:], ALU.add
                                        ).then_inc(h1_ready, 1)
                dve.wait_ge(h1_ready, g + 1)
                norm(h1[p], yn, ysq, st2, mu2, va2, c2, 0, va2_ready, g,
                     lambda: at_least(dve, yT_psr, g))

            def weights(i, p):
                g = num(i, p)
                at_least(dve, y_psr, g - 1)
                for m in range(2):
                    e = dve.value_load(route[0:1, bass.ds(4 * i + 2 * p + m, 1)], min_val=0, max_val=EXPERTS - 1)
                    nc.vector.tensor_tensor(wc[p][:, :, m, :], wr[:, :, bass.ds(e, 1), :].rearrange("p l a n -> p l (a n)"), ws[:], ALU.add)
                    last = nc.vector.tensor_copy(bc[p][:, m, :], br[:, :, bass.ds(e, 1)].rearrange("p l a -> p (l a)"))
                last.then_inc(wc_ready, 1)

            def final(i, p):
                g = num(i, p)
                dve.wait_ge(y_psr, g + 1)
                dve.wait_ge(h1b_ready, g + 1)
                at_least(dve, fin_out[p], 32 * i)
                nc.vector.tensor_tensor(fin[p][:], ff_ps[:, 0:192].rearrange("p (b d) -> p b d", b=3), h1b[p][:], ALU.add
                                        ).then_inc(fin_ready, 1)

            for p in range(2):
                norm1(0, p)
                norm1_end(0, p)

            def step(i, p, b):
                here, prev, old = at(i, p, 0, 0), at(i, p, 0, 3), at(i, p, 0, 6)
                nxt2 = here and at(i, p, 0, -6)
                if here:
                    masked(i, p, b)
                if b == 2 and prev:
                    norm_end(yn, rs2, rs2_ready, yn_ready, num(prev[0], prev[1]))
                if b == 2 and nxt2:
                    norm1(*nxt2[0:2])
                if c := at(i, p, b, 1):
                    total(*c)
                if b == 2 and nxt2:
                    norm1_end(*nxt2[0:2])
                if b == 0 and prev:
                    o_norm(*prev[0:2])
                if b == 0 and old:
                    final(*old[0:2])
                if b == 1 and here:
                    weights(i, p)
                if b == 1 and prev:
                    residual(*prev[0:2])
            each_step(dve, step, 2, 3)

        @block.gpsimd
        def _(pool):
            pool.wait_ge(t_setup, 6)

            def power(va, rs, va_ready, rs_ready, i, p):
                g = num(i, p)
                pool.wait_ge(va_ready, g + 1)
                waits_apart(pool, t_passed)
                nc.gpsimd.tensor_scalar(va[:], va[:], 1.0 / 64, EPS, ALU.mult, ALU.add).then_inc(rs_ready, 1)
                pool.wait_ge(rs_ready, 2 * g + 1)
                nc.gpsimd.tensor_tensor(rs[:], va[:], mh[:], ALU.pow).then_inc(rs_ready, 1)

            def keys(i, p):
                g = num(i, p)
                pool.wait_ge(k_ready, g + 1)
                at_least(pool, s_psr, 3 * (g - 1))
                for m in range(2):
                    last = nc.gpsimd.tensor_tensor(km[p][0:64, m], kT[:, m:m + 1, :].to_broadcast([64, HEADS, TOK]),
                                                   hmask[:].unsqueeze(2).to_broadcast([64, HEADS, TOK]), ALU.mult)
                last.then_inc(km_ready, 1)

            def shift(i, p, b):
                pool.wait_ge(mx_ready, 3 * num(i, p) + b + 1)
                n = (3 * p + b) % 2
                nc.gpsimd.tensor_tensor(sm[n][:], sm[n][:], mx[n][:].unsqueeze(2).to_broadcast([128, HEADS, KEYS]),
                                        ALU.subtract).then_inc(sub_ready, 1)

            def with_bias(i, p):
                g = num(i, p)
                pool.wait_ge(h1_ready, g + 1)
                at_least(pool, fin_ready, g - 1)
                nc.gpsimd.tensor_tensor(h1b[p][:], h1[p][:], bo[:].unsqueeze(1).to_broadcast([128, 3, 64]), ALU.add
                                        ).then_inc(h1b_ready, 1)

            for p in range(2):
                power(va1, rs1, va1_ready, rs1_ready, 0, p)
            keys(0, 0)

            def step(i, p, b):
                here, prev = at(i, p, 0, 0), at(i, p, 0, 3)
                nxt, nxt2 = here and at(i, p, 0, -3), here and at(i, p, 0, -6)
                if here:
                    shift(i, p, b)
                if b == 0 and nxt:
                    keys(*nxt[0:2])
                if b == 1 and prev:
                    power(va2, rs2, va2_ready, rs2_ready, *prev[0:2])
                    with_bias(*prev[0:2])
                if b == 2 and nxt2:
                    power(va1, rs1, va1_ready, rs1_ready, *nxt2[0:2])
            each_step(pool, step, 1, 3)


def layouts(inp):
    f = lambda k: np.asarray(inp[k])
    out = {}
    x = f("x").reshape(PAIRS, 2, YQ, CHUNKS, 4, X, 3)
    out["x"] = x.transpose(0, 4, 2, 6, 3, 1, 5).reshape(PAIRS, 48, CHUNKS, 128)
    wr, wi = (np.concatenate([f("L0_tok_w1" + a), f("L0_tok_w2" + a)], axis=3)
              .reshape(LAYERS, C, C, KY, 6, 2).transpose(0, 5, 1, 4, 3, 2) for a in "ri")
    w = np.empty((LAYERS, 2, 2, C, 6, KY, 2, C), np.float32)
    w[:, :, 0, ..., 0, :], w[:, :, 0, ..., 1, :] = wr, wi
    w[:, :, 1, ..., 0, :], w[:, :, 1, ..., 1, :] = wi, wr
    out["w"] = w.reshape(LAYERS, 128, MODES, 2, C)
    cw = np.zeros((C, YQ, LAYERS, YQ, C), np.float32)
    fc0 = np.zeros((128, YC, C), np.float32)
    fc1 = np.zeros((4, C, 4, 128), np.float32)
    for y in range(4):
        cw[:, y, :, y, :] = f("L0_tok_conv_w").transpose(2, 0, 1)
        fc1[y, :, y] = f("L0_tok_fc1_w")
    for y in range(YC):
        fc0[3 * y:3 * y + 3, y] = f("L0_tok_fc0_w")
    fc0[48] = f("L0_tok_fc0_b")
    out["conv_w"] = cw.reshape(128, LAYERS, 4, C)
    out["fc0"] = fc0
    out["conv_b"] = np.repeat(f("L0_tok_conv_b")[:, None, :], Y, axis=1)
    g = np.concatenate([f("L0_tok_ln0_g")[None], f("L0_tok_ln_g")])
    b = np.concatenate([f("L0_tok_ln0_b")[None], f("L0_tok_ln_b")])
    out["lnp"] = np.tile(np.stack([g[-1], b[-1]], axis=-1), (4, 1))
    out["gbx"] = np.tile(np.stack([g, b], axis=1)[None, 0:LAYERS], (128, 1, 1, 1))
    out["fc1_w"] = fc1.reshape(128, 4, 128)
    out["fc1_b"] = f("L0_tok_fc1_b")[:, None]
    out["fc2_w"] = f("L0_tok_fc2_w")
    out["fc2_b"] = np.tile(f("L0_tok_fc2_b"), 2)[:, None]
    fc3 = np.zeros((2, 64, 2), np.float32)
    for y in range(2):
        fc3[y, :, y] = f("L0_tok_fc3_w")[:, 0]
    out["fc3_w"] = fc3.reshape(128, 2)
    out["fc3_b"] = np.repeat(f("L0_tok_fc3_b")[:, None], 128, axis=0)
    st = f("x_txt")
    out["state"] = np.concatenate([st, st]).astype(np.int32)
    out["pos"] = np.tile(np.arange(TXT, dtype=np.float32), (128, 1))
    out["txt_gb"] = np.tile(np.stack([f("L0_txt_gamma"), f("L0_txt_beta")])[None], (128, 1, 1))
    for k in ("token_emb", "instr_emb", "arg_emb"):
        out[k] = f("L0_txt_" + k)
    rows = lambda a: np.concatenate([a, np.zeros((128 - len(a),) + a.shape[1:])])
    mask = np.zeros((128, 3, KEYS), np.float32)
    for b_ in range(3):
        q, k = (a // 11 * np.array([1]) for a in (BLK * b_ + np.arange(BLK), KEY0[b_] + np.arange(KEYS)))
        qc, kc = (BLK * b_ + np.arange(BLK)) % 11, (KEY0[b_] + np.arange(KEYS)) % 11
        far = (abs(q[:, None] - k[None]) > 3) | (abs(qc[:, None] - kc[None]) > 3)
        for m in range(2):
            mask[64 * m:64 * m + BLK, b_] = np.where(far, -1e30, 0)
    out["mask"] = mask
    out["hmask"] = np.where(np.arange(64)[:, None] // HD == np.arange(HEADS), HD ** -0.5, 0)
    out["temp"] = np.tile(f("L0_attn_temperature"), 64)[:, None]
    for n, k in enumerate(("wq", "wk", "wv")):
        out[k] = rows(f("L0_attn_W_qkv")[64 * n:64 * n + 64].T)
    out["wp"] = rows(np.concatenate([f("L0_attn_W_proj").T, f("L0_attn_b_proj")[None]]))
    out["wi"] = rows(f("L0_ffn_Wi").T)
    out["bi"] = f("L0_ffn_bi")[:, None]
    out["wr"] = f("L0_ffn_Wr").transpose(3, 0, 1, 2)
    out["ws"] = f("L0_ffn_Ws")[:, 0].transpose(2, 0, 1)
    out["br"] = f("L0_ffn_br").transpose(2, 0, 1)
    out["bs"] = f("L0_ffn_bs")[:, 0].T
    out["wo"] = f("L0_ffn_Wo").T
    out["bo"] = np.tile(f("L0_ffn_bo"), (128, 1))
    out["route"] = f("L0_ffn_route_id")[None].astype(np.int32)
    kx, n64 = np.arange(KX), np.arange(64)
    ky = np.concatenate([np.arange(KYH), np.arange(64 - KYH, 64)])
    tx = 2 * np.pi * np.outer(n64, kx) / 64
    ty = 2 * np.pi * np.outer(n64, ky) / 64
    d1 = np.zeros((2, 64, 2, KX, 3))
    ex = np.zeros((2, KX, 2, 2, 64))
    weight = np.where(kx == 0, 1.0, 2.0)[:, None] / (64 * 64)
    for m in range(2):
        d1[m, :, m, :, 0], d1[m, :, m, :, 1], d1[m, :, m, :, 2] = np.cos(tx), -np.sin(tx), -np.cos(tx)
        ex[m, :, 0, m], ex[m, :, 1, m] = weight * np.cos(tx.T), -weight * np.sin(tx.T)
    out["d1"] = d1.reshape(128, 2, KX, 3)
    rows = lambda a: np.concatenate([a, np.zeros((128 - len(a),) + a.shape[1:])])
    ex = ex.reshape(2, KX // 2, 2, 2, 128).transpose(0, 2, 1, 3, 4)
    out["ex"] = rows(np.concatenate([ex.reshape(2 * TRIG, 128), np.ones((1, 128))]))
    out["cy"] = np.concatenate([np.cos(ty), np.sin(ty)])
    out["dyi"] = np.concatenate([rows(np.cos(ty.T))[0:64], rows(-np.sin(ty.T))[0:64]])
    out["sgn"] = np.tile(np.repeat([1.0, -1.0], C), 2)[:, None]
    out["ident"] = np.eye(128)
    out["ones"] = np.ones((1, 512))
    return {k: np.ascontiguousarray(v, dtype=v.dtype if v.dtype.kind == "i" else np.float32) for k, v in out.items()}


def kernel(**inputs):
    import concourse.bacc as bacc
    from concourse.bass_utils import run_bass_kernel_spmd

    nc = bacc.Bacc("TRN2", target_bir_lowering=False, num_devices=1)
    arrays = {f"in_{k}": v for k, v in layouts(inputs).items()}
    t = {k[3:]: nc.dram_tensor(k, v.shape, mybir.dt.from_np(v.dtype), kind="ExternalInput").ap()
         for k, v in arrays.items()}
    out = nc.dram_tensor("out", [IMGS, TOK, 64], F32, kind="ExternalOutput").ap()
    tokens = nc.dram_tensor("tokens", [IMGS, TOK, 64], F32).ap()
    token_network(nc, t, tokens)
    text_embedding(nc, t, tokens)
    attention_and_experts(nc, t, tokens, out)
    r = run_bass_kernel_spmd(nc, [arrays], core_ids=[0])
    return r.results[0]["out"]
```

```python
import numpy as np
import concourse.bass as bass
from concourse import mybir
from contextlib import ExitStack

F32 = mybir.dt.float32
I32 = mybir.dt.int32
ALU = mybir.AluOpType
ACT = mybir.ActivationFunctionType
AX = mybir.AxisListType

IMGS, Y, X, C = 64, 64, 64, 32
PAIRS = IMGS // 2
KX, KYH = 12, 12
KY = 2 * KYH
MODES = KYH * KX
LAYERS = 4
CHUNKS = 4
YC = Y // CHUNKS
YQ = 4
STEM = 0
COUPLES = PAIRS // 2
TRIG = 2 * KX
EPS = 1e-5
TXT = 77
TOK = Y + TXT
TH = (TXT + 1) // 2
GATHERS = 4
WCH = MODES // COUPLES
ROWBUFS = 4
PART1 = 64


def at_least(eng, sem, value):
    if isinstance(value, int) and value <= 0:
        return
    eng.wait_ge(sem, value)


def waits_apart(eng, passed):
    eng.sem_inc(passed, 1)


def each_step(eng, step, drain, per=CHUNKS):
    def couple(i, pairs=2):
        for p in range(pairs):
            for j in range(per):
                step(i, p, j)
    couple(0)
    couple(1)
    with eng.Fori(2, COUPLES - 1) as i:
        couple(i)
    couple(COUPLES - 1)
    couple(COUPLES, drain)


def behind(i, p, j, lag, per=CHUNKS):
    n, j = divmod(per * p + j - lag, per)
    i, p = i + n // 2, n % 2
    if isinstance(i, int) and not 0 <= i < COUPLES:
        return None
    return i, p, j


def token_network(nc, t, tokens):
    with ExitStack() as ctx:
        def sb(name, shape, dt=F32):
            return ctx.enter_context(nc.sbuf_tensor(name, shape, dt))

        def sem(name):
            return ctx.enter_context(nc.semaphore(name))

        h_dram = nc.dram_tensor("h_scratch", [PAIRS, 128, 16 * 128], F32).ap()
        g_dram = nc.dram_tensor("g_scratch", [IMGS, KY, KX * 2 * C], F32).ap()
        cb_dram = nc.dram_tensor("cb_scratch", [LAYERS, Y * C], F32).ap()

        wsb = sb("wsb", [128, MODES, 2, C])
        xsb = sb("xsb", [128, MODES, IMGS])
        hc = [sb(f"hc{p}", [128, 16, 128]) for p in range(2)]
        hp = [sb(f"hp{p}", [128, C, Y]) for p in range(2)]
        zb = [sb(f"zb{p}", [128, Y, C]) for p in range(2)]
        gt = [sb(f"gt{p}", [128, 2, KX, 2, C]) for p in range(2)]
        asb = sb("asb", [128, 2 * KX, 2, C])
        sq = [sb(f"sq{p}", [128, YC, C + 1]) for p in range(2)]
        zt = [sb(f"zt{p}", [128, YC, C]) for p in range(2)]
        var = [sb(f"var{p}", [128, YC]) for p in range(2)]
        rstd = [sb(f"rstd{p}", [128, YC]) for p in range(2)]
        mhalf = sb("mhalf", [128, YC])
        wmean = sb("wmean", [128, 2 * WCH])
        gs = [sb(f"gs{n}", [2 * IMGS, KX // 2, 2, C]) for n in range(ROWBUFS)]
        xin = [sb(f"xin{p}", [128, CHUNKS, 128]) for p in range(2)]
        a1 = [sb(f"a1{p}", [128, 512]) for p in range(2)]
        a2 = [sb(f"a2{p}", [128, 512]) for p in range(2)]
        hst = [sb(f"hst{p}", [34, 16, 128]) for p in range(2)]

        ident = sb("ident", [128, 128])
        d1 = sb("d1", [128, 2, KX, 3])
        cy = sb("cy", [128, KY])
        gbx = sb("gbx", [128, LAYERS, 2, C])
        dyi = sb("dyi", [128, Y])
        ex = sb("ex", [128, 128])
        sgn = sb("sgn", [128, 1])
        cw = sb("cw", [128, LAYERS, 4, C])
        cwm = sb("cwm", [128, LAYERS * 4])
        cbt = hp[0][0:LAYERS].rearrange("l c y -> l (c y)").rearrange("l (y c) -> l y c", c=C)
        cbm = hp[1][0:LAYERS, 0, :]
        f0 = sb("f0", [128, YC, C])
        f0m = sb("f0m", [128, YC])
        lnp = sb("lnp", [128, 2])
        fc1 = sb("fc1", [128, 4, 128])
        fc1b = sb("fc1b", [128, 1])
        fc2 = sb("fc2", [128, 64])
        fc2b = sb("fc2b", [128, 1])
        fc3 = sb("fc3", [128, 2])
        fc3b = sb("fc3b", [128, 1])

        state = sb("state", [128, TXT], I32)
        idx = sb("idx", [128, 3, TH], I32)
        emb = sb("emb", [128, TH, 64])
        txt_gb = sb("txt_gb", [128, 2, 64])
        tstat = sb("tstat", [128, TH])
        tmhalf = sb("tmhalf", [128, TH])
        PAD = 64
        add = [a1[b][:, 0:PAD + TXT] for b in range(2)]
        top = [a2[b][:, 0:PAD + TXT] for b in range(2)]
        pos, args = a1[0][:, 256:256 + TXT], a2[0][:, 256:256 + TXT]
        spare = [(hp[p][:], xin[p][:].rearrange("p j (a n) -> p (j a) n", n=64)[:, 0:TH - C]) for p in range(2)]
        pieces = [slice(0, C), slice(C, TH)]

        ps = ctx.enter_context(nc.psum_tensor("ps", [128, 8, 512], F32))
        t_ps, x_ps = ps[:, 2, :], ps[:, 5, 0:MODES * 2]

        def z_ps(s, j, h):
            return ps[64 * h:64 * h + 2 * TRIG, 3 if j % 2 and not is_last(s) else 4, :]

        def main_ps(s, j):
            return ps[:, (0, 1, 3, 4)[j] if s is STEM else j % 2, :]

        def is_last(s):
            return isinstance(s, int) and s == LAYERS

        a_ps = [ps[:, 6 + b, 0:4 * 2 * KX * 3] for b in range(2)]
        f1_ps = [ps[:, 6, :], ps[:, 7, :]]
        f2_ps = [ps[:, 3, :], ps[:, 5, :]]
        f3_ps = [ps[64 + 32 * b:66 + 32 * b, 4, :] for b in range(2)]

        const_in = sem("const_in")
        late_in = sem("late_in")
        xin_zero = sem("xin_zero")
        small_step = sem("small_step")
        passed = sem("passed")
        zeroed = sem("zeroed")
        consts_ready = sem("consts_ready")
        cb_out = sem("cb_out")
        zbias_in = sem("zbias_in")
        xin_in = [sem(f"xin_in{p}") for p in range(2)]
        w_in = sem("w_in")
        w_mean = sem("w_mean")
        w_sub = sem("w_sub")
        w_cent = sem("w_cent")
        main_ready = sem("main_ready")
        sq_ready = sem("sq_ready")
        var_ready = sem("var_ready")
        rstd_ready = sem("rstd_ready")
        norm_ready = sem("norm_ready")
        gain_ready = sem("gain_ready")
        zt_ready = sem("zt_ready")
        hp_ready = sem("hp_ready")
        t_ready = sem("t_ready")
        hc_ready = sem("hc_ready")
        a_psr = sem("a_psr")
        a_ready = [sem(f"a_ready{b}") for b in range(2)]
        x_psr = sem("x_psr")
        x_ready = sem("x_ready")
        z_psr = sem("z_psr")
        zb_ready = [sem(f"zb_ready{h}") for h in range(2)]
        h_out = [sem(f"h_out{j}") for j in range(CHUNKS)]
        h_in = [[sem(f"h_in{p}{j}") for j in range(CHUNKS)] for p in range(2)]
        gt_in = [sem(f"gt_in{p}") for p in range(2)]
        mix_ready = sem("mix_ready")
        gs_ready = sem("gs_ready")
        g_out = [sem(f"g_out{n}") for n in range(ROWBUFS)]
        gt_ready = sem("gt_ready")
        f1_psr = sem("f1_psr")
        a1_ready = sem("a1_ready")
        f2_psr = sem("f2_psr")
        a2_ready = sem("a2_ready")
        f3_psr = sem("f3_psr")
        hst_ready = sem("hst_ready")
        tok_out = [sem(f"tok_out{p}") for p in range(2)]

        txt_in = sem("txt_in")
        scan = sem("scan")
        idx_ready = sem("idx_ready")
        gathered = sem("gathered")
        tnorm = sem("tnorm")
        trstd_ready = sem("trstd_ready")
        txt_out = sem("txt_out")

        block = ctx.enter_context(nc.Block())
        loads = [(f0, t["fc0"]), (cbt, t["conv_b"]), (cw, t["conv_w"]), (gbx, t["gbx"]), (lnp, t["lnp"]),
                 (ident, t["ident"]), (d1, t["d1"]), (cy, t["cy"])]
        late_loads = [(dyi, t["dyi"]), (ex, t["ex"]), (sgn, t["sgn"]), (fc1, t["fc1_w"]), (fc1b, t["fc1_b"]),
                      (fc2, t["fc2_w"]), (fc2b, t["fc2_b"]), (fc3, t["fc3_w"]), (fc3b, t["fc3_b"])]
        CONSTS = 8
        TNORM = 15
        NCONST = 16 * (len(loads) + 2)
        NLATE = 16 * len(late_loads)

        def rank(s, i, p):
            return s * PAIRS + 2 * i + p

        def stored(eng, s, r):
            if r >= ROWBUFS:
                eng.wait_ge(g_out[r % ROWBUFS], 32 * (KY // ROWBUFS * (s - 1) + r // ROWBUFS))

        def copy_parts(copy, eng, s, i, p, j):
            eng.wait_ge(a_psr, 4 * rank(s, i, p) + j + 1)
            for a in range(2):
                for h in range(2):
                    last = copy(asb[64 * a:64 * a + 64, :, :, 8 * j + h:8 * j + 8:2].rearrange("p x s g -> p g x s"),
                                a_ps[j % 2][64 * h:64 * h + 64].rearrange("p (g x s) -> p g x s", g=4, s=3)[:, :, :, a:a + 2])
            last.then_inc(a_ready[j % 2], 1)

        def z_halves(s):
            return range(1) if is_last(s) else range(2)

        def z_half(p, j, h):
            return zb[p][0:2 * TRIG, :, 8 * j + h:8 * j + 8:2].rearrange("k y c -> k c y")

        @block.sync
        def _(sp):
            for dst, src in loads:
                sp.dma_start(dst[:], src[:]).then_inc(const_in, 16)
            sp.wait_ge(xin_zero, 2)
            for p in range(2):
                sp.dma_start(xin[p][48:49], t["ones"][:, 0:512].rearrange("a (j n) -> a j n", j=CHUNKS)).then_inc(const_in, 16)
            for p in range(2):
                sp.dma_start(xin[p][0:48], t["x"][p]).then_inc(xin_in[p], 16)
            for dst, src in late_loads:
                sp.dma_start(dst[:], src[:]).then_inc(late_in, 16)
            for dst, name in ((state[:], "state"), (pos, "pos"), (txt_gb[:], "txt_gb")):
                sp.dma_start(dst, t[name]).then_inc(txt_in, 16)
            sp.wait_ge(zeroed, 4)
            sp.wait_ge(consts_ready, 1)
            sp.dma_start(cb_dram.rearrange("l (y c) -> l y c", c=C), cbt[:]).then_inc(cb_out, 16)
            sp.wait_ge(cb_out, 16)

            def load_w(s, i):
                if not (isinstance(i, int) and i == 0 and isinstance(s, int) and s == 0):
                    sp.wait_ge(w_cent, s * COUPLES + i)
                    waits_apart(sp, passed)
                sp.dma_start(wsb[:, bass.ds(i * WCH, WCH)], t["w"][bass.ds(s, 1), :, bass.ds(i * WCH, WCH)]
                             .rearrange("a p m s c -> (a p) m s c")).then_inc(w_in, 16)

            def h_chunk(i, p, j):
                return h_dram[bass.ds(2 * i + p, 1), :, 512 * j:512 * j + 512].rearrange("a p n -> (a p) n")

            def hc_chunk(p, j):
                return hc[p][:, 4 * j:4 * j + 4, :].rearrange("p a n -> p (a n)")

            def store_h(s, i, p, j):
                sp.wait_ge(hc_ready, 4 * rank(s, i, p) + j + 1)
                waits_apart(sp, passed)
                sp.dma_start(h_chunk(i, p, j), hc_chunk(p, j)).then_inc(h_out[j], 16)

            def load_h(i, p, j):
                sp.dma_start(hc_chunk(p, j), h_chunk(i, p, j)).then_inc(h_in[p][j], 16)

            def load_gt(i, p):
                sp.dma_start(gt[p][0:KY].rearrange("k m x s c -> k m (x s c)"),
                             g_dram[bass.ds(4 * i + 2 * p, 2)].rearrange("m k n -> k m n")).then_inc(gt_in[p], 16)

            def stem_step(i, p, j):
                if behind(i, p, j, 0):
                    if p == 0 and j == 0:
                        load_w(0, i)
                if c := behind(i, p, j, 3):
                    store_h(0, *c)
                    if c[2] == 3 and (nxt := behind(*c, -2 * CHUNKS)):
                        sp.wait_ge(main_ready, 4 * rank(0, c[0], c[1]) + 4)
                        waits_apart(sp, passed)
                        sp.dma_start(xin[c[1]][0:48], t["x"][bass.ds(2 * nxt[0] + nxt[1], 1)]
                                     .rearrange("a k j n -> (a k) j n")).then_inc(xin_in[c[1]], 16)
            each_step(sp, stem_step, 1)

            def between(s):
                for j in range(CHUNKS):
                    sp.wait_ge(h_out[j], 16 * PAIRS * s)
                waits_apart(sp, passed)
                for p in range(2):
                    for j in range(CHUNKS):
                        load_h(0, p, j)
                    sp.dma_start(zb[p][2 * TRIG:2 * TRIG + 1].rearrange("a y c -> a (y c)"),
                                 cb_dram[bass.ds(s - 1, 1)]).then_inc(zbias_in, 16)
                for r in range(KY):
                    row = (s - 1) * KY + r
                    sp.wait_ge(gs_ready, row + 1)
                    waits_apart(sp, passed)
                    for b in range(2):
                        sp.dma_start(g_dram[:, r, KX * C * b:KX * C * (b + 1)],
                                     gs[r % ROWBUFS][64 * b:64 * b + IMGS].rearrange("i x s c -> i (x s c)")
                                     ).then_inc(g_out[r % ROWBUFS], 16)
                for n in range(ROWBUFS):
                    sp.wait_ge(g_out[n], 32 * (KY // ROWBUFS) * s)
                    waits_apart(sp, passed)
                for p in range(2):
                    load_gt(0, p)

            def layer_pass(s, final):
                between(s)

                def step(i, p, j):
                    if behind(i, p, j, 0) and j == 0:
                        if p == 0 and not final:
                            load_w(s, i)
                        if nxt := behind(i, p, 0, -2 * CHUNKS):
                            sp.wait_ge(z_psr, 4 * (rank(s, i, p) - PAIRS) + 4)
                            waits_apart(sp, passed)
                            load_gt(*nxt[0:2])
                    if not final and (c := behind(i, p, j, 3)):
                        store_h(s, *c)
                    if c := behind(i, p, j, 4):
                        if nxt := behind(*c, -2 * CHUNKS):
                            if final:
                                sp.wait_ge(hst_ready, 4 * (2 * c[0] + c[1]) + c[2] + 1)
                                waits_apart(sp, passed)
                            else:
                                sp.wait_ge(h_out[c[2]], 16 * (PAIRS * s + 2 * c[0] + c[1] + 1))
                                waits_apart(sp, passed)
                            load_h(*nxt)
                        if final and c[2] == 3:
                            n = 2 * c[0] + c[1]
                            sp.wait_ge(hst_ready, 4 * n + 4)
                            waits_apart(sp, passed)
                            for m in range(2):
                                for b in range(2):
                                    sp.dma_start(tokens[bass.ds(2 * n + m, 1), 32 * b:32 * b + 32, :]
                                                 .rearrange("a (q r) x -> (a q) r x", q=2),
                                                 hst[c[1]][32 * b:32 * b + 2, :, 64 * m:64 * m + 64]
                                                 ).then_inc(tok_out[c[1]], 16)
                each_step(sp, step, 1)

            with sp.Fori(1, LAYERS) as s:
                layer_pass(s, False)
            layer_pass(LAYERS, True)
            sp.wait_ge(tnorm, TNORM)
            sp.dma_start(tokens[:, Y:Y + TH, :], emb[0:64]).then_inc(txt_out, 16)
            sp.dma_start(tokens[:, Y + TH:TOK, :], emb[64:128, 0:TXT - TH]).then_inc(txt_out, 16)
            sp.wait_ge(txt_out, 32)
            for p in range(2):
                sp.wait_ge(tok_out[p], 64 * COUPLES)

        @block.tensor
        def _(pe):
            pe.wait_ge(const_in, NCONST)
            pe.wait_ge(consts_ready, CONSTS)

            def main(s, i, p, j):
                g = rank(s, i, p)
                q = 4 * g + j
                m = main_ps(s, j)
                at_least(pe, norm_ready, q - 3 if s is STEM else q - 1)
                if s is STEM:
                    if j == 0:
                        pe.wait_ge(xin_in[p], 16 * (i + 1))
                    nc.tensor.matmul(m, xin[p][:, j, :], f0[:].rearrange("k y c -> k (y c)"),
                                     start=True, stop=True).then_inc(main_ready, 1)
                    return
                pe.wait_ge(h_in[p][j], 16 * (COUPLES * (s - 1) + i + 1))
                if j == 0:
                    for h in z_halves(s):
                        pe.wait_ge(zb_ready[h], 4 * (g - PAIRS) + 4)
                    if isinstance(i, int) and i == 0 and p == 0:
                        pe.wait_ge(zbias_in, 32 * s)
                nc.tensor.matmul(m, ex[:], zb[p][:].rearrange("k (q r) c -> k r q c", q=YQ)[:, 4 * j:4 * j + 4],
                                 start=True, stop=False, skip_group_check=True)
                for k in range(4):
                    last = nc.tensor.matmul(m[:, 128 * k:128 * k + 128], hc[p][:, 4 * j + k, :],
                                            cw[:, bass.ds(s - 1, 1)].rearrange("p a y c -> p (a y c)"),
                                            start=False, stop=True, skip_group_check=True)
                last.then_inc(main_ready, 1)

            def i1(s, i, p, j):
                idx = 4 * (rank(s, i, p) - PAIRS) + j
                if j == 0:
                    pe.wait_ge(gt_ready, rank(s, i, p) - PAIRS + 1)
                ago = 1 if is_last(s) else 2
                if not (isinstance(i, int) and i == 0 and p == 0 and j < ago):
                    for h in z_halves(s):
                        pe.wait_ge(zb_ready[h], idx + 1 - ago)
                for k in range(8):
                    w = len(z_halves(s))
                    h, n = k % w, k // w
                    last = nc.tensor.matmul(z_ps(s, j, h)[:, 64 * n:64 * n + 64],
                                            gt[p][:, :, :, :, 8 * j + k].rearrange("k m x s -> k (m x s)"),
                                            dyi[:], start=True, stop=True)
                last.then_inc(z_psr, 1)

            def turn(s, i, p, j, final=False):
                q = 4 * rank(s, i, p) + j
                at_least(pe, hc_ready, q)
                if final:
                    pe.wait_ge(norm_ready, q + 1)
                else:
                    pe.wait_ge(hp_ready, q + 1)
                for k in range(4):
                    if final:
                        src = zt[j % 2][:, 4 * k:4 * k + 4, :].rearrange("p y c -> p (y c)")
                    else:
                        src = hp[p][:].rearrange("p c (q r) -> p (c q) r", q=YQ)[:, :, 4 * j + k]
                    last = nc.tensor.transpose(t_ps[:, 128 * k:128 * k + 128], src, ident[:])
                last.then_inc(t_ready, 1)

            def f1(s, i, p, j):
                g = rank(s, i, p)
                if j == 0:
                    pe.wait_ge(hp_ready, 4 * g + 4)
                at_least(pe, a_ready[j % 2], 2 * g + j // 2)
                for k in range(8):
                    h, n = k % 2, k // 2
                    last = nc.tensor.matmul(a_ps[j % 2][64 * h:64 * h + 64, 72 * n:72 * n + 72], hp[p][:, 8 * j + k, :],
                                            d1[:].rearrange("p m x s -> p (m x s)"), start=True, stop=True)
                last.then_inc(a_psr, 1)

            def f2(s, i, p, half):
                g = rank(s, i, p)
                if half == 0:
                    for b in range(2):
                        pe.wait_ge(a_ready[b], 2 * g + 2)
                    at_least(pe, x_ready, g)
                for k in range(KX // 2 * half, KX // 2 * half + KX // 2):
                    last = nc.tensor.matmul(x_ps[:, KY * k:KY * k + KY],
                                            asb[:, 2 * k:2 * k + 2].rearrange("y x s c -> y (x s c)"),
                                            cy[:], start=True, stop=True)
                if half:
                    last.then_inc(x_psr, 1)

            def run_pass(s):
                def step(i, p, j):
                    if behind(i, p, j, 0):
                        main(s, i, p, j)
                    if s is not STEM and (c := behind(i, p, j, -CHUNKS)):
                        i1(s, *c)
                    prev = behind(i, p, j, CHUNKS)
                    if prev and j >= 2:
                        f1(s, prev[0], prev[1], 2 * (j - 2))
                    if c := behind(i, p, j, 3):
                        turn(s, *c)
                    if prev and j >= 2:
                        f1(s, prev[0], prev[1], 2 * (j - 2) + 1)
                    if j < 2 and (c := behind(i, p, j, 2 * CHUNKS)):
                        f2(s, c[0], c[1], j)
                each_step(pe, step, 2)

            def mix(s):
                pe.wait_ge(x_ready, PAIRS * s)
                pe.wait_ge(w_cent, COUPLES * s)
                waits_apart(pe, passed)
                for r in range(KY):
                    row = (s - 1) * KY + r
                    if r >= ROWBUFS:
                        pe.wait_ge(gs_ready, row - ROWBUFS + 1)
                        waits_apart(pe, passed)
                    for a in range(6):
                        for b in range(2):
                            k = slice(64 * b, 64 * b + 64)
                            last = nc.tensor.matmul(
                                ps[64 * b:64 * b + IMGS, r % ROWBUFS, 64 * a:64 * a + 64],
                                xsb[k, KY * a + r, :], wsb[k, KY * a + r].rearrange("k s c -> k (s c)"),
                                start=True, stop=True, tile_position=(64 * b, 64 * b))
                    last.then_inc(mix_ready, 1)
                pe.wait_ge(gs_ready, KY * s)

            def fc3_rows(i, p, j, b):
                c = 4 * (2 * i + p) + j
                pe.wait_ge(a2_ready, 2 * c + b + 1)
                if b == 0:
                    at_least(pe, hst_ready, c)
                nc.tensor.matmul(f3_ps[b], fc3[:], a2[b][:], start=True, stop=True).then_inc(f3_psr, 1)

            def head(i, p, j):
                c = 4 * (2 * i + p) + j
                pe.wait_ge(hc_ready, 4 * rank(LAYERS, i, p) + j + 1)

                def fc1_row(y):
                    at_least(pe, a1_ready, 4 * c + y - 1)
                    nc.tensor.matmul(f1_ps[y % 2], fc1[:, y, :],
                                     hc[p][:, 4 * j:4 * j + 4, :].rearrange("c a n -> c (a n)"),
                                     start=True, stop=True).then_inc(f1_psr, 1)

                def fc2_row(y):
                    pe.wait_ge(a1_ready, 4 * c + y + 1)
                    if y % 2 == 0:
                        at_least(pe, a2_ready, 2 * c + y // 2 - 1)
                    nc.tensor.matmul(f2_ps[y // 2][64 * (y % 2):64 * (y % 2) + 64], fc2[:], a1[y % 2][:],
                                     start=True, stop=True).then_inc(f2_psr, 1)

                fc1_row(0)
                fc1_row(1)
                fc2_row(0)
                fc1_row(2)
                fc2_row(1)
                fc1_row(3)
                fc2_row(2)
                fc2_row(3)
                fc3_rows(i, p, j, 0)

            def final_pass(s):
                def step(i, p, j):
                    if c := behind(i, p, j, 2):
                        turn(s, *c, final=True)
                    if behind(i, p, j, 0):
                        main(s, i, p, j)
                    if c := behind(i, p, j, -CHUNKS):
                        i1(s, *c)
                    if c := behind(i, p, j, 4):
                        fc3_rows(*c, 1)
                    if c := behind(i, p, j, 3):
                        head(*c)
                each_step(pe, step, 1)

            run_pass(STEM)
            pe.wait_ge(late_in, NLATE)
            with pe.Fori(1, LAYERS) as s:
                mix(s)
                for j in range(CHUNKS):
                    i1(s, 0, 0, j)
                run_pass(s)
            mix(LAYERS)
            for j in range(CHUNKS):
                i1(LAYERS, 0, 0, j)
            final_pass(LAYERS)

        @block.scalar
        def _(act):
            act.wait_ge(const_in, NCONST)
            act.wait_ge(consts_ready, CONSTS)
            act.wait_ge(cb_out, 16)

            def square(s, i, p, j):
                q = 4 * rank(s, i, p) + j
                act.wait_ge(main_ready, q + 1)
                at_least(act, var_ready, q - 1)
                nc.scalar.activation(sq[j % 2][:, :, 0:C], main_ps(s, j).rearrange("p (y c) -> p y c", c=C), ACT.Square
                                     ).then_inc(sq_ready, 1)

            def chunk_of_hc(p, j):
                return hc[p][:, 4 * j:4 * j + 4, :].rearrange("p a n -> p (a n)")

            def activate(s, i, p, j, func):
                g = rank(s, i, p)
                if j == 0:
                    at_least(act, a_psr, 4 * (g - 1))
                act.wait_ge(zt_ready, 4 * g + j + 1)
                nc.scalar.activation(hp[p][:].rearrange("p c (q r) -> p c q r", q=YQ)[:, :, :, 4 * j:4 * j + 4],
                                     zt[j % 2][:].rearrange("p (k q) c -> p c q k", k=4), func).then_inc(hp_ready, 1)

            def hc_copy(s, i, p, j):
                if s is STEM:
                    at_least(act, h_out[j], 16 * (2 * i + p - 1))
                act.wait_ge(t_ready, 4 * rank(s, i, p) + j + 1)
                nc.scalar.copy(chunk_of_hc(p, j), t_ps).then_inc(hc_ready, 1)

            def affine(s, i, p, j):
                act.wait_ge(t_ready, 4 * rank(s, i, p) + j + 1)
                nc.scalar.activation(chunk_of_hc(p, j), t_ps, ACT.Identity, bias=lnp[:, 1:2], scale=lnp[:, 0:1]
                                     ).then_inc(hc_ready, 1)

            def a_copy(s, i, p, j):
                copy_parts(nc.scalar.copy, act, s, i, p, j)

            def z_copy(s, i, p, j):
                idx = 4 * (rank(s, i, p) - PAIRS) + j
                act.wait_ge(z_psr, idx + 1)
                nc.scalar.copy(z_half(p, j, 1), z_ps(s, j, 1)[:, 0:256].rearrange("k (c y) -> k c y", c=4)
                               ).then_inc(zb_ready[1], 1)

            def x_copy(s, i, p):
                act.wait_ge(x_psr, rank(s, i, p) + 1)
                nc.scalar.copy(xsb[:, :, bass.ds(4 * i + 2 * p, 2)].rearrange("p k m -> p m k"),
                               x_ps.rearrange("p (m k) -> p m k", m=2)).then_inc(x_ready, 1)

            def run_pass(s, func):
                def step(i, p, j):
                    if behind(i, p, j, 0):
                        square(s, i, p, j)
                    if c := behind(i, p, j, 2):
                        activate(s, *c, func)
                    if s is not STEM and (c := behind(i, p, j, -CHUNKS)):
                        z_copy(s, *c)
                    prev = behind(i, p, j, CHUNKS)
                    if prev and j >= 2:
                        a_copy(s, prev[0], prev[1], 2 * (j - 2))
                    if c := behind(i, p, j, 3):
                        hc_copy(s, *c)
                    if s is not STEM and j == 3 and (c := behind(i, p, 0, -2 * CHUNKS)):
                        gt_part1(s, c[0], c[1])
                    if j == 1 and (c := behind(i, p, j, 2 * CHUNKS)):
                        x_copy(s, c[0], c[1])
                each_step(act, step, 2)

            def gt_part1(s, i, p):
                act.wait_ge(gt_in[p], 16 * (COUPLES * (s - 1) + i + 1))
                re, im = gt[p][0:KY, :, :, 0, :], gt[p][0:KY, :, :, 1, :]
                nc.scalar.copy(gt[p][PART1:PART1 + KY, :, :, 0, :], im)
                nc.scalar.mul(gt[p][PART1:PART1 + KY, :, :, 1, :], re, -1.0).then_inc(gt_ready, 1)

            def head(i, p, j):
                c = 4 * (2 * i + p) + j

                def gelu1(y):
                    act.wait_ge(f1_psr, 4 * c + y + 1)
                    at_least(act, f2_psr, 4 * c + y - 1)
                    nc.scalar.activation(a1[y % 2][:], f1_ps[y % 2], ACT.Gelu, bias=fc1b[:]).then_inc(a1_ready, 1)

                def gelu2(b):
                    act.wait_ge(f2_psr, 4 * c + 2 * b + 2)
                    at_least(act, f3_psr, 2 * c + b - 1)
                    nc.scalar.activation(a2[b][:], f2_ps[b], ACT.Gelu, bias=fc2b[:]).then_inc(a2_ready, 1)

                gelu1(0)
                gelu1(1)
                gelu1(2)
                gelu2(0)
                gelu1(3)
                gelu2(1)

            def final_pass(s):
                def step(i, p, j):
                    if c := behind(i, p, j, 2):
                        affine(s, *c)
                    if behind(i, p, j, 0):
                        square(s, i, p, j)
                    if j == 3 and (c := behind(i, p, 0, -2 * CHUNKS)):
                        gt_part1(s, c[0], c[1])
                    if c := behind(i, p, j, 3):
                        head(*c)
                each_step(act, step, 1)

            run_pass(STEM, ACT.Identity)
            act.wait_ge(late_in, NLATE)
            with act.Fori(1, LAYERS) as s:
                gt_part1(s, 0, 0)
                for j in range(CHUNKS):
                    z_copy(s, 0, 0, j)
                gt_part1(s, 0, 1)
                run_pass(s, ACT.Gelu)
            for p in range(2):
                gt_part1(LAYERS, 0, p)
            final_pass(LAYERS)

        @block.vector
        def _(dve):
            def text_rows():
                n = 0

                def link(*ins):
                    nonlocal n
                    for x in ins:
                        x.then_inc(scan, 1)
                    n += len(ins)
                    dve.wait_ge(scan, n)

                v = nc.vector
                link(*[v.memset(tile, 0.0) for tile in (*add, *top)], v.memset(idx[:], 0), v.memset(tmhalf[:], -0.5))
                dve.wait_ge(txt_in, 48)
                link(v.tensor_scalar(add[0][:, PAD + 1:], state[:, 0:TXT - 1], 5.0, None, ALU.is_equal))
                link(v.tensor_tensor(top[0][:, PAD:], add[0][:, PAD:], pos, ALU.mult))
                b = 0
                for d in (1, 2, 4, 8, 16, 32, 64):
                    link(v.tensor_tensor(add[1 - b][:, PAD:], add[b][:, PAD:], add[b][:, PAD - d:PAD - d + TXT], ALU.add),
                         v.tensor_tensor(top[1 - b][:, PAD:], top[b][:, PAD:], top[b][:, PAD - d:PAD - d + TXT], ALU.max))
                    b = 1 - b
                link(v.tensor_tensor(args, pos, top[b][:, PAD:], ALU.subtract))
                for half in range(2):
                    k, r, w = TH * half, slice(64 * half, 64 * half + 64), TH if half == 0 else TXT - TH
                    for m, src in enumerate((state[r, k:k + w], add[b][r, PAD + k:PAD + k + w], args[r, k:k + w])):
                        v.tensor_copy(idx[r, m, 0:w], src).then_inc(idx_ready, 1)

            def text_step(n):
                v, wide = nc.vector, [128, TH, 64]
                done = (0, 2, 4, 5, 7, 9, 11, 12, 13)[n]
                if n == 0:
                    dve.wait_ge(gathered, 16 * 3 * TH)
                dve.wait_ge(tnorm, done)
                if n < 2:
                    for piece, rows in zip(pieces, spare[n]):
                        v.tensor_tensor(emb[:, piece], emb[:, piece], rows, ALU.add).then_inc(tnorm, 1)
                if n == 2:
                    v.tensor_reduce(tstat[:], emb[:], axis=AX.X, op=ALU.add).then_inc(tnorm, 1)
                if n == 3:
                    v.tensor_scalar(tstat[:], tstat[:], 1.0 / 64, None, ALU.mult).then_inc(tnorm, 1)
                    dve.wait_ge(tnorm, done + 1)
                    v.tensor_tensor(emb[:], emb[:], tstat[:].unsqueeze(2).to_broadcast(wide), ALU.subtract).then_inc(tnorm, 1)
                if n == 4:
                    for piece, rows in zip(pieces, spare[0]):
                        v.tensor_tensor(rows, emb[:, piece], emb[:, piece], ALU.mult).then_inc(tnorm, 1)
                if n == 5:
                    for piece, rows in zip(pieces, spare[0]):
                        v.tensor_reduce(tstat[:, piece], rows, axis=AX.X, op=ALU.add).then_inc(tnorm, 1)
                if n == 6:
                    v.tensor_scalar(tstat[:], tstat[:], 1.0 / 64, EPS, ALU.mult, ALU.add).then_inc(tnorm, 1)
                if n == 7:
                    dve.wait_ge(trstd_ready, 1)
                    v.tensor_tensor(emb[:], emb[:], tstat[:].unsqueeze(2).to_broadcast(wide), ALU.mult).then_inc(tnorm, 1)
                if n == 8:
                    v.tensor_tensor(emb[:], emb[:], txt_gb[:, 0:1, :].to_broadcast(wide), ALU.mult).then_inc(tnorm, 1)
                    dve.wait_ge(tnorm, done + 1)
                    v.tensor_tensor(emb[:], emb[:], txt_gb[:, 1:2, :].to_broadcast(wide), ALU.add).then_inc(tnorm, 1)

            for p in range(2):
                nc.vector.memset(xin[p][:], 0.0).then_inc(xin_zero, 1)
            dve.wait_ge(const_in, NCONST)
            small = [(cbt[:], cbm), (cw[:].rearrange("p l y c -> p (l y) c"), cwm[:]), (f0[:], f0m[:])]
            for n, (tile, mean) in enumerate(small):
                shape = list(tile.shape)
                nc.vector.tensor_reduce(mean, tile, axis=AX.X, op=ALU.add).then_inc(small_step, 1)
                dve.wait_ge(small_step, 2 * n + 1)
                nc.vector.tensor_scalar(mean, mean, 1.0 / C, None, ALU.mult).then_inc(small_step, 1)
                dve.wait_ge(small_step, 2 * n + 2)
                nc.vector.tensor_tensor(tile, tile, mean.unsqueeze(2).to_broadcast(shape), ALU.subtract
                                        ).then_inc(consts_ready, 1)
            nc.vector.memset(mhalf[:], -0.5).then_inc(consts_ready, 1)
            for p in range(2):
                nc.vector.memset(sq[p][:, :, C:C + 1], C * EPS).then_inc(consts_ready, 1)
            for gain in (gbx[:, :, 0, :], lnp[:, 0:1]):
                nc.vector.tensor_scalar(gain, gain, float(np.sqrt(C)), None, ALU.mult).then_inc(consts_ready, 1)
            dve.wait_ge(consts_ready, CONSTS)

            def reduce(s, i, p, j):
                q = 4 * rank(s, i, p) + j
                dve.wait_ge(sq_ready, q + 1)
                at_least(dve, rstd_ready, q - 1)
                nc.vector.tensor_reduce(var[j % 2][:], sq[j % 2][:], axis=AX.X, op=ALU.add).then_inc(var_ready, 1)

            def normalise(s, i, p, j, final=False):
                q = 4 * rank(s, i, p) + j
                dve.wait_ge(rstd_ready, q + 1)
                if final:
                    dve.wait_ge(t_ready, q - 1)
                else:
                    at_least(dve, hp_ready, q - 1)
                nc.vector.tensor_tensor(zt[j % 2][:], main_ps(s, j).rearrange("p (y c) -> p y c", c=C),
                                        rstd[j % 2][:].unsqueeze(2).to_broadcast([128, YC, C]), ALU.mult
                                        ).then_inc(norm_ready, 1)

            def affine(s, i, p, j, bias):
                q = 4 * rank(s, i, p) + j
                z = zt[j % 2][:]
                which, op, before, after = (1, ALU.add, gain_ready, zt_ready) if bias else (0, ALU.mult, norm_ready, gain_ready)
                dve.wait_ge(before, q + 1)
                nc.vector.tensor_tensor(z, z, gbx[:, bass.ds(s, 1), which, :].to_broadcast([128, YC, C]), op
                                        ).then_inc(after, 1)

            def z_copy(s, i, p, j, final=False):
                idx = 4 * (rank(s, i, p) - PAIRS) + j
                dve.wait_ge(z_psr, idx + 1)
                if final:
                    nc.vector.tensor_copy(zb[p][0:2 * TRIG, :, 8 * j:8 * j + 8].rearrange("k y c -> k c y"),
                                          z_ps(s, j, 0).rearrange("k (c y) -> k c y", c=8)).then_inc(zb_ready[0], 1)
                else:
                    nc.vector.tensor_copy(z_half(p, j, 0), z_ps(s, j, 0)[:, 0:256].rearrange("k (c y) -> k c y", c=4)
                                          ).then_inc(zb_ready[0], 1)

            def w_sum(s, i):
                dve.wait_ge(w_in, 16 * (COUPLES * s + i + 1))
                if not (isinstance(i, int) and i == 0 and s is STEM):
                    dve.wait_ge(w_cent, COUPLES * s + i)
                nc.vector.tensor_reduce(wmean[:], wsb[:, bass.ds(i * WCH, WCH)].rearrange("p m s c -> p (m s) c"),
                                        axis=AX.X, op=ALU.add).then_inc(w_mean, 1)

            def a_copy(s, i, p, j):
                copy_parts(nc.vector.tensor_copy, dve, s, i, p, j)

            def run_pass(s, final=False):
                def step(i, p, j):
                    if behind(i, p, j, 0):
                        reduce(s, i, p, j)
                    nxt = s is not STEM and behind(i, p, j, -CHUNKS)
                    if nxt and j == 3:
                        z_copy(s, *nxt, final)
                    c = behind(i, p, j, 1)
                    if c:
                        normalise(s, *c, final)
                    if c and not final:
                        affine(s, *c, bias=False)
                    if nxt and j < 3:
                        z_copy(s, *nxt, final)
                    if c and not final:
                        affine(s, *c, bias=True)
                    prev = None if final else behind(i, p, j, CHUNKS)
                    if prev and j >= 2:
                        a_copy(s, prev[0], prev[1], 2 * (j - 2) + 1)
                    if final and (c := behind(i, p, j, 4)):
                        out_copy(*c)
                    if not final and p == 0 and j == 1 and behind(i, p, j, 0):
                        w_sum(s, i)
                    if final and isinstance(i, int) and 0 <= (n := CHUNKS * (2 * (i - COUPLES + 1) + p) + j) < 9:
                        text_step(n)
                each_step(dve, step, 2)

            def out_copy(i, p, j):
                c = 4 * (2 * i + p) + j
                dve.wait_ge(f3_psr, 2 * c + 2)
                if j == 0 and not (isinstance(i, int) and i == 0):
                    dve.wait_ge(tok_out[p], 64 * i)
                for b in range(2):
                    last = nc.vector.tensor_scalar(hst[p][32 * b:32 * b + 2, 4 * j:4 * j + 4, :].rearrange("k a n -> k (a n)"),
                                                   f3_ps[b], fc3b[64 + 32 * b:66 + 32 * b], None, ALU.add)
                last.then_inc(hst_ready, 1)

            def mix(s):
                for r in range(KY):
                    stored(dve, s, r)
                    dve.wait_ge(mix_ready, (s - 1) * KY + r + 1)
                    nc.vector.tensor_copy(gs[r % ROWBUFS][:].rearrange("i a s c -> i (a s c)"), ps[:, r % ROWBUFS, 0:KX * C]
                                          ).then_inc(gs_ready, 1)

            run_pass(STEM)
            dve.wait_ge(late_in, NLATE)
            with dve.Fori(1, LAYERS) as s:
                mix(s)
                for j in range(CHUNKS):
                    z_copy(s, 0, 0, j)
                run_pass(s)
            text_rows()
            mix(LAYERS)
            for j in range(CHUNKS):
                z_copy(LAYERS, 0, 0, j, final=True)
            run_pass(LAYERS, final=True)

        @block.gpsimd
        def _(pool):
            for tile in (gt[0], gt[1], zb[0], zb[1]):
                nc.gpsimd.memset(tile[:], 0.0).then_inc(zeroed, 1)
            pool.wait_ge(const_in, NCONST)
            pool.wait_ge(consts_ready, CONSTS)

            def rstds(s, i, p, j):
                q = 4 * rank(s, i, p) + j
                pool.wait_ge(var_ready, q + 1)
                nc.gpsimd.tensor_tensor(rstd[j % 2][:], var[j % 2][:], mhalf[:], ALU.pow).then_inc(rstd_ready, 1)

            def w_centre(s, i):
                k = COUPLES * s + i
                chunk = wsb[:, bass.ds(i * WCH, WCH)]
                if s is STEM and isinstance(i, int) and i == 0:
                    pool.wait_ge(late_in, NLATE)
                pool.wait_ge(w_mean, k + 1)
                waits_apart(pool, passed)
                nc.gpsimd.tensor_scalar(wmean[:], wmean[:], 1.0 / C, None, ALU.mult).then_inc(w_sub, 1)
                pool.wait_ge(w_sub, 2 * k + 1)
                flat = chunk.rearrange("p m s c -> p (m s) c")
                nc.gpsimd.tensor_tensor(flat, flat, wmean[:].unsqueeze(2).to_broadcast([128, 2 * WCH, C]),
                                        ALU.subtract).then_inc(w_sub, 1)
                pool.wait_ge(w_sub, 2 * k + 2)
                waits_apart(pool, passed)
                nc.gpsimd.tensor_tensor(chunk[:, :, 0, :], chunk[:, :, 0, :], sgn[:].unsqueeze(2).to_broadcast([128, WCH, C]),
                                        ALU.mult).then_inc(w_cent, 1)

            def run_pass(s, final=False):
                def step(i, p, j):
                    if behind(i, p, j, 0):
                        rstds(s, i, p, j)
                        if p == 0 and j == 1 and not final:
                            w_centre(s, i)
                        if final and isinstance(i, int) and i < 2:
                            gather(EARLY + GATHERS * (CHUNKS * (2 * i + p) + j), GATHERS)
                        if final and isinstance(i, int) and i == COUPLES - 1 and p == 1 and j == 2:
                            pool.wait_ge(tnorm, 12)
                            nc.gpsimd.tensor_tensor(tstat[:], tstat[:], tmhalf[:], ALU.pow).then_inc(trstd_ready, 1)
                each_step(pool, step, 0)

            EARLY = 3 * TH - GATHERS * CHUNKS * 4

            def gather(first, count):
                for k, c in [divmod(n, TH) for n in range(first, first + count)]:
                    dst = emb[:, c, :] if k == 0 else spare[k - 1][0][:, c, :] if c < C else spare[k - 1][1][:, c - C, :]
                    nc.gpsimd.indirect_dma_start(
                        out=dst, out_offset=None, in_=t[("token_emb", "instr_emb", "arg_emb")[k]],
                        in_offset=bass.IndirectOffsetOnAxis(ap=idx[:, k, c:c + 1], axis=0)).then_inc(gathered, 16)

            run_pass(STEM)
            with pool.Fori(1, LAYERS) as s:
                run_pass(s)
            pool.wait_ge(idx_ready, 6)
            pool.wait_ge(t_ready, CHUNKS * PAIRS * LAYERS)
            pool.wait_ge(a_psr, CHUNKS * PAIRS * LAYERS)
            gather(0, EARLY)
            run_pass(LAYERS, final=True)



BLK = TOK // 3
KEYS = 119
KEY0 = [0, 11, 22]
HEADS, HD = 8, 8
HID, EXPERTS = 128, 16
QPAD = 160
assert 3 * BLK == TOK and KEY0[2] + KEYS == TOK


def attention_and_experts(nc, t, tokens, out):
    with ExitStack() as ctx:
        def sb(name, shape, dt=F32):
            return ctx.enter_context(nc.sbuf_tensor(name, shape, dt))

        def sem(name):
            return ctx.enter_context(nc.semaphore(name))

        xs = [sb(f"xs{p}", [128, 3, 64]) for p in range(2)]
        xr = [sb(f"xr{p}", [128, 3, 64]) for p in range(2)]
        xn = sb("xn", [128, 3, 64])
        xsq = sb("xsq", [128, 3, 64])
        st1 = sb("st1", [128, 3])
        mu1 = sb("mu1", [128, 3])
        va1 = sb("va1", [128, 3])
        rs1 = sb("rs1", [128, 3])
        xT = sb("xT", [128, 2, QPAD])
        qT = [sb(f"qT{p}", [128, 2, QPAD]) for p in range(2)]
        kT = sb("kT", [64, 2, TOK])
        km = [sb(f"km{p}", [128, 2, HEADS, TOK]) for p in range(2)]
        vv = [sb(f"vv{p}", [KEYS, 2, 3, HEADS, HD + 1]) for p in range(2)]
        sm = [sb(f"sm{b}", [128, HEADS, KEYS]) for b in range(2)]
        mx = [sb(f"mx{b}", [128, HEADS]) for b in range(2)]
        rden = sb("rden", [128, 3 * HEADS])
        pT = sb("pT", [KEYS, HEADS, 128])
        osb = sb("osb", [128, 3, 64])
        oT = sb("oT", [128, 3, 128])
        h1 = [sb(f"h1{p}", [128, 3, 64]) for p in range(2)]
        h1b = [sb(f"h1b{p}", [128, 3, 64]) for p in range(2)]
        yn = sb("yn", [128, 3, 64])
        ysq = sb("ysq", [128, 3, 64])
        st2 = sb("st2", [128, 3])
        mu2 = sb("mu2", [128, 3])
        va2 = sb("va2", [128, 3])
        rs2 = sb("rs2", [128, 3])
        yT = sb("yT", [128, 3, 128])
        ff = [sb(f"ff{k}", [128, 3, 2, 64]) for k in range(3)]
        wc = [sb(f"wc{p}", [128, 2, 2, HID]) for p in range(2)]
        bc = [sb(f"bc{p}", [128, 2, 2]) for p in range(2)]
        fin = [sb(f"fin{p}", [128, 3, 64]) for p in range(2)]

        ident = sb("identt", [128, 128])
        mask = sb("mask", [128, 3, KEYS])
        hmask = sb("hmask", [64, HEADS])
        temp = sb("temp", [64, 1])
        mh = sb("mh", [128, 3])
        wq = sb("wq", [128, 64])
        wk = sb("wk", [128, 64])
        wv = sb("wv", [128, 64])
        wp = sb("wp", [128, 64])
        wi = sb("wi", [128, HID])
        bi = sb("bi", [128, 1])
        wr = sb("wr", [128, 2, EXPERTS, HID])
        ws = sb("ws", [128, 2, HID])
        br = sb("br", [128, 2, EXPERTS])
        bs = sb("bs", [128, 2])
        wo = sb("wo", [128, 64])
        bo = sb("bo", [128, 64])
        route = sb("route", [1, IMGS], I32)

        ps = ctx.enter_context(nc.psum_tensor("pst", [128, 8, 512], F32))
        s_ps = ps[:, 0:2, 0:4 * KEYS]
        p_ps = ps[0:KEYS, 2:4, :]
        o_ps = ps[:, 4, 0:3 * HEADS * (HD + 1)]
        fr_ps = [ps[:, 5, :], ps[:, 6, :]]
        ff_ps = ps[:, 7, :]

        t_const = sem("t_const")
        t_experts = sem("t_experts")
        xs_zero = sem("xs_zero")
        t_zero = sem("t_zero")
        t_passed = sem("t_passed")
        t_setup = sem("t_setup")
        xs_in = [sem(f"xs_in{p}") for p in range(2)]
        xr_in = [sem(f"xr_in{p}") for p in range(2)]
        c1 = sem("c1")
        va1_ready = sem("va1_ready")
        rs1_ready = sem("rs1_ready")
        xn_ready = sem("xn_ready")
        xT_psr = sem("xT_psr")
        xT_ready = sem("xT_ready")
        q_psr = sem("q_psr")
        k_psr = sem("k_psr")
        q_ready = sem("q_ready")
        k_ready = sem("k_ready")
        km_ready = sem("km_ready")
        v_psr = sem("v_psr")
        v_ready = sem("v_ready")
        s_psr = sem("s_psr")
        sm_ready = sem("sm_ready")
        mx_ready = sem("mx_ready")
        sub_ready = sem("sub_ready")
        exp_ready = sem("exp_ready")
        p_psr = sem("p_psr")
        pT_ready = sem("pT_ready")
        o_psr = sem("o_psr")
        rden_ready = sem("rden_ready")
        osb_ready = sem("osb_ready")
        oT_psr = sem("oT_psr")
        oT_ready = sem("oT_ready")
        pr_psr = sem("pr_psr")
        h1_ready = sem("h1_ready")
        h1b_ready = sem("h1b_ready")
        c2 = sem("c2")
        va2_ready = sem("va2_ready")
        rs2_ready = sem("rs2_ready")
        yn_ready = sem("yn_ready")
        yT_psr = sem("yT_psr")
        yT_ready = sem("yT_ready")
        f_psr = sem("f_psr")
        f_ready = sem("f_ready")
        wc_ready = sem("wc_ready")
        y_psr = sem("y_psr")
        fin_ready = sem("fin_ready")
        fin_out = [sem(f"fin_out{p}") for p in range(2)]

        loads = [(ident, "ident"), (wk, "wk"), (wq, "wq"), (wv, "wv"), (hmask, "hmask"), (temp, "temp"), (mask, "mask")]
        expert_loads = [(wp, "wp"), (wi, "wi"), (bi, "bi"), (ws, "ws"), (br, "br"), (bs, "bs"),
                        (wo, "wo"), (bo, "bo"), (route, "route"), (wr, "wr")]
        block = ctx.enter_context(nc.Block())

        def at(i, p, b, lag):
            return behind(i, p, b, lag, 3)

        def num(i, p):
            return 2 * i + p

        @block.sync
        def _(sp):
            for dst, name in loads:
                sp.dma_start(dst[:], t[name]).then_inc(t_const, 16)
            sp.wait_ge(xs_zero, 2)

            def load(dst, i, p, done):
                for m in range(2):
                    sp.dma_start(dst[64 * m:64 * m + BLK], tokens[bass.ds(2 * num(i, p) + m, 1)]
                                 .rearrange("a (b r) d -> (a r) b d", b=3)).then_inc(done, 16)
            for p in range(2):
                load(xs[p], 0, p, xs_in[p])
            for dst, name in expert_loads:
                sp.dma_start(dst[:], t[name]).then_inc(t_experts, 16)
            sp.wait_ge(t_setup, 4)

            def step(i, p, b):
                if b == 0 and at(i, p, 0, 0):
                    if not (isinstance(i, int) and i == 0):
                        sp.wait_ge(h1_ready, num(i, p) - 1)
                        waits_apart(sp, t_passed)
                    load(xr[p], i, p, xr_in[p])
                if b == 0 and at(i, p, 0, 0) and (c := at(i, p, 0, -6)):
                    sp.wait_ge(xn_ready, num(i, p) + 1)
                    waits_apart(sp, t_passed)
                    load(xs[p], c[0], c[1], xs_in[p])
                if b == 2 and (c := at(i, p, 0, 6)):
                    sp.wait_ge(fin_ready, num(c[0], c[1]) + 1)
                    waits_apart(sp, t_passed)
                    for m in range(2):
                        sp.dma_start(out[bass.ds(2 * num(c[0], c[1]) + m, 1)].rearrange("a (b r) d -> (a r) b d", b=3),
                                     fin[c[1]][64 * m:64 * m + BLK]).then_inc(fin_out[c[1]], 16)
            each_step(sp, step, 2, 3)
            for p in range(2):
                sp.wait_ge(fin_out[p], 32 * COUPLES)

        @block.tensor
        def _(pe):
            pe.wait_ge(t_const, 16 * len(loads))
            pe.wait_ge(t_zero, 6)
            pe.wait_ge(t_setup, 6)

            def front1(i, p):
                g = num(i, p)
                pe.wait_ge(xn_ready, g + 1)
                at_least(pe, h1_ready, g - 2)
                waits_apart(pe, t_passed)
                for b in range(3):
                    last = nc.tensor.transpose(fr_ps[0][0:64, 128 * b:128 * b + 128], xn[:, b, :], ident[:])
                last.then_inc(xT_psr, 1)

            def front2(i, p):
                g = num(i, p)
                pe.wait_ge(xT_ready, g + 1)
                at_least(pe, v_ready, g)
                nc.tensor.matmul(fr_ps[1][0:64, 0:2 * TOK], wk[:], xT[:, :, 0:TOK], start=True, stop=True).then_inc(k_psr, 1)
                nc.tensor.matmul(fr_ps[0][0:64, 0:2 * TOK], wq[:], xT[:, :, 0:TOK], start=True, stop=True).then_inc(q_psr, 1)

            def front3(i, p):
                pe.wait_ge(k_ready, num(i, p) + 1)
                for m in range(2):
                    for b in range(3):
                        o = 64 * (3 * m + b)
                        last = nc.tensor.matmul(fr_ps[1][0:KEYS, o:o + 64], xT[:, m, KEY0[b]:KEY0[b] + KEYS], wv[:],
                                                start=True, stop=True)
                last.then_inc(v_psr, 1)

            def scores(i, p, b):
                k = 3 * num(i, p) + b
                if b == 0:
                    pe.wait_ge(km_ready, 2 * num(i, p) + 2)
                    pe.wait_ge(q_ready, num(i, p) + 1)
                at_least(pe, sm_ready, k)
                for h in range(2):
                    for m in range(2):
                        last = nc.tensor.matmul(s_ps[64 * m:64 * m + 64, h, :], qT[p][:, m, BLK * b:BLK * b + 64],
                                                km[p][:, m, 4 * h:4 * h + 4, KEY0[b]:KEY0[b] + KEYS],
                                                start=True, stop=True)
                last.then_inc(s_psr, 1)

            def turn(i, p, b):
                k = 3 * num(i, p) + b
                pe.wait_ge(exp_ready, k + 1)
                at_least(pe, pT_ready, k)
                for h in range(HEADS):
                    last = nc.tensor.transpose(p_ps[:, h // 4, 128 * (h % 4):128 * (h % 4) + 128],
                                               sm[(3 * p + b) % 2][:, h, :], ident[:])
                last.then_inc(p_psr, 1)

            def values(i, p, b):
                k = 3 * num(i, p) + b
                pe.wait_ge(pT_ready, k + 1)
                if b == 0:
                    pe.wait_ge(v_ready, num(i, p) + 1)
                    at_least(pe, osb_ready, num(i, p))
                for h in range(HEADS):
                    for m in range(2):
                        o = (HEADS * b + h) * (HD + 1)
                        last = nc.tensor.matmul(o_ps[64 * m:64 * m + 64, o:o + HD + 1],
                                                pT[:, h, 64 * m:64 * m + 64], vv[p][:, m, b, h, :],
                                                start=True, stop=True)
                last.then_inc(o_psr, 1)

            def back_o(i, p):
                g = num(i, p)
                pe.wait_ge(osb_ready, g + 1)
                pe.wait_ge(q_ready, min(g + 3, PAIRS) if isinstance(g, int) else g + 3)
                waits_apart(pe, t_passed)
                for b in range(3):
                    last = nc.tensor.transpose(fr_ps[0][0:64, 128 * b:128 * b + 128], osb[:, b, :], ident[:])
                last.then_inc(oT_psr, 1)

            def back_proj(i, p):
                pe.wait_ge(oT_ready, num(i, p) + 1)
                for b in range(3):
                    last = nc.tensor.matmul(fr_ps[0][:, 64 * b:64 * b + 64], oT[:, b, :], wp[:], start=True, stop=True)
                last.then_inc(pr_psr, 1)

            def back_y(i, p):
                g = num(i, p)
                pe.wait_ge(yn_ready, g + 1)
                at_least(pe, fin_ready, g)
                waits_apart(pe, t_passed)
                for b in range(3):
                    last = nc.tensor.transpose(ff_ps[0:64, 128 * b:128 * b + 128], yn[:, b, :], ident[:])
                last.then_inc(yT_psr, 1)

            def back_in(i, p):
                pe.wait_ge(yT_ready, num(i, p) + 1)
                nc.tensor.matmul(ff_ps[:, 0:384], wi[:], yT[:].rearrange("d b n -> d (b n)"),
                                 start=True, stop=True).then_inc(f_psr, 1)

            def back_layer(i, p, l):
                g = num(i, p)
                pe.wait_ge(f_ready, 3 * g + l + 1)
                if l == 0:
                    pe.wait_ge(wc_ready, g + 1)
                for m in range(2):
                    last = nc.tensor.matmul(ff_ps[:, 192 * m:192 * m + 192], wc[p][:, l, m, :], ff[l][:, :, m, :],
                                            start=True, stop=True)
                last.then_inc(f_psr, 1)

            def back_out(i, p):
                pe.wait_ge(f_ready, 3 * num(i, p) + 3)
                for b in range(3):
                    last = nc.tensor.matmul(ff_ps[:, 64 * b:64 * b + 64], ff[2][:, b].rearrange("k m n -> k (m n)"), wo[:],
                                            start=True, stop=True)
                last.then_inc(y_psr, 1)

            front1(0, 0)
            front2(0, 0)
            front3(0, 0)
            scores(0, 0, 0)
            pe.wait_ge(t_experts, 16 * len(expert_loads))

            def step(i, p, b):
                here, prev, old = at(i, p, 0, 0), at(i, p, 0, 3), at(i, p, 0, 6)
                nxt = here and at(i, p, 0, -3)
                if c := at(i, p, b, 1):
                    turn(*c)
                if b == 0 and nxt:
                    front1(*nxt[0:2])
                if b == 1 and prev:
                    back_o(*prev[0:2])
                if b == 1 and old:
                    back_layer(old[0], old[1], 0)
                if b == 2 and old:
                    back_out(*old[0:2])
                if c := at(i, p, b, -1):
                    scores(*c)
                if b == 0 and old:
                    back_y(*old[0:2])
                if c := at(i, p, b, 1):
                    values(*c)
                if b == 0 and nxt:
                    front2(*nxt[0:2])
                if b == 0 and old:
                    back_in(*old[0:2])
                if b == 1 and nxt:
                    front3(*nxt[0:2])
                if b == 1 and prev:
                    back_proj(*prev[0:2])
                if b == 1 and old:
                    back_layer(old[0], old[1], 1)
            each_step(pe, step, 2, 3)

        @block.scalar
        def _(act):
            act.wait_ge(t_zero, 6)
            act.wait_ge(t_const, 16 * len(loads))

            def xT_copy(i, p):
                g = num(i, p)
                act.wait_ge(xT_psr, g + 1)
                at_least(act, v_psr, g)
                nc.scalar.copy(xT[0:64, :, 0:TOK].rearrange("d m (b r) -> d b m r", b=3),
                               fr_ps[0][0:64, 0:384].rearrange("d (b m r) -> d b m r", b=3, m=2)[:, :, :, 0:BLK]
                               ).then_inc(xT_ready, 1)

            def qk_copy(i, p):
                g = num(i, p)
                act.wait_ge(k_psr, g + 1)
                at_least(act, km_ready, 2 * g)
                nc.scalar.copy(kT[:].rearrange("d m n -> d (m n)"), fr_ps[1][0:64, 0:2 * TOK]).then_inc(k_ready, 1)
                act.wait_ge(q_psr, g + 1)
                nc.scalar.copy(qT[p][0:64, :, 0:TOK], fr_ps[0][0:64, 0:2 * TOK].rearrange("d (m n) -> d m n", m=2)
                               ).then_inc(q_ready, 1)

            def v_copy(i, p):
                act.wait_ge(v_psr, num(i, p) + 1)
                nc.scalar.copy(vv[p][:].rearrange("k m b h d -> k (m b h) d")[:, :, 0:HD],
                               fr_ps[1][0:KEYS, 0:384].rearrange("k (c d) -> k c d", d=HD)).then_inc(v_ready, 1)

            def exp(i, p, b):
                act.wait_ge(sub_ready, 3 * num(i, p) + b + 1)
                tile = sm[(3 * p + b) % 2][:].rearrange("p h k -> p (h k)")
                nc.scalar.activation(tile, tile, ACT.Exp).then_inc(exp_ready, 1)

            def pT_copy(i, p, b):
                k = 3 * num(i, p) + b
                act.wait_ge(p_psr, k + 1)
                at_least(act, o_psr, k)
                nc.scalar.copy(pT[:].rearrange("k h n -> k (h n)"), p_ps.rearrange("k a n -> k (a n)")).then_inc(pT_ready, 1)

            def oT_copy(i, p):
                act.wait_ge(oT_psr, num(i, p) + 1)
                nc.scalar.copy(oT[0:64].rearrange("d b n -> d (b n)"), fr_ps[0][0:64, 0:384]).then_inc(oT_ready, 1)

            def yT_copy(i, p):
                act.wait_ge(yT_psr, num(i, p) + 1)
                nc.scalar.copy(yT[0:64].rearrange("d b n -> d (b n)"), ff_ps[0:64, 0:384]).then_inc(yT_ready, 1)

            def relu_in(i, p):
                act.wait_ge(f_psr, 3 * num(i, p) + 1)
                nc.scalar.activation(ff[0][:].rearrange("k b m n -> k (b m n)"), ff_ps[:, 0:384], ACT.Relu, bias=bi[:]
                                     ).then_inc(f_ready, 1)

            def relu_layer(i, p, l):
                act.wait_ge(f_psr, 3 * num(i, p) + l + 2)
                for m in range(2):
                    last = nc.scalar.activation(ff[l + 1][:, :, m, :], ff_ps[:, 192 * m:192 * m + 192]
                                                .rearrange("k (b n) -> k b n", b=3), ACT.Relu, bias=bc[p][:, m, l:l + 1])
                last.then_inc(f_ready, 1)

            xT_copy(0, 0)
            qk_copy(0, 0)
            v_copy(0, 0)
            act.wait_ge(t_experts, 16 * len(expert_loads))

            def step(i, p, b):
                here, prev, old = at(i, p, 0, 0), at(i, p, 0, 3), at(i, p, 0, 6)
                nxt = here and at(i, p, 0, -3)
                if c := at(i, p, b, 1):
                    pT_copy(*c)
                if b == 0 and nxt:
                    xT_copy(*nxt[0:2])
                if b == 0 and old:
                    yT_copy(*old[0:2])
                if b == 0 and nxt:
                    qk_copy(*nxt[0:2])
                if b == 1 and prev:
                    oT_copy(*prev[0:2])
                if b == 1 and old:
                    relu_layer(old[0], old[1], 0)
                if b == 1 and nxt:
                    v_copy(*nxt[0:2])
                if here:
                    exp(i, p, b)
                if b == 0 and old:
                    relu_in(*old[0:2])
                if b == 1 and old:
                    relu_layer(old[0], old[1], 1)
            each_step(act, step, 2, 3)

        @block.vector
        def _(dve):
            for p in range(2):
                nc.vector.memset(xs[p][:], 0.0).then_inc(xs_zero, 1)
            for tile in (xT, qT[0], qT[1], yT):
                nc.vector.memset(tile[:], 0.0).then_inc(t_zero, 1)
            for p in range(2):
                nc.vector.memset(vv[p][:, :, :, :, HD:HD + 1], 1.0).then_inc(t_setup, 1)
                nc.vector.memset(xr[p][:], 0.0).then_inc(t_setup, 1)
            nc.vector.memset(oT[:], 0.0).then_inc(c1, 1)
            nc.vector.memset(mh[:], -0.5)
            dve.wait_ge(c1, 1)
            nc.vector.memset(oT[64:65], 1.0).then_inc(t_setup, 1)
            dve.wait_ge(t_const, 16 * len(loads))
            nc.vector.tensor_scalar(hmask[:], hmask[:], temp[:], None, ALU.mult).then_inc(t_setup, 1)

            def norm(x, n, sq, st, mu, va, chain, base, va_ready, g, free):
                wide = [128, 3, 64]
                nc.vector.tensor_reduce(st[:], x[:], axis=AX.X, op=ALU.add).then_inc(chain, 1)
                dve.wait_ge(chain, base + 4 * g + 1)
                nc.vector.tensor_scalar(mu[:], st[:], 1.0 / 64, None, ALU.mult).then_inc(chain, 1)
                dve.wait_ge(chain, base + 4 * g + 2)
                free()
                nc.vector.tensor_tensor(n[:], x[:], mu[:].unsqueeze(2).to_broadcast(wide), ALU.subtract).then_inc(chain, 1)
                dve.wait_ge(chain, base + 4 * g + 3)
                nc.vector.tensor_tensor(sq[:], n[:], n[:], ALU.mult).then_inc(chain, 1)
                dve.wait_ge(chain, base + 4 * g + 4)
                nc.vector.tensor_reduce(va[:], sq[:], axis=AX.X, op=ALU.add).then_inc(va_ready, 1)

            def norm_end(n, rs, rs_ready, n_ready, g):
                dve.wait_ge(rs_ready, 2 * g + 2)
                nc.vector.tensor_tensor(n[:], n[:], rs[:].unsqueeze(2).to_broadcast([128, 3, 64]), ALU.mult).then_inc(n_ready, 1)

            def norm1(i, p):
                g = num(i, p)
                dve.wait_ge(xs_in[p], 32 * (i + 1))
                norm(xs[p], xn, xsq, st1, mu1, va1, c1, 1, va1_ready, g,
                     lambda: at_least(dve, xT_psr, g))

            def norm1_end(i, p):
                norm_end(xn, rs1, rs1_ready, xn_ready, num(i, p))

            def masked(i, p, b):
                k = 3 * num(i, p) + b
                dve.wait_ge(s_psr, k + 1)
                at_least(dve, p_psr, k - 1)
                tile = sm[(3 * p + b) % 2]
                nc.vector.tensor_tensor(tile[:].rearrange("p (a h) k -> p a h k", a=2),
                                        s_ps.rearrange("p a (h k) -> p a h k", h=4),
                                        mask[:, b, :].unsqueeze(1).unsqueeze(1).to_broadcast([128, 2, 4, KEYS]),
                                        ALU.add).then_inc(sm_ready, 1)
                dve.wait_ge(sm_ready, k + 1)
                at_least(dve, sub_ready, k - 1)
                nc.vector.tensor_reduce(mx[(3 * p + b) % 2][:], tile[:], axis=AX.X, op=ALU.max).then_inc(mx_ready, 1)

            def o_norm(i, p):
                g = num(i, p)
                dve.wait_ge(o_psr, 3 * g + 3)
                sums = o_ps.rearrange("p (c d) -> p c d", d=HD + 1)
                nc.vector.reciprocal(rden[:], sums[:, :, HD]).then_inc(rden_ready, 1)
                dve.wait_ge(rden_ready, g + 1)
                at_least(dve, oT_psr, g)
                nc.vector.tensor_tensor(osb[:].rearrange("p b (h d) -> p (b h) d", h=HEADS),
                                        sums[:, :, 0:HD], rden[:].unsqueeze(2).to_broadcast([128, 3 * HEADS, HD]),
                                        ALU.mult).then_inc(osb_ready, 1)

            def residual(i, p):
                g = num(i, p)
                dve.wait_ge(pr_psr, g + 1)
                dve.wait_ge(xr_in[p], 32 * (i + 1))
                at_least(dve, h1b_ready, g - 1)
                nc.vector.tensor_tensor(h1[p][:], fr_ps[0][:, 0:192].rearrange("p (b d) -> p b d", b=3), xr[p][:], ALU.add
                                        ).then_inc(h1_ready, 1)
                dve.wait_ge(h1_ready, g + 1)
                norm(h1[p], yn, ysq, st2, mu2, va2, c2, 0, va2_ready, g,
                     lambda: at_least(dve, yT_psr, g))

            def weights(i, p):
                g = num(i, p)
                at_least(dve, y_psr, g - 1)
                for m in range(2):
                    e = dve.value_load(route[0:1, bass.ds(4 * i + 2 * p + m, 1)], min_val=0, max_val=EXPERTS - 1)
                    nc.vector.tensor_tensor(wc[p][:, :, m, :], wr[:, :, bass.ds(e, 1), :].rearrange("p l a n -> p l (a n)"), ws[:], ALU.add)
                    last = nc.vector.tensor_copy(bc[p][:, m, :], br[:, :, bass.ds(e, 1)].rearrange("p l a -> p (l a)"))
                last.then_inc(wc_ready, 1)

            def final(i, p):
                g = num(i, p)
                dve.wait_ge(y_psr, g + 1)
                dve.wait_ge(h1b_ready, g + 1)
                at_least(dve, fin_out[p], 32 * i)
                nc.vector.tensor_tensor(fin[p][:], ff_ps[:, 0:192].rearrange("p (b d) -> p b d", b=3), h1b[p][:], ALU.add
                                        ).then_inc(fin_ready, 1)

            for p in range(2):
                norm1(0, p)
                norm1_end(0, p)
            dve.wait_ge(t_experts, 16 * len(expert_loads))
            nc.vector.tensor_tensor(ws[:], ws[:], ident[:].unsqueeze(1).to_broadcast([128, 2, 128]), ALU.add).then_inc(t_setup, 1)
            nc.vector.tensor_tensor(br[:], br[:], bs[:].unsqueeze(2).to_broadcast([128, 2, EXPERTS]), ALU.add).then_inc(t_setup, 1)
            dve.wait_ge(t_setup, 8)

            def step(i, p, b):
                here, prev, old = at(i, p, 0, 0), at(i, p, 0, 3), at(i, p, 0, 6)
                nxt2 = here and at(i, p, 0, -6)
                if here:
                    masked(i, p, b)
                if b == 0 and old:
                    norm_end(yn, rs2, rs2_ready, yn_ready, num(old[0], old[1]))
                if b == 2 and prev:
                    residual(*prev[0:2])
                if b == 2 and nxt2:
                    norm1(*nxt2[0:2])
                if b == 0 and prev:
                    o_norm(*prev[0:2])
                if b == 1 and prev:
                    weights(*prev[0:2])
                if b == 2 and nxt2:
                    norm1_end(*nxt2[0:2])
                if b == 2 and old:
                    final(*old[0:2])
            each_step(dve, step, 2, 3)

        @block.gpsimd
        def _(pool):
            for p in range(2):
                nc.gpsimd.memset(km[p][:], 0.0).then_inc(t_zero, 1)
            pool.wait_ge(t_zero, 6)
            pool.wait_ge(t_setup, 6)

            def power(va, rs, va_ready, rs_ready, i, p):
                g = num(i, p)
                pool.wait_ge(va_ready, g + 1)
                waits_apart(pool, t_passed)
                nc.gpsimd.tensor_scalar(va[:], va[:], 1.0 / 64, EPS, ALU.mult, ALU.add).then_inc(rs_ready, 1)
                pool.wait_ge(rs_ready, 2 * g + 1)
                nc.gpsimd.tensor_tensor(rs[:], va[:], mh[:], ALU.pow).then_inc(rs_ready, 1)

            def keys(i, p, m):
                g = num(i, p)
                if m == 0:
                    pool.wait_ge(k_ready, g + 1)
                    at_least(pool, s_psr, 3 * (g - 1))
                nc.gpsimd.tensor_tensor(km[p][0:64, m], kT[:, m:m + 1, :].to_broadcast([64, HEADS, TOK]),
                                        hmask[:].unsqueeze(2).to_broadcast([64, HEADS, TOK]), ALU.mult).then_inc(km_ready, 1)

            def shift(i, p, b):
                pool.wait_ge(mx_ready, 3 * num(i, p) + b + 1)
                n = (3 * p + b) % 2
                nc.gpsimd.tensor_tensor(sm[n][:], sm[n][:], mx[n][:].unsqueeze(2).to_broadcast([128, HEADS, KEYS]),
                                        ALU.subtract).then_inc(sub_ready, 1)

            def with_bias(i, p):
                g = num(i, p)
                pool.wait_ge(h1_ready, g + 1)
                at_least(pool, fin_ready, g - 1)
                nc.gpsimd.tensor_tensor(h1b[p][:], h1[p][:], bo[:].unsqueeze(1).to_broadcast([128, 3, 64]), ALU.add
                                        ).then_inc(h1b_ready, 1)

            for p in range(2):
                power(va1, rs1, va1_ready, rs1_ready, 0, p)
            keys(0, 0, 0)
            keys(0, 0, 1)
            pool.wait_ge(t_experts, 16 * len(expert_loads))

            def step(i, p, b):
                here, prev = at(i, p, 0, 0), at(i, p, 0, 3)
                nxt, nxt2 = here and at(i, p, 0, -3), here and at(i, p, 0, -6)
                if here:
                    shift(i, p, b)
                if b < 2 and nxt:
                    keys(nxt[0], nxt[1], b)
                if b == 2 and prev:
                    power(va2, rs2, va2_ready, rs2_ready, *prev[0:2])
                if b == 2 and nxt2:
                    power(va1, rs1, va1_ready, rs1_ready, *nxt2[0:2])
                if b == 2 and prev:
                    with_bias(*prev[0:2])
            each_step(pool, step, 2, 3)


def layouts(inp):
    f = lambda k: np.asarray(inp[k])
    out = {}
    x = f("x").reshape(PAIRS, 2, YQ, CHUNKS, 4, X, 3)
    out["x"] = x.transpose(0, 4, 2, 6, 3, 1, 5).reshape(PAIRS, 48, CHUNKS, 128)
    wr, wi = (np.concatenate([f("L0_tok_w1" + a), f("L0_tok_w2" + a)], axis=3)
              .reshape(LAYERS, C, C, KY, 6, 2).transpose(0, 5, 1, 4, 3, 2) for a in "ri")
    w = np.empty((LAYERS, 2, 2, C, 6, KY, 2, C), np.float32)
    w[:, :, 0, ..., 0, :], w[:, :, 0, ..., 1, :] = wr, wi
    w[:, :, 1, ..., 0, :], w[:, :, 1, ..., 1, :] = wi, wr
    out["w"] = w.reshape(LAYERS, 128, MODES, 2, C)
    cw = np.zeros((C, YQ, LAYERS, YQ, C), np.float32)
    fc0 = np.zeros((128, YC, C), np.float32)
    fc1 = np.zeros((4, C, 4, 128), np.float32)
    for y in range(4):
        cw[:, y, :, y, :] = f("L0_tok_conv_w").transpose(2, 0, 1)
        fc1[y, :, y] = f("L0_tok_fc1_w")
    for y in range(YC):
        fc0[3 * y:3 * y + 3, y] = f("L0_tok_fc0_w")
    fc0[48] = f("L0_tok_fc0_b")
    out["conv_w"] = cw.reshape(128, LAYERS, 4, C)
    out["fc0"] = fc0
    out["conv_b"] = np.repeat(f("L0_tok_conv_b")[:, None, :], Y, axis=1)
    g = np.concatenate([f("L0_tok_ln0_g")[None], f("L0_tok_ln_g")])
    b = np.concatenate([f("L0_tok_ln0_b")[None], f("L0_tok_ln_b")])
    out["lnp"] = np.tile(np.stack([g[-1], b[-1]], axis=-1), (4, 1))
    out["gbx"] = np.tile(np.stack([g, b], axis=1)[None, 0:LAYERS], (128, 1, 1, 1))
    out["fc1_w"] = fc1.reshape(128, 4, 128)
    out["fc1_b"] = f("L0_tok_fc1_b")[:, None]
    out["fc2_w"] = f("L0_tok_fc2_w")
    out["fc2_b"] = np.tile(f("L0_tok_fc2_b"), 2)[:, None]
    fc3 = np.zeros((2, 64, 2), np.float32)
    for y in range(2):
        fc3[y, :, y] = f("L0_tok_fc3_w")[:, 0]
    out["fc3_w"] = fc3.reshape(128, 2)
    out["fc3_b"] = np.repeat(f("L0_tok_fc3_b")[:, None], 128, axis=0)
    st = f("x_txt")
    out["state"] = np.concatenate([st, st]).astype(np.int32)
    out["pos"] = np.tile(np.arange(TXT, dtype=np.float32), (128, 1))
    out["txt_gb"] = np.tile(np.stack([f("L0_txt_gamma"), f("L0_txt_beta")])[None], (128, 1, 1))
    for k in ("token_emb", "instr_emb", "arg_emb"):
        out[k] = f("L0_txt_" + k)
    rows = lambda a: np.concatenate([a, np.zeros((128 - len(a),) + a.shape[1:])])
    mask = np.zeros((128, 3, KEYS), np.float32)
    for b_ in range(3):
        q, k = (a // 11 * np.array([1]) for a in (BLK * b_ + np.arange(BLK), KEY0[b_] + np.arange(KEYS)))
        qc, kc = (BLK * b_ + np.arange(BLK)) % 11, (KEY0[b_] + np.arange(KEYS)) % 11
        far = (abs(q[:, None] - k[None]) > 3) | (abs(qc[:, None] - kc[None]) > 3)
        for m in range(2):
            mask[64 * m:64 * m + BLK, b_] = np.where(far, -1e30, 0)
    out["mask"] = mask
    out["hmask"] = np.where(np.arange(64)[:, None] // HD == np.arange(HEADS), HD ** -0.5, 0)
    out["temp"] = np.tile(f("L0_attn_temperature"), 64)[:, None]
    for n, k in enumerate(("wq", "wk", "wv")):
        out[k] = rows(f("L0_attn_W_qkv")[64 * n:64 * n + 64].T)
    out["wp"] = rows(np.concatenate([f("L0_attn_W_proj").T, f("L0_attn_b_proj")[None]]))
    out["wi"] = rows(f("L0_ffn_Wi").T)
    out["bi"] = f("L0_ffn_bi")[:, None]
    out["wr"] = f("L0_ffn_Wr").transpose(3, 0, 1, 2)
    out["ws"] = f("L0_ffn_Ws")[:, 0].transpose(2, 0, 1)
    out["br"] = f("L0_ffn_br").transpose(2, 0, 1)
    out["bs"] = f("L0_ffn_bs")[:, 0].T
    out["wo"] = f("L0_ffn_Wo").T
    out["bo"] = np.tile(f("L0_ffn_bo"), (128, 1))
    out["route"] = f("L0_ffn_route_id")[None].astype(np.int32)
    kx, n64 = np.arange(KX), np.arange(64)
    ky = np.concatenate([np.arange(KYH), np.arange(64 - KYH, 64)])
    tx = 2 * np.pi * np.outer(n64, kx) / 64
    ty = 2 * np.pi * np.outer(n64, ky) / 64
    d1 = np.zeros((2, 64, 2, KX, 3))
    ex = np.zeros((2, KX, 2, 2, 64))
    weight = np.where(kx == 0, 1.0, 2.0)[:, None] / (64 * 64)
    for m in range(2):
        d1[m, :, m, :, 0], d1[m, :, m, :, 1], d1[m, :, m, :, 2] = np.cos(tx), -np.sin(tx), -np.cos(tx)
        ex[m, :, 0, m], ex[m, :, 1, m] = weight * np.cos(tx.T), -weight * np.sin(tx.T)
    out["d1"] = d1.reshape(128, 2, KX, 3)
    rows = lambda a: np.concatenate([a, np.zeros((128 - len(a),) + a.shape[1:])])
    ex = ex.reshape(2, KX // 2, 2, 2, 128).transpose(0, 2, 1, 3, 4)
    out["ex"] = rows(np.concatenate([ex.reshape(2 * TRIG, 128), np.ones((1, 128))]))
    out["cy"] = np.concatenate([np.cos(ty), np.sin(ty)])
    out["dyi"] = np.concatenate([rows(np.cos(ty.T))[0:64], rows(-np.sin(ty.T))[0:64]])
    out["sgn"] = np.tile(np.repeat([1.0, -1.0], C), 2)[:, None]
    out["ident"] = np.eye(128)
    out["ones"] = np.ones((1, 512))
    return {k: np.ascontiguousarray(v, dtype=v.dtype if v.dtype.kind == "i" else np.float32) for k, v in out.items()}


def kernel(**inputs):
    import concourse.bacc as bacc
    from concourse.bass_utils import run_bass_kernel_spmd

    nc = bacc.Bacc("TRN2", target_bir_lowering=False, num_devices=1)
    arrays = {f"in_{k}": v for k, v in layouts(inputs).items()}
    t = {k[3:]: nc.dram_tensor(k, v.shape, mybir.dt.from_np(v.dtype), kind="ExternalInput").ap()
         for k, v in arrays.items()}
    out = nc.dram_tensor("out", [IMGS, TOK, 64], F32, kind="ExternalOutput").ap()
    tokens = nc.dram_tensor("tokens", [IMGS, TOK, 64], F32).ap()
    token_network(nc, t, tokens)
    attention_and_experts(nc, t, tokens, out)
    r = run_bass_kernel_spmd(nc, [arrays], core_ids=[0])
    return r.results[0]["out"]
```
